# Optimizing a Trainium2 kernel written in Bass

```python
import numpy as np
import jax
import jax.numpy as jnp

def _softmax(x, axis=-1):
    return jax.nn.softmax(x, axis=axis)

def _gelu(x):
    return jax.nn.gelu(x, approximate=True)

def _silu(x):
    return jax.nn.silu(x)

def _sigmoid(x):
    return jax.nn.sigmoid(x)

def _layernorm(x, axis=-1, eps=1e-05):
    m = jnp.mean(x, axis=axis, keepdims=True)
    v = jnp.var(x, axis=axis, keepdims=True)
    return (x - m) / jnp.sqrt(v + eps)

def _scatter_add(tgt, idx, src, axis=0):
    return tgt.at[idx].add(src)

def _segment_sum(src, seg, n):
    return jax.ops.segment_sum(src, seg, n)
kernel_name = 'mk_conv_attn_hybrid_d2_conv_nchw256_r2_1b8eb7'

def setup_inputs(seed: int=0):
    np.random.seed(seed)
    _w = jnp.asarray

    def _rec_inputs():
        import jax
        import jax.numpy as jnp
        _gk = jax.random.key(seed)
        x = -0.0002928 + 1 * jax.random.normal(jax.random.fold_in(_gk, 1), (4, 128, 32, 32), jnp.float32)
        return x
    x = _rec_inputs()

    def _L0_conv_setup():
        import math
        import jax, jax.numpy as jnp
        import numpy as np
        B, C, H, W = (4, 128, 32, 32)
        KEEP = 0.1
        key = jax.random.key(seed)
        kx, kq, kk, kv = jax.random.split(key, 4)
        scale = 1.0 / math.sqrt(C)
        return {'x': jax.random.normal(kx, (B, C, H, W), dtype=jnp.float32), 'Wq': jax.random.normal(kq, (C, C), dtype=jnp.float32) * scale, 'Wk': jax.random.normal(kk, (C, C), dtype=jnp.float32) * scale, 'Wv': jax.random.normal(kv, (C, C), dtype=jnp.float32) * scale}
    _L0_conv_all = _L0_conv_setup()
    _L0_conv_in = {k: v for k, v in _L0_conv_all.items() if k in ('Wq', 'Wk', 'Wv')}
    del _L0_conv_all

    def _L1_attn_setup():
        import jax, jax.numpy as jnp
        import numpy as np
        D_MODEL = 128
        D_STATE = 16
        D_CONV = 4
        D_INNER = 256
        DT_RANK = 16
        BN = 64
        M = 32
        PARAM_NAMES = ['in_proj_w', 'conv_w', 'conv_b', 'x_proj_w', 'dt_proj_w', 'dt_proj_b', 'A_log', 'D', 'out_proj_w']

        def _mamba(x, in_proj_w, conv_w, conv_b, x_proj_w, dt_proj_w, dt_proj_b, A_log, Dvec, out_proj_w):
            xz = x @ in_proj_w.T
            xs, z = jnp.split(xz, 2, axis=-1)
            xs_pad = jnp.pad(xs, ((0, 0), (D_CONV - 1, 0), (0, 0)))
            kern = jnp.transpose(conv_w, (2, 1, 0))
            xs = jax.lax.conv_general_dilated(xs_pad, kern, (1,), 'VALID', dimension_numbers=('NWC', 'WIO', 'NWC'), feature_group_count=D_INNER) + conv_b
            xs = jax.nn.silu(xs)
            dbc = xs @ x_proj_w.T
            dt = jax.nn.softplus(dbc[..., :DT_RANK] @ dt_proj_w.T + dt_proj_b)
            Bm = dbc[..., DT_RANK:DT_RANK + D_STATE]
            Cm = dbc[..., DT_RANK + D_STATE:]
            A = -jnp.exp(A_log)
            dA = jnp.exp(dt[..., None] * A)
            dBu = dt[..., None] * Bm[:, :, None, :] * xs[..., None]

            def combine(c1, c2):
                a1, b1 = c1
                a2, b2 = c2
                return (a1 * a2, a2 * b1 + b2)
            _, hs = jax.lax.associative_scan(combine, (dA, dBu), axis=1)
            y = jnp.einsum('blds,bls->bld', hs, Cm) + xs * Dvec
            y = y * jax.nn.silu(z)
            return y @ out_proj_w.T

        def _core(x, ln_gamma, ln_beta, fp, bp):
            mu = x.mean(-1, keepdims=True)
            var = x.var(-1, keepdims=True)
            xn = (x - mu) / jnp.sqrt(var + 1e-05) * ln_gamma + ln_beta
            y_fwd = _mamba(xn, *fp)
            y_bwd = jnp.flip(_mamba(jnp.flip(xn, 1), *bp), 1)
            return y_fwd + y_bwd + x

        def _mamba_params(key):
            ks = jax.random.split(key, 5)
            s = 0.02
            return {'in_proj_w': jax.random.normal(ks[0], (2 * D_INNER, D_MODEL)) * s, 'conv_w': jax.random.normal(ks[1], (D_INNER, 1, D_CONV)) * s, 'conv_b': jnp.zeros((D_INNER,)), 'x_proj_w': jax.random.normal(ks[2], (DT_RANK + 2 * D_STATE, D_INNER)) * s, 'dt_proj_w': jax.random.normal(ks[3], (D_INNER, DT_RANK)) * s, 'dt_proj_b': jnp.full((D_INNER,), -4.6), 'A_log': jnp.log(jnp.tile(jnp.arange(1, D_STATE + 1, dtype=jnp.float32), (D_INNER, 1))), 'D': jnp.ones((D_INNER,)), 'out_proj_w': jax.random.normal(ks[4], (D_MODEL, D_INNER)) * s}
        key = jax.random.key(seed)
        kx, kf, kb = jax.random.split(key, 3)
        inp = {'x': jax.random.normal(kx, (BN, M, D_MODEL), dtype=jnp.float32), 'ln_gamma': jnp.ones((D_MODEL,), jnp.float32), 'ln_beta': jnp.zeros((D_MODEL,), jnp.float32)}
        fp = _mamba_params(kf)
        bp = _mamba_params(kb)
        for n in PARAM_NAMES:
            inp['f_' + n] = fp[n]
            inp['b_' + n] = bp[n]
        return inp
    _L1_attn_all = _L1_attn_setup()
    _L1_attn_in = {k: v for k, v in _L1_attn_all.items() if k in ('ln_gamma', 'ln_beta', 'f_in_proj_w', 'f_conv_w', 'f_conv_b', 'f_x_proj_w', 'f_dt_proj_w', 'f_dt_proj_b', 'f_A_log', 'f_D', 'f_out_proj_w', 'b_in_proj_w', 'b_conv_w', 'b_conv_b', 'b_x_proj_w', 'b_dt_proj_w', 'b_dt_proj_b', 'b_A_log', 'b_D', 'b_out_proj_w')}
    del _L1_attn_all

    def _L1_ffn_setup():
        import jax, jax.numpy as jnp
        import numpy as np
        NUM_EXPERTS = 8
        TOP_K = 2
        B, S, D = (8, 4096, 128)

        def _moe(tokens, router_w, w1, b1, w2, b2):
            N = tokens.shape[0]
            E = router_w.shape[0]
            logits = tokens.astype(jnp.float32) @ router_w.astype(jnp.float32).T
            probs = jax.nn.softmax(logits, axis=-1)
            rw, re = jax.lax.top_k(probs, TOP_K)
            if TOP_K > 1:
                rw = rw / jnp.maximum(rw.sum(-1, keepdims=True), 1e-12)
            rw = rw.astype(tokens.dtype)
            combine = jnp.zeros((N, E), tokens.dtype).at[jnp.arange(N)[:, None], re].set(rw)
            out = tokens
            for e in range(E):
                h = jax.nn.gelu(tokens @ w1[e] + b1[e], approximate=False)
                y = h @ w2[e] + b2[e]
                out = out + combine[:, e:e + 1] * y
            return out
        key = jax.random.key(seed)
        ks = jax.random.split(key, 4)
        scale = 1.0 / np.sqrt(D).astype(np.float32)
        return {'input_embeddings': jax.random.normal(ks[0], (B, S, D), jnp.float32), 'router_w': jax.random.normal(ks[1], (NUM_EXPERTS, D), jnp.float32) * scale, 'w1': jax.random.normal(ks[2], (NUM_EXPERTS, D, D), jnp.float32) * scale, 'b1': jnp.zeros((NUM_EXPERTS, D), jnp.float32), 'w2': jax.random.normal(ks[3], (NUM_EXPERTS, D, D), jnp.float32) * scale, 'b2': jnp.zeros((NUM_EXPERTS, D), jnp.float32)}
    _L1_ffn_all = _L1_ffn_setup()
    _L1_ffn_in = {k: v for k, v in _L1_ffn_all.items() if k in ('router_w', 'w1', 'b1', 'w2', 'b2')}
    del _L1_ffn_all
    return {'x': x, 'L0_conv_Wq': _L0_conv_in['Wq'], 'L0_conv_Wk': _L0_conv_in['Wk'], 'L0_conv_Wv': _L0_conv_in['Wv'], 'L1_attn_ln_gamma': _L1_attn_in['ln_gamma'], 'L1_attn_ln_beta': _L1_attn_in['ln_beta'], 'L1_attn_f_in_proj_w': _L1_attn_in['f_in_proj_w'], 'L1_attn_f_conv_w': _L1_attn_in['f_conv_w'], 'L1_attn_f_conv_b': _L1_attn_in['f_conv_b'], 'L1_attn_f_x_proj_w': _L1_attn_in['f_x_proj_w'], 'L1_attn_f_dt_proj_w': _L1_attn_in['f_dt_proj_w'], 'L1_attn_f_dt_proj_b': _L1_attn_in['f_dt_proj_b'], 'L1_attn_f_A_log': _L1_attn_in['f_A_log'], 'L1_attn_f_D': _L1_attn_in['f_D'], 'L1_attn_f_out_proj_w': _L1_attn_in['f_out_proj_w'], 'L1_attn_b_in_proj_w': _L1_attn_in['b_in_proj_w'], 'L1_attn_b_conv_w': _L1_attn_in['b_conv_w'], 'L1_attn_b_conv_b': _L1_attn_in['b_conv_b'], 'L1_attn_b_x_proj_w': _L1_attn_in['b_x_proj_w'], 'L1_attn_b_dt_proj_w': _L1_attn_in['b_dt_proj_w'], 'L1_attn_b_dt_proj_b': _L1_attn_in['b_dt_proj_b'], 'L1_attn_b_A_log': _L1_attn_in['b_A_log'], 'L1_attn_b_D': _L1_attn_in['b_D'], 'L1_attn_b_out_proj_w': _L1_attn_in['b_out_proj_w'], 'L1_ffn_router_w': _L1_ffn_in['router_w'], 'L1_ffn_w1': _L1_ffn_in['w1'], 'L1_ffn_b1': _L1_ffn_in['b1'], 'L1_ffn_w2': _L1_ffn_in['w2'], 'L1_ffn_b2': _L1_ffn_in['b2']}

def reference(x, L0_conv_Wq, L0_conv_Wk, L0_conv_Wv, L1_attn_ln_gamma, L1_attn_ln_beta, L1_attn_f_in_proj_w, L1_attn_f_conv_w, L1_attn_f_conv_b, L1_attn_f_x_proj_w, L1_attn_f_dt_proj_w, L1_attn_f_dt_proj_b, L1_attn_f_A_log, L1_attn_f_D, L1_attn_f_out_proj_w, L1_attn_b_in_proj_w, L1_attn_b_conv_w, L1_attn_b_conv_b, L1_attn_b_x_proj_w, L1_attn_b_dt_proj_w, L1_attn_b_dt_proj_b, L1_attn_b_A_log, L1_attn_b_D, L1_attn_b_out_proj_w, L1_ffn_router_w, L1_ffn_w1, L1_ffn_b1, L1_ffn_w2, L1_ffn_b2):
    import jax
    import jax.numpy as jnp

    def _L0_conv_ref(x, Wq, Wk, Wv):
        import math
        import jax, jax.numpy as jnp
        import numpy as np
        B, C, H, W = (4, 128, 32, 32)
        KEEP = 0.1
        b, c, h, w = x.shape
        n = h * w
        xt = x.reshape(b, c, n).transpose(0, 2, 1)
        q = jnp.einsum('bnc,dc->bnd', xt, Wq)
        k = jnp.einsum('bnc,dc->bnd', xt, Wk)
        v = jnp.einsum('bnc,dc->bnd', xt, Wv)
        scores = jnp.einsum('bqd,bkd->bqk', q, k) / math.sqrt(c)
        k_keep = max(1, int(KEEP * n))
        topk_vals, topk_idx = jax.lax.top_k(scores, k_keep)
        neg_inf = jnp.finfo(scores.dtype).min
        mask = jnp.full_like(scores, neg_inf)
        bi = jnp.arange(b)[:, None, None]
        qi = jnp.arange(n)[None, :, None]
        mask = mask.at[bi, qi, topk_idx].set(topk_vals)
        attn = jax.nn.softmax(mask, axis=-1)
        out = jnp.einsum('bqk,bkd->bqd', attn, v)
        return out.transpose(0, 2, 1).reshape(b, c, h, w)

    def _L1_attn_ref(x, ln_gamma, ln_beta, f_in_proj_w, f_conv_w, f_conv_b, f_x_proj_w, f_dt_proj_w, f_dt_proj_b, f_A_log, f_D, f_out_proj_w, b_in_proj_w, b_conv_w, b_conv_b, b_x_proj_w, b_dt_proj_w, b_dt_proj_b, b_A_log, b_D, b_out_proj_w):
        import jax, jax.numpy as jnp
        import numpy as np
        D_MODEL = 128
        D_STATE = 16
        D_CONV = 4
        D_INNER = 256
        DT_RANK = 16
        BN = 64
        M = 32
        PARAM_NAMES = ['in_proj_w', 'conv_w', 'conv_b', 'x_proj_w', 'dt_proj_w', 'dt_proj_b', 'A_log', 'D', 'out_proj_w']

        def _mamba(x, in_proj_w, conv_w, conv_b, x_proj_w, dt_proj_w, dt_proj_b, A_log, Dvec, out_proj_w):
            xz = x @ in_proj_w.T
            xs, z = jnp.split(xz, 2, axis=-1)
            xs_pad = jnp.pad(xs, ((0, 0), (D_CONV - 1, 0), (0, 0)))
            kern = jnp.transpose(conv_w, (2, 1, 0))
            xs = jax.lax.conv_general_dilated(xs_pad, kern, (1,), 'VALID', dimension_numbers=('NWC', 'WIO', 'NWC'), feature_group_count=D_INNER) + conv_b
            xs = jax.nn.silu(xs)
            dbc = xs @ x_proj_w.T
            dt = jax.nn.softplus(dbc[..., :DT_RANK] @ dt_proj_w.T + dt_proj_b)
            Bm = dbc[..., DT_RANK:DT_RANK + D_STATE]
            Cm = dbc[..., DT_RANK + D_STATE:]
            A = -jnp.exp(A_log)
            dA = jnp.exp(dt[..., None] * A)
            dBu = dt[..., None] * Bm[:, :, None, :] * xs[..., None]

            def combine(c1, c2):
                a1, b1 = c1
                a2, b2 = c2
                return (a1 * a2, a2 * b1 + b2)
            _, hs = jax.lax.associative_scan(combine, (dA, dBu), axis=1)
            y = jnp.einsum('blds,bls->bld', hs, Cm) + xs * Dvec
            y = y * jax.nn.silu(z)
            return y @ out_proj_w.T

        def _core(x, ln_gamma, ln_beta, fp, bp):
            mu = x.mean(-1, keepdims=True)
            var = x.var(-1, keepdims=True)
            xn = (x - mu) / jnp.sqrt(var + 1e-05) * ln_gamma + ln_beta
            y_fwd = _mamba(xn, *fp)
            y_bwd = jnp.flip(_mamba(jnp.flip(xn, 1), *bp), 1)
            return y_fwd + y_bwd + x

        def _mamba_params(key):
            ks = jax.random.split(key, 5)
            s = 0.02
            return {'in_proj_w': jax.random.normal(ks[0], (2 * D_INNER, D_MODEL)) * s, 'conv_w': jax.random.normal(ks[1], (D_INNER, 1, D_CONV)) * s, 'conv_b': jnp.zeros((D_INNER,)), 'x_proj_w': jax.random.normal(ks[2], (DT_RANK + 2 * D_STATE, D_INNER)) * s, 'dt_proj_w': jax.random.normal(ks[3], (D_INNER, DT_RANK)) * s, 'dt_proj_b': jnp.full((D_INNER,), -4.6), 'A_log': jnp.log(jnp.tile(jnp.arange(1, D_STATE + 1, dtype=jnp.float32), (D_INNER, 1))), 'D': jnp.ones((D_INNER,)), 'out_proj_w': jax.random.normal(ks[4], (D_MODEL, D_INNER)) * s}
        fp = (f_in_proj_w, f_conv_w, f_conv_b, f_x_proj_w, f_dt_proj_w, f_dt_proj_b, f_A_log, f_D, f_out_proj_w)
        bp = (b_in_proj_w, b_conv_w, b_conv_b, b_x_proj_w, b_dt_proj_w, b_dt_proj_b, b_A_log, b_D, b_out_proj_w)
        return _core(x, ln_gamma, ln_beta, fp, bp)

    def _L1_ffn_ref(input_embeddings, router_w, w1, b1, w2, b2):
        import jax, jax.numpy as jnp
        import numpy as np
        NUM_EXPERTS = 8
        TOP_K = 2
        B, S, D = (8, 4096, 128)

        def _moe(tokens, router_w, w1, b1, w2, b2):
            N = tokens.shape[0]
            E = router_w.shape[0]
            logits = tokens.astype(jnp.float32) @ router_w.astype(jnp.float32).T
            probs = jax.nn.softmax(logits, axis=-1)
            rw, re = jax.lax.top_k(probs, TOP_K)
            if TOP_K > 1:
                rw = rw / jnp.maximum(rw.sum(-1, keepdims=True), 1e-12)
            rw = rw.astype(tokens.dtype)
            combine = jnp.zeros((N, E), tokens.dtype).at[jnp.arange(N)[:, None], re].set(rw)
            out = tokens
            for e in range(E):
                h = jax.nn.gelu(tokens @ w1[e] + b1[e], approximate=False)
                y = h @ w2[e] + b2[e]
                out = out + combine[:, e:e + 1] * y
            return out
        b, s, d = input_embeddings.shape
        tokens = input_embeddings.reshape(b * s, d)
        return _moe(tokens, router_w, w1, b1, w2, b2).reshape(b, s, d)

    def _gn(v, G=32, eps=1e-05):
        B_, C_, H_, W_ = v.shape
        g = v.reshape(B_, G, C_ // G, H_, W_)
        m = jnp.mean(g, axis=(2, 3, 4), keepdims=True)
        s = jnp.var(g, axis=(2, 3, 4), keepdims=True)
        return ((g - m) / jnp.sqrt(s + eps)).reshape(v.shape)

    def _ln_c(v, eps=1e-06):
        m = jnp.mean(v, axis=1, keepdims=True)
        s = jnp.var(v, axis=1, keepdims=True)
        return (v - m) / jnp.sqrt(s + eps)

    def _ln_t(v, eps=1e-05):
        m = jnp.mean(v, axis=-1, keepdims=True)
        s = jnp.var(v, axis=-1, keepdims=True)
        return (v - m) / jnp.sqrt(s + eps)

    def _to_tokens(v):
        B_, C_, H_, W_ = v.shape
        return v.reshape(B_, C_, H_ * W_).transpose(0, 2, 1)

    def _from_tokens(t, like):
        B_, C_, H_, W_ = like.shape
        return t.transpose(0, 2, 1).reshape(B_, C_, H_, W_)
    x = x + _L0_conv_ref(_gn(x), L0_conv_Wq, L0_conv_Wk, L0_conv_Wv)
    t = _to_tokens(x)
    t = t + _L1_attn_ref(_ln_t(t), L1_attn_ln_gamma, L1_attn_ln_beta, L1_attn_f_in_proj_w, L1_attn_f_conv_w, L1_attn_f_conv_b, L1_attn_f_x_proj_w, L1_attn_f_dt_proj_w, L1_attn_f_dt_proj_b, L1_attn_f_A_log, L1_attn_f_D, L1_attn_f_out_proj_w, L1_attn_b_in_proj_w, L1_attn_b_conv_w, L1_attn_b_conv_b, L1_attn_b_x_proj_w, L1_attn_b_dt_proj_w, L1_attn_b_dt_proj_b, L1_attn_b_A_log, L1_attn_b_D, L1_attn_b_out_proj_w)
    t = t + _L1_ffn_ref(_ln_t(t), L1_ffn_router_w, L1_ffn_w1, L1_ffn_b1, L1_ffn_w2, L1_ffn_b2)
    x = _from_tokens(t, x)
    return x

_drawn_inputs = setup_inputs


def setup_inputs(seed=0):
    import zlib

    import numpy as np

    out = dict(_drawn_inputs(seed))
    spreads = {'L1_attn_ln_gamma': (1.0, 0.6),
     'L1_attn_ln_beta': (0.0, 0.8),
     'L1_attn_f_conv_b': (0.0, 0.8),
     'L1_attn_f_dt_proj_b': (-4.599999904632568, 0.6),
     'L1_attn_f_D': (1.0, 0.6),
     'L1_attn_b_conv_b': (0.0, 0.8),
     'L1_attn_b_dt_proj_b': (-4.599999904632568, 0.6),
     'L1_attn_b_D': (1.0, 0.6),
     'L1_ffn_b1': (0.0, 1.674),
     'L1_ffn_b2': (0.0, 1.124)}
    factors = {'L1_attn_f_in_proj_w': 8.0,
     'L1_attn_f_conv_w': 8.0,
     'L1_attn_f_x_proj_w': 8.0,
     'L1_attn_f_dt_proj_w': 8.0,
     'L1_attn_f_A_log': 8.0,
     'L1_attn_f_out_proj_w': 8.0,
     'L1_attn_b_in_proj_w': 8.0,
     'L1_attn_b_conv_w': 8.0,
     'L1_attn_b_x_proj_w': 8.0,
     'L1_attn_b_dt_proj_w': 8.0,
     'L1_attn_b_A_log': 8.0,
     'L1_attn_b_out_proj_w': 8.0}
    for name, (base, spread) in spreads.items():
        noise = np.random.default_rng([zlib.crc32(name.encode()), seed]).standard_normal(out[name].shape)
        drawn = base * np.exp(spread * noise) if base else spread * noise
        out[name] = jnp.asarray(drawn.astype(out[name].dtype))
    for name, factor in factors.items():
        out[name] = (out[name] * factor).astype(out[name].dtype)
    return out
```

```python
import concourse.bass as bass
from concourse import mybir
from contextlib import ExitStack
import math


def normal_tail(share):
    low, high = -9.0, 9.0
    for _ in range(60):
        mid = (low + high) / 2
        low, high = (mid, high) if 0.5 * math.erfc(mid / math.sqrt(2.0)) > share else (low, mid)
    return low


def hybrid_block(nc, t_in, out):
    F32, BF16 = mybir.dt.float32, mybir.dt.bfloat16
    ALU, ACT = mybir.AluOpType, mybir.ActivationFunctionType
    ds = bass.ds

    BATCH, C, H, W = t_in["x"].shape
    N = H * W
    P = 128
    TILES = N // P
    BANK = 512
    HALVES = N // BANK
    KEEP = max(1, int(0.1 * N))
    FULL_ROUNDS, LAST_ROUND = divmod(KEEP, 8)
    GROUP = C // 32
    D_INNER, D_STATE, DT_RANK, TAPS = 256, 16, 16, 4
    BLOCKS = D_INNER // P
    DIRS = 2
    EXPERTS = t_in["L1_ffn_router_w"].shape[0]
    UNITS = DIRS * BLOCKS * D_STATE
    BC = 2 * D_STATE
    PARTS = 3
    WINDOW = 16
    TARGET = KEEP - (WINDOW - 1) / 2
    Z0 = normal_tail(TARGET / N)
    DENSITY = math.exp(-Z0 * Z0 / 2) / math.sqrt(2 * math.pi)
    STEP = 1 / (N * DENSITY)
    DAMPING = (1.0, 0.6, 0.6)
    COUNTS = len(DAMPING) + 1
    ACT_TILES = 4
    REPLACED = -3.0e38
    CHOSEN = 3.0e38
    LN_EPS = 1e-5

    x_v = t_in["x"].rearrange("b c h w -> b c (h w)")
    out_v = out.rearrange("b c h w -> b c (h w)")

    ctx = ExitStack()
    with ctx:
        def sb(name, shape, dt=F32):
            return ctx.enter_context(nc.sbuf_tensor(name, shape, dt))

        def sem(name):
            return ctx.enter_context(nc.semaphore(name))

        ident = sb("ident", [P, P])
        ident_bf = sb("ident_bf", [P, P], BF16)
        group_avg = sb("group_avg", [P, P])
        pick = sb("pick", [PARTS * BC, BC, P], BF16)
        neg_half = sb("neg_half", [P, TILES])
        qk_w = sb("qk_w", [P, P])
        wv_t = sb("wv_t", [P, P])
        conv_in_t = sb("conv_in_t", [P, DIRS, BLOCKS, TAPS, P])
        z_in_t = sb("z_in_t", [P, DIRS, BLOCKS, P])
        xproj_t = sb("xproj_t", [P, DIRS, BLOCKS, P])
        dtproj_t = sb("dtproj_t", [P, DIRS, BLOCKS, P])
        outproj_t = sb("outproj_t", [P, DIRS, BLOCKS, P])
        skip_diag = sb("skip_diag", [P, DIRS, BLOCKS, P])
        w1 = sb("w1", [P, EXPERTS, P])
        w2 = sb("w2", [P, EXPERTS, P])
        router_t = sb("router_t", [P, EXPERTS])
        b1_t = sb("b1_t", [P, EXPERTS])
        b2 = sb("b2", [EXPERTS, P])
        conv_w = sb("conv_w", [P, DIRS, BLOCKS, TAPS])
        VECS = 3 * DIRS * BLOCKS + 2
        vec = sb("vec", [P, VECS])
        conv_b, dt_b, skip = (vec[:, i * DIRS * BLOCKS:(i + 1) * DIRS * BLOCKS].rearrange("p (d k) -> p d k", d=DIRS)
                              for i in range(3))
        gamma, beta = vec[:, VECS - 2:VECS - 1], vec[:, VECS - 1:VECS]
        decay = sb("decay", [P, DIRS, BLOCKS, D_STATE])
        raw_qkv = sb("raw_qkv", [P, 3, P])
        raw_vec = sb("raw_vec", [VECS, P])
        raw_small = sb("raw_small", [EXPERTS, 2, P])

        x_c = sb("x_c", [P, N])
        xn_c = sb("xn_c", [P, N])
        q_c = sb("q_c", [P, N])
        v_tok = sb("v_tok", [P, TILES, P])
        x_tok = sb("x_tok", [P, TILES, P])
        xk_c = sb("xk_c", [P, N])
        ring = sb("ring", [P, TILES, N])
        score = ring
        expo = sb("expo", [P, 2, N])
        work = sb("work", [P, 2, N])
        prob_t = sb("prob_t", [P, TILES, P])
        unused_a = sb("unused_a", [P, 2, N], BF16)
        unused_v = sb("unused_v", [P, 2, N], BF16)
        top8 = sb("top8", [P, 8])
        row_max = sb("row_max", [P, TILES])
        neg_max = sb("neg_max", [P, TILES])
        sum_sq = sb("sum_sq", [P, TILES])
        score_var = sb("score_var", [P, TILES])
        score_std = sb("score_std", [P, TILES])
        correction = sb("correction", [P, TILES])
        thresh = sb("thresh", [P, TILES])
        neg_thresh = sb("neg_thresh", [P, TILES])
        count = sb("count", [P, TILES])
        delta = sb("delta", [P, TILES])
        rank = sb("rank", [P, TILES])
        ladder = sb("ladder", [P, TILES, WINDOW + 1])
        rungs = sb("rungs", [P, TILES, WINDOW])
        hit = sb("hit", [P, TILES, WINDOW])
        at_rank = sb("at_rank", [P, TILES, WINDOW])
        after_rank = sb("after_rank", [P, TILES, WINDOW])
        kept_from = sb("kept_from", [P, TILES])
        next_below = sb("next_below", [P, TILES])
        found = sb("found", [P, TILES])
        missed = sb("missed", [P, TILES])
        ones = sb("ones", [P, 1])
        half_pow = sb("half_pow", [P, TILES])
        gn_kbias = sb("gn_kbias", [P, 1])
        missed_tiles = sb("missed_tiles", [1, TILES + 1])
        missed_bits = missed_tiles[:, :].bitcast(mybir.dt.int32)
        row_sum = sb("row_sum", [P, 2])
        row_inv = sb("row_inv", [P, 2])
        gn_stats = sb("gn_stats", [P, 2, 6])
        gn_mv = sb("gn_mv", [P, 2])
        gn_dev = sb("gn_dev", [P, 1])
        gn_sq = sb("gn_sq", [P, 1])
        gn_mean = sb("gn_mean", [P, 1])
        gn_var = sb("gn_var", [P, 1])
        gn_scale = sb("gn_scale", [P, 1])
        gn_bias = sb("gn_bias", [P, 1])
        t1 = sb("t1", [P, TILES, P])
        ln_stats = sb("ln_stats", [P, 6])
        ln_mv = sb("ln_mv", [P, TILES, 2])
        ln_var = sb("ln_var", [P, TILES])
        ln_rstd = sb("ln_rstd", [P, TILES])
        ln_var2 = sb("ln_var2", [P, TILES])
        ln_rstd2 = sb("ln_rstd2", [P, TILES])
        xh_scale = sb("xh_scale", [P, TILES])
        xh_bias = sb("xh_bias", [P, TILES])
        tu_scale = sb("tu_scale", [P, TILES])
        tu_bias = sb("tu_bias", [P, TILES])
        xh = sb("xh", [P, TILES, P])
        tu = sb("tu", [P, TILES, P])

        PAD = TAPS - 1
        mx = sb("mx", [P, PAD + N + PAD])
        conv_half = work[:, 0, :]
        conv_tanh = work[:, 1, :]
        xs = sb("xs", [P, BLOCKS, N])
        z_tanh = expo[:, 0, :]
        z_raw = expo[:, 1, :]
        gate = sb("gate", [P, DIRS, BLOCKS, N])
        dbc = sb("dbc", [P, N])
        bc_parts = sb("bc_parts", [PARTS * BC, N], BF16)
        bc_rest = sb("bc_rest", [PARTS * BC, N])
        bc_mid = sb("bc_mid", [PARTS * BC, N], BF16)
        dt_abs = conv_half
        dt_pos = conv_tanh
        dt_exp = z_tanh
        dt_log = z_raw
        dt = sb("dt", [P, BLOCKS, N])
        dtx = sb("dtx", [P, BLOCKS, N])
        dA, c_all, hs, hc = (ring[:, 2 * i:2 * i + 2, :] for i in range(4))

        tap_w = hc[:, :, :].rearrange("p a (j c) -> p (a j) c", c=P)
        raw_in = hs[:, 0, :].rearrange("p (d k c) -> p d k c", d=DIRS, k=2 * BLOCKS)
        raw_xproj = hs[:, 1, 0:BANK].rearrange("p (d c) -> p d c", d=DIRS)
        raw_out = hs[:, 1, BANK:N].rearrange("p (d c) -> p d c", d=DIRS)
        raw_dtproj = c_all[:, 0, 0:BANK].rearrange("p (d k c) -> p d k c", d=DIRS, k=BLOCKS)

        t2 = x_tok
        t2e = t1
        en = xh
        e_c = q_c
        logits = sb("logits", [P, TILES, 2 * EXPERTS])
        marked = sb("marked", [P, TILES, 2 * EXPERTS])
        r8 = sb("r8", [P, TILES, 8])
        rexp = sb("rexp", [P, TILES, EXPERTS])
        rsum = sb("rsum", [P, TILES])
        comb = sb("comb", [P, TILES, EXPERTS])
        comb_parts = sb("comb_parts", [P, TILES, PARTS * BC], BF16)
        comb_rest = sb("comb_rest", [P, TILES, EXPERTS])
        comb_t = dbc[0:EXPERTS, :]
        comb_parts_t = bc_parts
        act_e = hs
        sel_e = dA
        out_c = v_tok

        ps = [ctx.enter_context(nc.psum_tensor(f"ps{i}", [P, N], F32)) for i in range(4)]
        ps01, ps23, ps45, ps67 = ps

        w_loaded = sem("w_loaded")
        const_step = sem("const_step")
        waits_passed = sem("waits_passed")
        const_done = sem("const_done")
        setup_cleared = sem("setup_cleared")
        setup_t = sem("setup_t")
        setup_evac = sem("setup_evac")
        setup_taps = sem("setup_taps")
        setup_act = sem("setup_act")
        vstep = sem("vstep")
        astep = sem("astep")
        gstep = sem("gstep")
        x_loaded = sem("x_loaded")
        gn_dev_ready = sem("gn_dev_ready")
        gn_mean_ready = sem("gn_mean_ready")
        gn_vec_ready = sem("gn_vec_ready")
        gn_sq_ready = sem("gn_sq_ready")
        gn_pow = sem("gn_pow")
        gn_coef = sem("gn_coef")
        xtok_t = sem("xtok_t")
        xtok_copied = sem("xtok_copied")
        xn_ready = sem("xn_ready")
        qv_ready = sem("qv_ready")
        qv_copied = sem("qv_copied")
        scores_ready = sem("scores_ready")
        scores_copied = sem("scores_copied")
        squares_ready = sem("squares_ready")
        score_var_ready = sem("score_var_ready")
        score_std_ready = sem("score_std_ready")
        thresh_ready = sem("thresh_ready")
        counted = sem("counted")
        missed_ready = sem("missed_ready")
        missed_summed = sem("missed_summed")
        exact_step = sem("exact_step")
        neg_max_ready = sem("neg_max_ready")
        exp_ready = sem("exp_ready")
        prob_ready = sem("prob_ready")
        prob_transposed = sem("prob_transposed")
        probt_copied = sem("probt_copied")
        attn_ready = sem("attn_ready")
        t1_ready = sem("t1_ready")
        var_ready = sem("var_ready")
        rstd_ready = sem("rstd_ready")
        var2_ready = sem("var2_ready")
        rstd2_ready = sem("rstd2_ready")
        ln_coef = sem("ln_coef")
        xh_ready = sem("xh_ready")
        xh_t = sem("xh_t")
        tu_ready = sem("tu_ready")
        mx_ready = sem("mx_ready")
        pre_filled = sem("pre_filled")
        pre_read = sem("pre_read")
        conv_acts = sem("conv_acts")
        xs_ready = sem("xs_ready")
        z_acts = sem("z_acts")
        gate_ready = sem("gate_ready")
        hi_ready = sem("hi_ready")
        rest_ready = sem("rest_ready")
        mid_ready = sem("mid_ready")
        parts_ready = sem("parts_ready")
        dt_acts = sem("dt_acts")
        dt_ready = sem("dt_ready")
        dtx_ready = sem("dtx_ready")
        b_ready = sem("b_ready")
        dbu_ready = sem("dbu_ready")
        c_ready = sem("c_ready")
        c_copied = sem("c_copied")
        dA_ready = sem("dA_ready")
        scan_ready = sem("scan_ready")
        hc_ready = sem("hc_ready")
        y_added = sem("y_added")
        y_ready = sem("y_ready")
        gated = sem("gated")
        mamba_out = sem("mamba_out")
        t2_ready = sem("t2_ready")
        var3_ready = sem("var3_ready")
        rstd3_ready = sem("rstd3_ready")
        ln3_coef = sem("ln3_coef")
        en_ready = sem("en_ready")
        en_t = sem("en_t")
        ec_ready = sem("ec_ready")
        t2e_ready = sem("t2e_ready")
        logits_ready = sem("logits_ready")
        rdiff_ready = sem("rdiff_ready")
        rexp_ready = sem("rexp_ready")
        comb_ready = sem("comb_ready")
        comb_transposed = sem("comb_transposed")
        comb_copied = sem("comb_copied")
        hidden_ready = sem("hidden_ready")
        gelu_ready = sem("gelu_ready")
        weight_ready = sem("weight_ready")
        sel_ready = sem("sel_ready")
        expert_added = sem("expert_added")
        out_copied = sem("out_copied")
        out_stored = sem("out_stored")

        block = ctx.enter_context(nc.Block())

        def halves(tile):
            return [tile[:, h * BANK:(h + 1) * BANK] for h in range(HALVES)]

        WAYS = ["f", "b"]
        jobs = [(raw_qkv[:, 2, :], wv_t[:, :], 1.0)]
        for d in range(DIRS):
            for k in range(BLOCKS):
                for j in range(TAPS):
                    jobs.append((tap_w[:, (d * BLOCKS + k) * TAPS + j, :], conv_in_t[:, d, k, j, :], 0.5))
                jobs.append((raw_in[:, d, BLOCKS + k, :], z_in_t[:, d, k, :], 1.0))
                jobs.append((raw_xproj[:, d, k * P:(k + 1) * P], xproj_t[:, d, k, :], 1.0))
                jobs.append((raw_dtproj[:, d, k, :], dtproj_t[:, d, k, :], 1.0))
                jobs.append((raw_out[:, d, k * P:(k + 1) * P], outproj_t[:, d, k, :], 0.5))
        jobs.append((raw_vec[:, :], vec[:, :], 1.0))
        jobs.append((raw_small[:, 0, :], router_t[:, :], 1.0))
        jobs.append((raw_small[:, 1, :], b1_t[:, :], 1.0))
        QK_JOB = len(jobs)
        N_LOADS = 32

        CONSTS = 10 + WINDOW

        def passed(eng):
            eng.sem_inc(waits_passed, 1)

        @block.sync
        def _(sp):
            loads = 0

            def load(dst, src):
                sp.dma_start(dst, src).then_inc(w_loaded, 16)

            for i, name in enumerate(("Wq", "Wk", "Wv")):
                load(raw_qkv[:, i, :], t_in["L0_conv_" + name][:, :])
            sp.wait_ge(setup_cleared, 2)
            loads = 3
            for d, way in enumerate(WAYS):
                g = lambda s: t_in[f"L1_attn_{way}_{s}"]
                xp = g("x_proj_w")
                for part in range(PARTS):
                    load(raw_xproj[part * BC:(part + 1) * BC, d, :], xp[DT_RANK:DT_RANK + BC, :])
                load(raw_xproj[PARTS * BC:PARTS * BC + DT_RANK, d, :], xp[0:DT_RANK, :])
                load(raw_dtproj[:, d, :, PARTS * BC:PARTS * BC + DT_RANK],
                     g("dt_proj_w").rearrange("(k p) r -> p k r", p=P))
                load(raw_in[:, d, :, :], g("in_proj_w").rearrange("(k p) c -> p k c", p=P))
                load(raw_out[:, d, :], g("out_proj_w")[:, :])
                load(conv_w[:, d, :, :], g("conv_w").rearrange("(k p) o j -> p k (o j)", p=P))
                for i, name in enumerate(("conv_b", "dt_proj_b", "D")):
                    row = (i * DIRS + d) * BLOCKS
                    load(raw_vec[row:row + BLOCKS, :], g(name).rearrange("(k p) -> k p", p=P))
                load(decay[:, d, :, :], g("A_log").rearrange("(k p) s -> p k s", p=P))
                loads += 12
            load(w1[:, :, :], t_in["L1_ffn_w1"].rearrange("e d f -> d e f"))
            load(w2[:, :, :], t_in["L1_ffn_w2"].rearrange("e f d -> f e d"))
            load(raw_small[:, 0, :], t_in["L1_ffn_router_w"][:, :])
            load(raw_small[:, 1, :], t_in["L1_ffn_b1"][:, :])
            load(b2[:, :], t_in["L1_ffn_b2"][:, :])
            load(raw_vec[VECS - 2:VECS - 1, :], t_in["L1_attn_ln_gamma"].rearrange("(o p) -> o p", o=1))
            load(raw_vec[VECS - 1:VECS, :], t_in["L1_attn_ln_beta"].rearrange("(o p) -> o p", o=1))
            loads += 7
            assert loads == N_LOADS + 2, loads
            def sp_image(b):
                sp.wait_ge(xn_ready, 2 * b)
                sp.dma_start(x_c[:, :], x_v[ds(b, 1), :, :].rearrange("o c n -> (o c) n")).then_inc(x_loaded, 16)
                sp.wait_ge(out_copied, b + 1)
                passed(sp)
                sp.dma_start(out_v[ds(b, 1), :, :].rearrange("o c n -> (o c) n"),
                             out_c[:, :, :].rearrange("p a b -> p (a b)")).then_inc(out_stored, 16)
                sp.wait_ge(out_stored, 16 * (b + 1))
                passed(sp)

            sp_image(0)
            with sp.Fori(1, BATCH) as b:
                sp_image(b)

        @block.gpsimd
        def _(pool):
            pool.memset(raw_xproj[:, :, :], 0.0).then_inc(setup_cleared, 1)
            pool.memset(raw_dtproj[:, :, :, :], 0.0).then_inc(setup_cleared, 1)
            pool.memset(neg_half[:, :], -0.5).then_inc(const_done, 1)
            pool.memset(half_pow[:, :], 0.5).then_inc(const_done, 1)
            pool.memset(ones[:, :], 1.0).then_inc(const_done, 1)
            for j in range(WINDOW):
                pool.memset(rungs[:, :, j], float(j)).then_inc(const_done, 1)
            pool.memset(mx[:, :], 0.0).then_inc(const_done, 1)
            pool.memset(logits[:, :, :], REPLACED).then_inc(const_done, 1)
            pool.memset(comb_parts[:, :, :], 0.0).then_inc(const_done, 1)
            pool.memset(ident[:, :], 0.0).then_inc(const_step, 1)
            pool.memset(ident_bf[:, :], 0.0).then_inc(const_step, 1)
            pool.memset(group_avg[:, :], 1.0 / GROUP).then_inc(const_step, 1)
            pool.memset(pick[:, :, :], 0.0).then_inc(const_step, 1)
            pool.wait_ge(const_step, 4)
            for m in (ident, ident_bf):
                pool.affine_select(out=m[:, :], in_=m[:, :], compare_op=ALU.not_equal, fill=1.0, base=0,
                                   pattern=[[-1, P]], channel_multiplier=1).then_inc(const_done, 1)
            gv = group_avg[:, :].rearrange("p (g c) -> p g c", c=GROUP)
            pool.affine_select(out=gv, in_=gv, compare_op=ALU.is_ge, fill=0.0, base=0,
                               pattern=[[-GROUP, P // GROUP], [0, GROUP]], channel_multiplier=1).then_inc(const_step, 1)
            pool.wait_ge(const_step, 5)
            pool.affine_select(out=gv, in_=gv, compare_op=ALU.is_ge, fill=0.0, base=GROUP - 1,
                               pattern=[[GROUP, P // GROUP], [0, GROUP]], channel_multiplier=-1).then_inc(const_done, 1)
            for part in range(PARTS):
                pool.wait_ge(const_step, 5 + part)
                pool.affine_select(out=pick[:, :, :], in_=pick[:, :, :], compare_op=ALU.not_equal, fill=1.0,
                                   base=-part * BC, pattern=[[-1, BC], [0, P]],
                                   channel_multiplier=1).then_inc(const_step, 1)
            pool.wait_ge(const_step, 5 + PARTS)
            pool.memset(mx[:, 0:PAD], 0.0).then_inc(const_done, 1)

            def pool_image(b):
                pool.wait_ge(gn_sq_ready, 2 * b + 2)
                pool.tensor_tensor(gn_scale[:, :], gn_var[:, :], neg_half[:, 0:1], ALU.pow).then_inc(gn_pow, 1)
                pool.wait_ge(score_var_ready, b + 1)
                pool.tensor_tensor(score_std[:, :], score_var[:, :], half_pow[:, :], ALU.pow).then_inc(score_std_ready, 1)
                pool.wait_ge(var_ready, b + 1)
                pool.tensor_tensor(ln_rstd[:, :], ln_var[:, :], neg_half[:, :], ALU.pow).then_inc(rstd_ready, 1)
                pool.wait_ge(var2_ready, b + 1)
                pool.tensor_tensor(ln_rstd2[:, :], ln_var2[:, :], neg_half[:, :], ALU.pow).then_inc(rstd2_ready, 1)
                pool.wait_ge(ln_coef, b + 1)
                passed(pool)
                for i in range(TILES):
                    pool.tensor_scalar(tu[:, i, :], t1[:, i, :], tu_scale[:, i:i + 1], tu_bias[:, i:i + 1],
                                       ALU.mult, ALU.add).then_inc(tu_ready, 1)
                for d in range(DIRS):
                    for k in range(BLOCKS):
                        g = b * (DIRS * BLOCKS) + d * BLOCKS + k
                        pool.wait_ge(z_acts, 2 * g + 2)
                        passed(pool)
                        pool.tensor_scalar(z_tanh[:, :], z_tanh[:, :], 1.0, None, ALU.add).then_inc(gstep, 1)
                        pool.wait_ge(gstep, 2 * g + 1)
                        pool.tensor_tensor(gate[:, d, k, :], z_tanh[:, :], z_raw[:, :], ALU.mult).then_inc(gstep, 1)
                        pool.wait_ge(gstep, 2 * g + 2)
                        pool.sem_inc(gate_ready, 1)
                    pool.wait_ge(mid_ready, 2 * (b * DIRS + d) + 2)
                    pool.tensor_tensor(bc_parts[2 * BC:3 * BC, :], bc_rest[2 * BC:3 * BC, :],
                                       bc_mid[2 * BC:3 * BC, :], ALU.subtract).then_inc(parts_ready, 1)
                    pool.wait_ge(parts_ready, b * DIRS + d + 1)
                    for k in range(BLOCKS):
                        g = b * (DIRS * BLOCKS) + d * BLOCKS + k
                        pool.wait_ge(dt_acts, 2 * g + 2)
                        pool.wait_ge(scan_ready, b * UNITS + d * BLOCKS * D_STATE)
                        pool.tensor_tensor(dt[:, k, :], dt_pos[:, :], dt_log[:, :], ALU.add).then_inc(dt_ready, 1)
                        pool.wait_ge(dt_ready, g + 1)
                        pool.tensor_tensor(dtx[:, k, :], dt[:, k, :], xs[:, k, :], ALU.mult).then_inc(dtx_ready, 1)
                    for k in range(BLOCKS):
                        base = b * UNITS + (d * BLOCKS + k) * D_STATE
                        first = d == 0 and k == 0

                        def weigh(s, j, early):
                            pool.wait_ge(scan_ready, base + s + 1)
                            pool.wait_ge(c_copied, base + s + 1)
                            pool.wait_ge(y_added, base + s - (0 if early else 1))
                            pool.tensor_tensor(hc[:, j, :], hs[:, j, :], c_all[:, j, :], ALU.mult).then_inc(hc_ready, 1)

                        weigh(0, 0, first)
                        weigh(1, 1, False)
                        with pool.Fori(1, D_STATE // 2) as r:
                            for j in range(2):
                                weigh(2 * r + j, j, False)
                pool.wait_ge(var3_ready, b + 1)
                pool.tensor_tensor(ln_rstd[:, :], ln_var[:, :], neg_half[:, :], ALU.pow).then_inc(rstd3_ready, 1)
                for i in range(TILES):
                    pool.wait_ge(en_ready, TILES * b + i + 1)
                    pool.tensor_tensor(t2e[:, i, :], t2[:, i, :], en[:, i, :], ALU.add).then_inc(t2e_ready, 1)

            pool_image(0)
            with pool.Fori(1, BATCH) as b:
                pool_image(b)

        @block.scalar
        def _(act):
            def copy(dst, src, **kw):
                return nc.scalar.activation(dst, src, ACT.Copy, **kw)

            act.wait_ge(w_loaded, 16 * (N_LOADS + 2))
            flat = decay[:, :, :, :].rearrange("p d k s -> p (d k s)")
            nc.scalar.activation(flat, flat, ACT.Exp).then_inc(setup_act, 1)
            act.wait_ge(setup_act, 1)
            nc.scalar.mul(flat, flat, -1.0).then_inc(setup_act, 1)
            act.wait_ge(setup_act, 2)
            act.wait_ge(setup_evac, QK_JOB + 1)
            act.wait_ge(setup_taps, DIRS * BLOCKS * (TAPS + 1) + 1)
            act.wait_ge(const_done, CONSTS)

            def act_image(b):
                act.wait_ge(xtok_t, b + 1)
                copy(x_tok[:, :, :].rearrange("p a c -> p (a c)"), ps67[:, :]).then_inc(xtok_copied, 1)
                act.wait_ge(gn_coef, b + 1)
                nc.scalar.activation(xn_c[:, :], x_c[:, :], ACT.Identity, bias=gn_bias[:, 0:1],
                                     scale=gn_scale[:, 0:1]).then_inc(xn_ready, 1)
                nc.scalar.activation(xk_c[:, :], x_c[:, :], ACT.Identity, bias=gn_kbias[:, 0:1],
                                     scale=gn_scale[:, 0:1]).then_inc(xn_ready, 1)
                act.wait_ge(qv_ready, 2 * b + 1)
                copy(q_c[:, :], ps01[:, :]).then_inc(qv_copied, 1)
                act.wait_ge(qv_ready, 2 * b + 2)
                copy(v_tok[:, :, :].rearrange("p a c -> p (a c)"), ps67[:, :]).then_inc(qv_copied, 1)

                for i in range(TILES):
                    n = b * TILES + i
                    act.wait_ge(scores_copied, n + 1)
                    act.wait_ge(squares_ready, b * TILES + max(i - 1, 0))
                    nc.scalar.activation(unused_a[:, i % 2, :], score[:, i, :], ACT.Square,
                                         accum_out=sum_sq[:, i:i + 1]).then_inc(squares_ready, 1)
                for c in range(COUNTS):
                    act.wait_ge(thresh_ready, b * COUNTS + c + 1)
                    if c == 0:
                        act.wait_ge(squares_ready, TILES * (b + 1))
                    for i in range(ACT_TILES):
                        act.wait_ge(counted, (b * COUNTS + c) * ACT_TILES + max(i - 1, 0))
                        nc.scalar.activation(unused_a[:, i % 2, :], score[:, i, :], ACT.Sign,
                                             bias=neg_thresh[:, i:i + 1],
                                             accum_out=count[:, i:i + 1]).then_inc(counted, 1)

                def exponent(i):
                    act.wait_ge(prob_transposed, b * TILES + max(i - 1, 0))
                    nc.scalar.activation(expo[:, i % 2, :], score[:, i, :], ACT.Exp,
                                         bias=neg_max[:, i:i + 1]).then_inc(exp_ready, 1)

                act.wait_ge(neg_max_ready, b + 1)
                exponent(0)
                for i in range(TILES):
                    n = b * TILES + i
                    if i + 1 < TILES:
                        exponent(i + 1)
                    act.wait_ge(prob_transposed, n + 1)
                    act.wait_ge(attn_ready, n)
                    copy(prob_t[:, :, :].rearrange("p a c -> p (a c)"), ps[1 + i % 2][:, :]).then_inc(probt_copied, 1)
                act.wait_ge(ln_coef, b + 1)
                for i in range(TILES):
                    nc.scalar.activation(xh[:, i, :], t1[:, i, :], ACT.Identity, bias=xh_bias[:, i:i + 1],
                                         scale=xh_scale[:, i:i + 1]).then_inc(xh_ready, 1)
                act.wait_ge(xh_t, b + 1)
                nc.scalar.activation(mx[:, PAD:PAD + N], ps01[:, :], ACT.Identity, bias=beta[:, 0:1],
                                     scale=gamma[:, 0:1]).then_inc(mx_ready, 1)
                for d in range(DIRS):
                    fills = (b * DIRS + d) * (3 * BLOCKS + 1)

                    for k in range(BLOCKS):
                        g = b * (DIRS * BLOCKS) + d * BLOCKS + k
                        act.wait_ge(pre_filled, fills + k + 1)
                        act.wait_ge(xs_ready, g)
                        if k == 0:
                            act.wait_ge(dtx_ready, g)
                        src = ps[1 + 2 * (k % 2)]
                        nc.scalar.activation(conv_half[:, :], src[:, :], ACT.Identity,
                                             bias=conv_b[:, d, k:k + 1]).then_inc(conv_acts, 1)
                        nc.scalar.activation(conv_tanh[:, :], src[:, :], ACT.Tanh,
                                             bias=conv_b[:, d, k:k + 1]).then_inc(conv_acts, 1)
                        act.wait_ge(conv_acts, 2 * g + 2)
                        act.sem_inc(pre_read, 1)
                    for k in range(BLOCKS):
                        g = b * (DIRS * BLOCKS) + d * BLOCKS + k
                        act.wait_ge(pre_filled, fills + BLOCKS + k + 1)
                        act.wait_ge(gate_ready, g)
                        src = ps[1 + 2 * (k % 2)]
                        nc.scalar.activation(z_tanh[:, :], src[:, :], ACT.Tanh, scale=0.5).then_inc(z_acts, 1)
                        copy(z_raw[:, :], src[:, :]).then_inc(z_acts, 1)
                        act.wait_ge(z_acts, 2 * g + 2)
                        act.sem_inc(pre_read, 1)
                    e = b * DIRS + d
                    act.wait_ge(pre_filled, fills + 2 * BLOCKS + 1)
                    copy(dbc[:, :], ps23[:, :]).then_inc(hi_ready, 1)
                    copy(bc_parts[:, :], ps23[0:PARTS * BC, :]).then_inc(hi_ready, 1)
                    act.wait_ge(hi_ready, 2 * e + 2)
                    act.sem_inc(pre_read, 1)
                    act.wait_ge(rest_ready, e + 1)
                    copy(bc_parts[BC:2 * BC, :], bc_rest[BC:2 * BC, :]).then_inc(mid_ready, 1)
                    copy(bc_mid[2 * BC:3 * BC, :], bc_rest[2 * BC:3 * BC, :]).then_inc(mid_ready, 1)
                    for k in range(BLOCKS):
                        g = b * (DIRS * BLOCKS) + d * BLOCKS + k
                        act.wait_ge(pre_filled, fills + 2 * BLOCKS + 2 + k)
                        act.wait_ge(xs_ready, (b * DIRS + d + 1) * BLOCKS)
                        act.wait_ge(gate_ready, (b * DIRS + d + 1) * BLOCKS)
                        act.wait_ge(dt_ready, g)
                        src = ps[3 - 2 * (k % 2)]
                        bias = dt_b[:, d, k:k + 1]
                        nc.scalar.activation(dt_pos[:, :], src[:, :], ACT.Relu, bias=bias).then_inc(dt_acts, 1)
                        nc.scalar.activation(dt_abs[:, :], src[:, :], ACT.Abs, bias=bias).then_inc(astep, 1)
                        act.wait_ge(astep, 2 * g + 1)
                        act.sem_inc(pre_read, 1)
                        nc.scalar.activation(dt_exp[:, :], dt_abs[:, :], ACT.Exp, scale=-1.0).then_inc(astep, 1)
                        act.wait_ge(astep, 2 * g + 2)
                        nc.scalar.activation(dt_log[:, :], dt_exp[:, :], ACT.Ln, bias=1.0).then_inc(dt_acts, 1)
                    for k in range(BLOCKS):
                        base = b * UNITS + (d * BLOCKS + k) * D_STATE
                        first = d == 0 and k == 0
                        act.wait_ge(dt_ready, (b * DIRS + d) * BLOCKS + k + 1)

                        def decay_and_c(s, j, early):
                            act.wait_ge(scan_ready, base + s - (0 if early else 1))
                            nc.scalar.activation(dA[:, j, :], dt[:, k, :], ACT.Exp,
                                                 scale=decay[:, d, k, ds(s, 1)]).then_inc(dA_ready, 1)
                            act.wait_ge(c_ready, base + s + 1)
                            act.wait_ge(hc_ready, base + s - (0 if early else 1))
                            copy(c_all[:, j, :], ps67[:, :]).then_inc(c_copied, 1)

                        decay_and_c(0, 0, first)
                        decay_and_c(1, 1, False)
                        with act.Fori(1, D_STATE // 2) as r:
                            for j in range(2):
                                decay_and_c(2 * r + j, j, False)
                act.wait_ge(ln3_coef, b + 1)
                for i in range(TILES):
                    nc.scalar.activation(en[:, i, :], t2[:, i, :], ACT.Identity, bias=xh_bias[:, i:i + 1],
                                         scale=xh_scale[:, i:i + 1]).then_inc(en_ready, 1)
                act.wait_ge(en_t, b + 1)
                copy(e_c[:, :], ps67[:, :]).then_inc(ec_ready, 1)
                act.wait_ge(rdiff_ready, b + 1)
                nc.scalar.activation(rexp[:, :, :], rexp[:, :, :], ACT.Exp).then_inc(rexp_ready, 1)
                act.wait_ge(comb_transposed, 2 * b + 1)
                copy(comb_t[:, :], ps45[0:EXPERTS, :]).then_inc(comb_copied, 1)
                act.wait_ge(comb_transposed, 2 * b + 2)
                copy(comb_parts_t[:, :], ps67[0:PARTS * BC, :].bitcast(BF16)[:, 0:N]).then_inc(comb_copied, 1)
                for x in range(EXPERTS):
                    n = b * EXPERTS + x
                    act.wait_ge(hidden_ready, n + 1)
                    act.wait_ge(sel_ready, n - 1 if x else b * EXPERTS)
                    nc.scalar.activation(act_e[:, x % 2, :], ps[1 + 2 * (x % 2)][:, :], ACT.Gelu,
                                         bias=b1_t[:, x:x + 1]).then_inc(gelu_ready, 1)
                act.wait_ge(expert_added, (b + 1) * EXPERTS)
                act.wait_ge(out_stored, 16 * b)
                copy(out_c[:, :, :].rearrange("p a c -> p (a c)"), ps01[:, :]).then_inc(out_copied, 1)

            act_image(0)
            with act.Fori(1, BATCH) as b:
                act_image(b)

        @block.vector
        def _(dve):
            v = nc.vector
            dve.wait_ge(w_loaded, 16 * (N_LOADS + 2))
            dve.wait_ge(const_done, CONSTS)
            for d in range(DIRS):
                for k in range(BLOCKS):
                    for j in range(TAPS):
                        v.tensor_scalar(tap_w[:, (d * BLOCKS + k) * TAPS + j, :], raw_in[:, d, k, :],
                                        conv_w[:, d, k, j:j + 1], None, ALU.mult).then_inc(setup_taps, 1)
            for n, (src, dst, factor) in enumerate(jobs):
                dve.wait_ge(setup_t, n + 1)
                v.tensor_scalar(dst, ps[n % 4][:, 0:dst.shape[1]], factor, None, ALU.mult).then_inc(setup_evac, 1)
            dve.wait_ge(setup_t, QK_JOB + 1)
            v.tensor_scalar(qk_w[:, :], ps[QK_JOB % 4][:, 0:P], float(C) ** -0.5, None, ALU.mult).then_inc(setup_evac, 1)
            dve.wait_ge(setup_evac, QK_JOB + 1)
            for d in range(DIRS):
                for k in range(BLOCKS):
                    v.tensor_scalar(skip_diag[:, d, k, :], ident[:, :], skip[:, d, k:k + 1], None,
                                    ALU.mult).then_inc(setup_taps, 1)
            v.tensor_scalar(vec[:, 0:DIRS * BLOCKS], vec[:, 0:DIRS * BLOCKS], 0.5, None,
                            ALU.mult).then_inc(setup_taps, 1)

            state = {"n": 0}

            def link(ins):
                state["n"] += 1
                ins.then_inc(vstep, 1)
                dve.wait_ge(vstep, state["b"] * V_STEPS + state["n"])
                passed(dve)

            def step(ins):
                state["n"] += 1
                ins.then_inc(vstep, 1)

            def after():
                dve.wait_ge(vstep, state["b"] * V_STEPS + state["n"] - 1)
                passed(dve)

            def settle():
                dve.wait_ge(vstep, state["b"] * V_STEPS + state["n"])
                passed(dve)

            V_STEPS = 27 + 2 * COUNTS + COUNTS * (TILES - ACT_TILES) + 11 * TILES

            def dve_image(b):
                state["b"], state["n"] = b, 0
                dve.wait_ge(x_loaded, 16 * (b + 1))
                for h, part in enumerate(halves(x_c)):
                    last = v.bn_stats(gn_stats[:, h, :], part)
                    link(last)
                link(v.bn_aggr(gn_mv[:, :], gn_stats[:, :, :].rearrange("p a s -> p (a s)")))
                dve.sem_inc(gn_dev_ready, 1)
                dve.wait_ge(gn_mean_ready, 2 * b + 1)
                link(v.tensor_copy(gn_mean[:, :], ps45[:, 0:1]))
                link(v.tensor_tensor(gn_dev[:, :], gn_mv[:, 0:1], gn_mean[:, :], ALU.subtract))
                v.scalar_tensor_tensor(gn_sq[:, :], gn_dev[:, :], gn_dev[:, 0:1], gn_mv[:, 1:2], ALU.mult,
                                       ALU.add).then_inc(gn_sq_ready, 1)
                dve.wait_ge(gn_mean_ready, 2 * b + 2)
                v.tensor_scalar(gn_var[:, :], ps45[:, 0:1], 1e-5, None, ALU.add).then_inc(gn_sq_ready, 1)
                dve.wait_ge(gn_pow, b + 1)
                v.scalar_tensor_tensor(gn_kbias[:, :], gn_mv[:, 0:1], -1.0, gn_scale[:, :], ALU.mult, ALU.mult)
                v.scalar_tensor_tensor(gn_bias[:, :], gn_mean[:, :], -1.0, gn_scale[:, :], ALU.mult,
                                       ALU.mult).then_inc(gn_coef, 1)

                def attended(i):
                    n = b * TILES + i
                    dve.wait_ge(attn_ready, n + 1)
                    dve.wait_ge(xtok_copied, b + 1)
                    link(v.scalar_tensor_tensor(t1[:, i, :], ps67[:, i % 2 * BANK:i % 2 * BANK + P], row_inv[:, i % 2:i % 2 + 1],
                                                x_tok[:, i, :], ALU.mult, ALU.add))
                    dve.sem_inc(t1_ready, 1)
                    link(v.bn_stats(ln_stats[:, :], t1[:, i, :]))
                    link(v.bn_aggr(ln_mv[:, i, :], ln_stats[:, :]))

                for i in range(TILES):
                    n = b * TILES + i
                    dve.wait_ge(scores_ready, n + 1)
                    dve.wait_ge(expert_added, b * EXPERTS)
                    v.tensor_scalar(score[:, i, :], ps[(i + 1) % 2][:, :], 0.0, None, ALU.add, ALU.max,
                                    accum_out=row_max[:, i:i + 1]).then_inc(scores_copied, 1)
                dve.wait_ge(scores_copied, TILES * (b + 1))
                v.tensor_scalar(neg_max[:, :], row_max[:, :], -1.0, None, ALU.mult).then_inc(neg_max_ready, 1)
                dve.wait_ge(squares_ready, TILES * (b + 1))
                v.tensor_scalar(score_var[:, :], sum_sq[:, :], 1.0 / N, None, ALU.mult).then_inc(score_var_ready, 1)
                dve.wait_ge(score_std_ready, b + 1)
                by_sign, by_count = slice(0, ACT_TILES), slice(ACT_TILES, TILES)
                v.tensor_scalar(correction[:, by_sign], score_std[:, by_sign], STEP / 2, None, ALU.mult)
                v.tensor_scalar(correction[:, by_count], score_std[:, by_count], STEP, None, ALU.mult)
                v.tensor_scalar(neg_thresh[:, :], score_std[:, :], -Z0, None, ALU.mult).then_inc(thresh_ready, 1)
                link(v.tensor_scalar(thresh[:, :], score_std[:, :], Z0, None, ALU.mult))
                for c in range(COUNTS):
                    for i in range(ACT_TILES, TILES):
                        after()
                        step(v.tensor_scalar(unused_v[:, i % 2, :], score[:, i, :], thresh[:, i:i + 1], None,
                                             ALU.is_ge, ALU.add, accum_out=count[:, i:i + 1]))
                    settle()
                    dve.wait_ge(counted, (b * COUNTS + c + 1) * ACT_TILES)
                    if c < COUNTS - 1:
                        v.scalar_tensor_tensor(delta[:, by_sign], count[:, by_sign], N - 2 * TARGET,
                                               correction[:, by_sign], ALU.add, ALU.mult)
                        link(v.scalar_tensor_tensor(delta[:, by_count], count[:, by_count], -TARGET,
                                                    correction[:, by_count], ALU.add, ALU.mult))
                        v.scalar_tensor_tensor(neg_thresh[:, :], delta[:, :], -DAMPING[c], neg_thresh[:, :],
                                               ALU.mult, ALU.add).then_inc(thresh_ready, 1)
                        link(v.scalar_tensor_tensor(thresh[:, :], delta[:, :], DAMPING[c], thresh[:, :],
                                                    ALU.mult, ALU.add))
                v.tensor_scalar(rank[:, by_sign], count[:, by_sign], -0.5, KEEP - N / 2, ALU.mult, ALU.add)
                v.tensor_scalar(rank[:, by_count], count[:, by_count], -1.0, float(KEEP), ALU.mult, ALU.add)
                link(v.tensor_copy(ladder[:, :, 0], thresh[:, :]))
                for i in range(0, TILES, 2):
                    pair = (i, i + 1)
                    for j in pair:
                        after()
                        step(v.scalar_tensor_tensor(work[:, j % 2, :], score[:, j, :], thresh[:, j:j + 1],
                                                    score[:, j, :], ALU.is_lt, ALU.mult))
                    for j in pair:
                        after()
                        step(v.max(ladder[:, j, 1:9], work[:, j % 2, :]))
                    for j in pair:
                        after()
                        step(v.match_replace(work[:, j % 2, :], ladder[:, j, 1:9], work[:, j % 2, :], REPLACED))
                    for j in pair:
                        after()
                        step(v.max(ladder[:, j, 9:17], work[:, j % 2, :]))
                settle()
                rank_b = rank[:, :].unsqueeze(2).to_broadcast([P, TILES, WINDOW])
                link(v.tensor_tensor(hit[:, :, :], rungs[:, :, :], rank_b, ALU.is_equal))
                v.tensor_tensor(at_rank[:, :, :], hit[:, :, :], ladder[:, :, 0:WINDOW], ALU.mult)
                link(v.tensor_tensor(after_rank[:, :, :], hit[:, :, :], ladder[:, :, 1:WINDOW + 1], ALU.mult))
                v.reduce_sum(kept_from[:, :], at_rank[:, :, :], axis=mybir.AxisListType.X)
                link(v.reduce_sum(next_below[:, :], after_rank[:, :, :], axis=mybir.AxisListType.X))
                link(v.tensor_tensor(found[:, :], kept_from[:, :], next_below[:, :], ALU.is_gt))
                link(v.scalar_tensor_tensor(found[:, :], kept_from[:, :], 0.0, found[:, :], ALU.is_gt, ALU.mult))
                v.tensor_scalar(missed[:, :], found[:, :], -1.0, 1.0, ALU.mult, ALU.add).then_inc(missed_ready, 1)
                dve.wait_ge(missed_summed, b + 1)
                v.tensor_copy(missed_tiles[:, 0:TILES], ps01[0:1, 0:TILES])
                link(v.reduce_sum(missed_tiles[:, TILES:TILES + 1], ps01[0:1, 0:TILES], axis=mybir.AxisListType.X))
                any_missed = dve.value_load(missed_bits[0:1, TILES:TILES + 1])

                def exact(i):
                    dve.sem_clear(exact_step)
                    v.tensor_copy(work[:, 0, :], score[:, i, :]).then_inc(exact_step, 1)
                    with dve.Fori(0, FULL_ROUNDS) as r:
                        dve.wait_ge(exact_step, 2 * r + 1)
                        passed(dve)
                        v.max(top8[:, :], work[:, 0, :]).then_inc(exact_step, 1)
                        dve.wait_ge(exact_step, 2 * r + 2)
                        passed(dve)
                        v.match_replace(work[:, 0, :], top8[:, :], work[:, 0, :], REPLACED).then_inc(exact_step, 1)
                    done = 2 * FULL_ROUNDS + 1
                    dve.wait_ge(exact_step, done)
                    v.max(top8[:, :], work[:, 0, :]).then_inc(exact_step, 1)
                    dve.wait_ge(exact_step, done + 1)
                    v.memset(top8[:, LAST_ROUND:8], REPLACED).then_inc(exact_step, 1)
                    dve.wait_ge(exact_step, done + 2)
                    v.match_replace(work[:, 0, :], top8[:, :], work[:, 0, :], REPLACED).then_inc(exact_step, 1)
                    dve.wait_ge(exact_step, done + 3)
                    v.tensor_scalar(score[:, i, :], work[:, 0, :], REPLACED, 0.5, ALU.is_equal,
                                    ALU.subtract).then_inc(exact_step, 1)
                    v.memset(kept_from[:, i:i + 1], 0.0).then_inc(exact_step, 1)
                    dve.wait_ge(exact_step, done + 5)

                for i in range(TILES):
                    n = b * TILES + i
                    dve.wait_ge(exp_ready, n + 1)
                    passed(dve)
                    with dve.If(any_missed != 0):
                        rows_missed = dve.value_load(missed_bits[0:1, i:i + 1])
                        with dve.If(rows_missed != 0):
                            exact(i)
                    link(v.scalar_tensor_tensor(expo[:, i % 2, :], score[:, i, :], kept_from[:, i:i + 1],
                                                expo[:, i % 2, :], ALU.is_ge, ALU.mult,
                                                accum_out=row_sum[:, i % 2:i % 2 + 1]))
                    dve.sem_inc(prob_ready, 1)
                    link(v.reciprocal(row_inv[:, i % 2:i % 2 + 1], row_sum[:, i % 2:i % 2 + 1]))
                    if i:
                        attended(i - 1)
                attended(TILES - 1)
                mean, var = ln_mv[:, :, 0], ln_mv[:, :, 1]
                v.tensor_scalar(ln_var[:, :], var, LN_EPS, None, ALU.add).then_inc(var_ready, 1)
                dve.wait_ge(rstd_ready, b + 1)
                link(v.tensor_tensor(ln_var2[:, :], var, ln_rstd[:, :], ALU.mult))
                link(v.tensor_tensor(ln_var2[:, :], ln_var2[:, :], ln_rstd[:, :], ALU.mult))
                v.tensor_scalar(ln_var2[:, :], ln_var2[:, :], LN_EPS, None, ALU.add).then_inc(var2_ready, 1)
                v.tensor_scalar(tu_scale[:, :], ln_rstd[:, :], 1.0, None, ALU.add)
                v.scalar_tensor_tensor(tu_bias[:, :], mean, -1.0, ln_rstd[:, :], ALU.mult, ALU.mult)
                dve.wait_ge(rstd2_ready, b + 1)
                link(v.tensor_tensor(xh_scale[:, :], ln_rstd[:, :], ln_rstd2[:, :], ALU.mult))
                v.scalar_tensor_tensor(xh_bias[:, :], mean, -1.0, xh_scale[:, :], ALU.mult,
                                       ALU.mult).then_inc(ln_coef, 1)

                for d in range(DIRS):
                    for k in range(BLOCKS):
                        g = b * (DIRS * BLOCKS) + d * BLOCKS + k
                        dve.wait_ge(conv_acts, 2 * g + 2)
                        dve.wait_ge(y_added, b * UNITS + d * BLOCKS * D_STATE)
                        dve.wait_ge(dtx_ready, (b * DIRS + d) * BLOCKS)
                        v.scalar_tensor_tensor(xs[:, k, :], conv_tanh[:, :], 1.0, conv_half[:, :], ALU.add,
                                               ALU.mult).then_inc(xs_ready, 1)
                    dve.wait_ge(hi_ready, 2 * (b * DIRS + d) + 2)
                    v.tensor_tensor(bc_rest[:, :], dbc[0:PARTS * BC, :], bc_parts[:, :],
                                    ALU.subtract).then_inc(rest_ready, 1)
                    for k in range(BLOCKS):
                        base = b * UNITS + (d * BLOCKS + k) * D_STATE
                        first = d == 0 and k == 0
                        dve.wait_ge(dtx_ready, (b * DIRS + d) * BLOCKS + k + 1)
                        order = slice(None) if d == 0 else slice(None, None, -1)

                        def scan(s, j, early):
                            dve.wait_ge(b_ready, base + s + 1)
                            dve.wait_ge(scan_ready, base + s)
                            v.tensor_tensor(ps45[:, :], dtx[:, k, :], ps23[:, :], ALU.mult).then_inc(dbu_ready, 1)
                            dve.wait_ge(dA_ready, base + s + 1)
                            dve.wait_ge(dbu_ready, base + s + 1)
                            dve.wait_ge(hc_ready, base + s - (0 if early else 1))
                            v.tensor_tensor_scan(hs[:, j, order], dA[:, j, order], ps45[:, order], 0.0,
                                                 ALU.mult, ALU.add).then_inc(scan_ready, 1)

                        scan(0, 0, first)
                        scan(1, 1, False)
                        with dve.Fori(1, D_STATE // 2) as r:
                            for j in range(2):
                                scan(2 * r + j, j, False)
                        g = b * (DIRS * BLOCKS) + d * BLOCKS + k
                        dve.wait_ge(y_ready, g + 1)
                        dve.wait_ge(gate_ready, g + 1)
                        v.tensor_tensor(gate[:, d, k, :], gate[:, d, k, :], ps01[:, :], ALU.mult).then_inc(gated, 1)

                dve.wait_ge(mamba_out, b + 1)
                dve.wait_ge(tu_ready, TILES * (b + 1))
                t2f, tuf = (a[:, :, :].rearrange("p a c -> p (a c)") for a in (t2, tu))
                link(v.tensor_tensor(t2f, tuf, ps67[:, :], ALU.add))
                dve.sem_inc(t2_ready, 1)
                for i in range(TILES):
                    link(v.bn_stats(ln_stats[:, :], t2[:, i, :]))
                    link(v.bn_aggr(ln_mv[:, i, :], ln_stats[:, :]))
                v.tensor_scalar(ln_var[:, :], var, LN_EPS, None, ALU.add).then_inc(var3_ready, 1)
                dve.wait_ge(rstd3_ready, b + 1)
                dve.wait_ge(xh_ready, TILES * (b + 1))
                link(v.tensor_copy(xh_scale[:, :], ln_rstd[:, :]))
                v.scalar_tensor_tensor(xh_bias[:, :], mean, -1.0, ln_rstd[:, :], ALU.mult,
                                       ALU.mult).then_inc(ln3_coef, 1)
                dve.wait_ge(logits_ready, b + 1)
                link(v.tensor_copy(logits[:, :, 0:EXPERTS],
                                   ps45[:, 0:TILES * EXPERTS].rearrange("p (a e) -> p a e", e=EXPERTS)))
                for i in range(TILES):
                    last = v.max(r8[:, i, :], logits[:, i, :])
                link(last)
                v.tensor_tensor(rexp[:, :, :], logits[:, :, 0:EXPERTS],
                                r8[:, :, 0:1].to_broadcast([P, TILES, EXPERTS]), ALU.subtract).then_inc(rdiff_ready, 1)
                dve.wait_ge(rdiff_ready, b + 1)
                link(v.memset(r8[:, :, 2:8], REPLACED))
                for i in range(TILES):
                    last = v.match_replace(marked[:, i, :], r8[:, i, :], logits[:, i, :], CHOSEN)
                link(last)
                dve.wait_ge(rexp_ready, b + 1)
                link(v.scalar_tensor_tensor(comb[:, :, :], marked[:, :, 0:EXPERTS], CHOSEN, rexp[:, :, :],
                                            ALU.is_equal, ALU.mult))
                link(v.reduce_sum(rsum[:, :], comb[:, :, :], axis=mybir.AxisListType.X))
                link(v.reciprocal(rsum[:, :], rsum[:, :]))
                link(v.tensor_tensor(comb[:, :, :], comb[:, :, :],
                                     rsum[:, :].unsqueeze(2).to_broadcast([P, TILES, EXPERTS]), ALU.mult))
                part = [comb_parts[:, :, i * BC:i * BC + EXPERTS] for i in range(PARTS)]
                link(v.tensor_copy(part[0], comb[:, :, :]))
                link(v.tensor_tensor(comb_rest[:, :, :], comb[:, :, :], part[0], ALU.subtract))
                link(v.tensor_copy(part[1], comb_rest[:, :, :]))
                v.tensor_tensor(part[2], comb_rest[:, :, :], part[1], ALU.subtract).then_inc(comb_ready, 1)
                for x in range(EXPERTS):
                    n = b * EXPERTS + x
                    dve.wait_ge(weight_ready, n + 1)
                    dve.wait_ge(gelu_ready, n + 1)
                    dve.wait_ge(expert_added, n - 1 if x else b * EXPERTS)
                    v.tensor_tensor(sel_e[:, x % 2, :], act_e[:, x % 2, :], ps45[:, :], ALU.mult).then_inc(sel_ready, 1)
                assert state["n"] == V_STEPS, state["n"] - V_STEPS

            dve_image(0)
            with dve.Fori(1, BATCH) as b:
                dve_image(b)

        @block.tensor
        def _(pe):
            mm, tr = nc.tensor.matmul, nc.tensor.transpose
            pe.wait_ge(w_loaded, 16 * (N_LOADS + 2))
            pe.wait_ge(const_done, CONSTS)
            pe.wait_ge(setup_taps, DIRS * BLOCKS * TAPS)
            for n, (src, dst, _) in enumerate(jobs):
                if n >= 4:
                    pe.wait_ge(setup_evac, n - 3)
                k = src.shape[0]
                tr(ps[n % 4][:, 0:k], src, ident[0:k, 0:k]).then_inc(setup_t, 1)
            pe.wait_ge(setup_evac, QK_JOB - 3)
            mm(ps[QK_JOB % 4][:, 0:P], raw_qkv[:, 0, :], raw_qkv[:, 1, :], start=True, stop=True).then_inc(setup_t, 1)
            pe.wait_ge(setup_evac, QK_JOB + 1)
            pe.wait_ge(setup_taps, DIRS * BLOCKS * (TAPS + 1) + 1)
            pe.wait_ge(setup_act, 2)

            def pe_image(b):
                pe.wait_ge(x_loaded, 16 * (b + 1))
                for i in range(TILES):
                    last = tr(ps67[:, i * P:(i + 1) * P], x_c[:, i * P:(i + 1) * P], ident[:, :])
                last.then_inc(xtok_t, 1)
                pe.wait_ge(gn_dev_ready, b + 1)
                mm(ps45[:, 0:1], group_avg[:, :], gn_mv[:, 0:1], start=True, stop=True).then_inc(gn_mean_ready, 1)
                pe.wait_ge(gn_sq_ready, 2 * b + 1)
                mm(ps45[:, 0:1], group_avg[:, :], gn_sq[:, :], start=True, stop=True).then_inc(gn_mean_ready, 1)
                pe.wait_ge(xn_ready, 2 * b + 2)
                pe.wait_ge(out_copied, b)
                for h in range(HALVES):
                    last = mm(halves(ps01)[h], qk_w[:, :], halves(xn_c)[h], start=True, stop=True)
                last.then_inc(qv_ready, 1)
                pe.wait_ge(xtok_copied, b + 1)
                for i in range(TILES):
                    last = mm(ps67[:, i * P:(i + 1) * P], xn_c[:, i * P:(i + 1) * P], wv_t[:, :],
                              start=True, stop=True)
                last.then_inc(qv_ready, 1)
                pe.wait_ge(qv_copied, 2 * b + 1)

                def scores(i):
                    n = b * TILES + i
                    if i >= 2:
                        pe.wait_ge(scores_copied, n - 1)
                    for h in range(HALVES):
                        last = mm(halves(ps[(i + 1) % 2])[h], q_c[:, i * P:(i + 1) * P], halves(xk_c)[h],
                                  start=True, stop=True)
                    last.then_inc(scores_ready, 1)

                for i in range(TILES):
                    scores(i)
                pe.wait_ge(missed_ready, b + 1)
                mm(ps01[0:1, 0:TILES], ones[:, :], missed[:, :], start=True, stop=True).then_inc(missed_summed, 1)
                pe.wait_ge(qv_copied, 2 * b + 2)
                for i in range(TILES):
                    n = b * TILES + i
                    pe.wait_ge(prob_ready, n + 1)
                    pe.wait_ge(probt_copied, b * TILES + max(i - 1, 0))
                    for j in range(TILES):
                        last = tr(ps[1 + i % 2][:, j * P:(j + 1) * P], expo[:, i % 2, j * P:(j + 1) * P], ident[:, :])
                    last.then_inc(prob_transposed, 1)
                    pe.wait_ge(probt_copied, n + 1)
                    pe.wait_ge(t1_ready, b * TILES + max(i - 1, 0))
                    at = i % 2 * BANK
                    for j in range(TILES):
                        last = mm(ps67[:, at:at + P], prob_t[:, j, :], v_tok[:, j, :], start=j == 0, stop=j == TILES - 1)
                    last.then_inc(attn_ready, 1)
                pe.wait_ge(xh_ready, TILES * (b + 1))
                pe.wait_ge(scores_copied, TILES * (b + 1))
                for i in range(TILES):
                    last = tr(ps01[:, i * P:(i + 1) * P], xh[:, i, :], ident[:, :])
                last.then_inc(xh_t, 1)

                pe.wait_ge(mx_ready, b + 1)
                for d in range(DIRS):
                    fills = (b * DIRS + d) * (3 * BLOCKS + 1)
                    pe.wait_ge(dbu_ready, b * UNITS + d * BLOCKS * D_STATE)
                    pe.wait_ge(c_copied, b * UNITS + d * BLOCKS * D_STATE)
                    pe.wait_ge(t1_ready, TILES * (b + 1))
                    for k in range(BLOCKS):
                        dst = ps[1 + 2 * (k % 2)]
                        for h in range(HALVES):
                            for j in range(TAPS):
                                at = h * BANK + (j if d == 0 else 2 * PAD - j)
                                last = mm(halves(dst)[h], conv_in_t[:, d, k, j, :], mx[:, at:at + BANK],
                                          start=j == 0, stop=j == TAPS - 1)
                        last.then_inc(pre_filled, 1)
                    for k in range(BLOCKS):
                        pe.wait_ge(pre_read, fills + k + 1)
                        dst = ps[1 + 2 * (k % 2)]
                        for h in range(HALVES):
                            at = h * BANK + PAD
                            last = mm(halves(dst)[h], z_in_t[:, d, k, :], mx[:, at:at + BANK], start=True, stop=True)
                        last.then_inc(pre_filled, 1)
                    pe.wait_ge(pre_read, fills + BLOCKS + 1)
                    pe.wait_ge(xs_ready, (b * DIRS + d + 1) * BLOCKS)
                    for h in range(HALVES):
                        for k in range(BLOCKS):
                            last = mm(halves(ps23)[h], xproj_t[:, d, k, :], xs[:, k, h * BANK:(h + 1) * BANK],
                                      start=k == 0, stop=k == BLOCKS - 1)
                    last.then_inc(pre_filled, 1)
                    pe.wait_ge(hi_ready, 2 * (b * DIRS + d) + 2)
                    rows = slice(PARTS * BC, PARTS * BC + DT_RANK)
                    for k in range(BLOCKS):
                        pe.wait_ge(pre_read, fills + BLOCKS + 2 + k)
                        dst = ps[3 - 2 * (k % 2)]
                        for h in range(HALVES):
                            last = mm(halves(dst)[h], dtproj_t[rows, d, k, :], dbc[rows, h * BANK:(h + 1) * BANK],
                                      start=True, stop=True)
                        last.then_inc(pre_filled, 1)
                    pe.wait_ge(pre_read, fills + 3 * BLOCKS + 1)
                    pe.wait_ge(parts_ready, b * DIRS + d + 1)
                    pe.wait_ge(mid_ready, 2 * (b * DIRS + d) + 2)
                    for k in range(BLOCKS):
                        g = b * (DIRS * BLOCKS) + d * BLOCKS + k
                        base = b * UNITS + (d * BLOCKS + k) * D_STATE
                        pe.wait_ge(gated, g)
                        for h in range(HALVES):
                            mm(halves(ps01)[h], skip_diag[:, d, k, :], xs[:, k, h * BANK:(h + 1) * BANK],
                               start=True, stop=False)

                        def spread(s):
                            pe.wait_ge(dbu_ready, base + s)
                            for h in range(HALVES):
                                last = mm(halves(ps23)[h], pick[:, ds(s, 1), :].rearrange("p o m -> p (o m)"),
                                          bc_parts[:, h * BANK:(h + 1) * BANK], start=True, stop=True)
                            last.then_inc(b_ready, 1)
                            pe.wait_ge(c_copied, base + s)
                            for h in range(HALVES):
                                last = mm(halves(ps67)[h], pick[:, ds(s + D_STATE, 1), :].rearrange("p o m -> p (o m)"),
                                          bc_parts[:, h * BANK:(h + 1) * BANK], start=True, stop=True)
                            last.then_inc(c_ready, 1)

                        def add(s, j, stop=False):
                            pe.wait_ge(hc_ready, base + s + 1)
                            for h in range(HALVES):
                                last = mm(halves(ps01)[h], ident[:, :], hc[:, j, h * BANK:(h + 1) * BANK],
                                          start=False, stop=stop)
                            return last.then_inc(y_added, 1)

                        spread(0)
                        spread(1)
                        with pe.Fori(1, D_STATE // 2) as r:
                            for j in range(2):
                                spread(2 * r + j)
                                add(2 * r + j - 2, j)
                        add(D_STATE - 2, 0)
                        add(D_STATE - 1, 1, stop=True)
                        pe.wait_ge(y_added, base + D_STATE)
                        pe.sem_inc(y_ready, 1)
                pe.wait_ge(gated, DIRS * BLOCKS * (b + 1))
                pe.wait_ge(c_copied, UNITS * (b + 1))
                for i in range(TILES):
                    for d in range(DIRS):
                        for k in range(BLOCKS):
                            last = mm(ps67[:, i * P:(i + 1) * P], gate[:, d, k, i * P:(i + 1) * P],
                                      outproj_t[:, d, k, :], start=d + k == 0, stop=d + k == DIRS + BLOCKS - 2)
                last.then_inc(mamba_out, 1)

                pe.wait_ge(en_ready, TILES * (b + 1))
                pe.wait_ge(t2_ready, b + 1)
                for i in range(TILES):
                    last = tr(ps67[:, i * P:(i + 1) * P], en[:, i, :], ident[:, :])
                last.then_inc(en_t, 1)
                pe.wait_ge(ec_ready, b + 1)
                for i in range(TILES):
                    last = mm(ps45[:, i * EXPERTS:(i + 1) * EXPERTS], e_c[:, i * P:(i + 1) * P], router_t[:, :],
                              start=True, stop=True)
                last.then_inc(logits_ready, 1)
                pe.wait_ge(comb_ready, b + 1)
                for i in range(TILES):
                    last = tr(ps45[0:EXPERTS, i * P:(i + 1) * P], comb[:, i, :], ident[:, :])
                last.then_inc(comb_transposed, 1)
                parts_ps = ps67[0:PARTS * BC, :].bitcast(BF16)
                for i in range(TILES):
                    last = tr(parts_ps[:, i * P:(i + 1) * P], comb_parts[:, i, :], ident_bf[:, :])
                last.then_inc(comb_transposed, 1)
                pe.wait_ge(comb_copied, 2 * b + 2)
                for h in range(HALVES):
                    mm(halves(ps01)[h], b2[:, :], comb_t[:, h * BANK:(h + 1) * BANK], start=True, stop=False)
                pe.wait_ge(t2e_ready, TILES * (b + 1))
                for i in range(TILES):
                    mm(ps01[:, i * P:(i + 1) * P], t2e[:, i, :], ident[:, :], start=False, stop=False)

                def hidden(x):
                    n = b * EXPERTS + x
                    if x >= 2:
                        pe.wait_ge(gelu_ready, n - 1)
                    for h in range(HALVES):
                        last = mm(halves(ps[1 + 2 * (x % 2)])[h], w1[:, x, :], halves(e_c)[h], start=True, stop=True)
                    last.then_inc(hidden_ready, 1)

                def weights(x):
                    pe.wait_ge(sel_ready, b * EXPERTS + x)
                    for h in range(HALVES):
                        last = mm(halves(ps45)[h], pick[:, x, :], comb_parts_t[:, h * BANK:(h + 1) * BANK],
                                  start=True, stop=True)
                    last.then_inc(weight_ready, 1)

                hidden(0)
                for x in range(EXPERTS):
                    if x + 1 < EXPERTS:
                        hidden(x + 1)
                    weights(x)
                    pe.wait_ge(sel_ready, b * EXPERTS + x + 1)
                    for h in range(HALVES):
                        last = mm(halves(ps01)[h], w2[:, x, :], sel_e[:, x % 2, h * BANK:(h + 1) * BANK],
                                  start=False, stop=x == EXPERTS - 1)
                    last.then_inc(expert_added, 1)

            pe_image(0)
            with pe.Fori(1, BATCH) as b:
                pe_image(b)


_WAY = ["in_proj_w", "conv_w", "conv_b", "x_proj_w", "dt_proj_w", "dt_proj_b", "A_log", "D", "out_proj_w"]
_INS = (["x", "L0_conv_Wq", "L0_conv_Wk", "L0_conv_Wv", "L1_attn_ln_gamma", "L1_attn_ln_beta"]
        + [f"L1_attn_{way}_{name}" for way in "fb" for name in _WAY]
        + ["L1_ffn_" + name for name in ("router_w", "w1", "b1", "w2", "b2")])


def kernel(**inputs):
    import numpy as _np
    import concourse.bacc as _bacc
    from concourse import mybir as _mybir
    from concourse.bass_utils import run_bass_kernel_spmd as _run

    nc = _bacc.Bacc("TRN2", target_bir_lowering=False, num_devices=1)
    arrays, args = {}, {}
    for name in _INS:
        a = _np.ascontiguousarray(inputs[name])
        arrays[f"in_{name}"] = a
        args[name] = nc.dram_tensor(f"in_{name}", a.shape, _mybir.dt.from_np(a.dtype), kind="ExternalInput").ap()
    out = nc.dram_tensor("out_0", inputs["x"].shape, _mybir.dt.from_np(_np.dtype("float32")),
                         kind="ExternalOutput").ap()
    hybrid_block(nc, args, out)
    r = _run(nc, [arrays], core_ids=[0])
    return r.results[0]["out_0"]
```

```python
import concourse.bass as bass
from concourse import mybir
from contextlib import ExitStack
import math


def normal_tail(share):
    low, high = -9.0, 9.0
    for _ in range(60):
        mid = (low + high) / 2
        low, high = (mid, high) if 0.5 * math.erfc(mid / math.sqrt(2.0)) > share else (low, mid)
    return low


def hybrid_block(nc, t_in, out):
    F32, BF16 = mybir.dt.float32, mybir.dt.bfloat16
    ALU, ACT = mybir.AluOpType, mybir.ActivationFunctionType
    ds = bass.ds

    BATCH, C, H, W = t_in["x"].shape
    N = H * W
    P = 128
    TILES = N // P
    BANK = 512
    HALVES = N // BANK
    KEEP = max(1, int(0.1 * N))
    FULL_ROUNDS, LAST_ROUND = divmod(KEEP, 8)
    GROUP = C // 32
    D_INNER, D_STATE, DT_RANK, TAPS = 256, 16, 16, 4
    BLOCKS = D_INNER // P
    DIRS = 2
    EXPERTS = t_in["L1_ffn_router_w"].shape[0]
    UNITS = DIRS * BLOCKS * D_STATE
    BC = 2 * D_STATE
    PARTS = 3
    WINDOW = 16
    TARGET = KEEP - (WINDOW - 1) / 2
    Z0 = normal_tail(TARGET / N)
    DENSITY = math.exp(-Z0 * Z0 / 2) / math.sqrt(2 * math.pi)
    STEP = 1 / (N * DENSITY)
    DAMPING = (1.0, 0.6, 0.6)
    COUNTS = len(DAMPING) + 1
    ACT_TILES = 4
    REPLACED = -3.0e38
    CHOSEN = 3.0e38
    LN_EPS = 1e-5

    x_v = t_in["x"].rearrange("b c h w -> b c (h w)")
    out_v = out.rearrange("b c h w -> b c (h w)")

    ctx = ExitStack()
    with ctx:
        def sb(name, shape, dt=F32):
            return ctx.enter_context(nc.sbuf_tensor(name, shape, dt))

        def sem(name):
            return ctx.enter_context(nc.semaphore(name))

        ident = sb("ident", [P, P])
        ident_bf = sb("ident_bf", [P, P], BF16)
        group_avg = sb("group_avg", [P, P])
        pick = sb("pick", [PARTS * BC, BC, P], BF16)
        neg_half = sb("neg_half", [P, TILES])
        qk_w = sb("qk_w", [P, P])
        wv_t = sb("wv_t", [P, P])
        x_in_t = sb("x_in_t", [P, DIRS, BLOCKS, P])
        z_in_t = sb("z_in_t", [P, DIRS, BLOCKS, P])
        xproj_t = sb("xproj_t", [P, DIRS, BLOCKS, P])
        dtproj_t = sb("dtproj_t", [P, DIRS, BLOCKS, P])
        outproj_t = sb("outproj_t", [P, DIRS, BLOCKS, P])
        skip_diag = sb("skip_diag", [P, DIRS, BLOCKS, P])
        w1 = sb("w1", [P, EXPERTS, P])
        w2 = sb("w2", [P, EXPERTS, P])
        router_t = sb("router_t", [P, EXPERTS])
        b1_t = sb("b1_t", [P, EXPERTS])
        b2 = sb("b2", [EXPERTS, P])
        conv_w = sb("conv_w", [P, DIRS, BLOCKS, TAPS])
        VECS = 3 * DIRS * BLOCKS + 2
        vec = sb("vec", [P, VECS])
        conv_b, dt_b, skip = (vec[:, i * DIRS * BLOCKS:(i + 1) * DIRS * BLOCKS].rearrange("p (d k) -> p d k", d=DIRS)
                              for i in range(3))
        gamma, beta = vec[:, VECS - 2:VECS - 1], vec[:, VECS - 1:VECS]
        decay = sb("decay", [P, DIRS, BLOCKS, D_STATE])
        raw_qkv = sb("raw_qkv", [P, 3, P])
        raw_vec = sb("raw_vec", [VECS, P])
        raw_small = sb("raw_small", [EXPERTS, 2, P])

        x_c = sb("x_c", [P, N])
        xn_c = sb("xn_c", [P, N])
        q_c = sb("q_c", [P, N])
        v_tok = sb("v_tok", [P, TILES, P])
        x_tok = sb("x_tok", [P, TILES, P])
        xk_c = sb("xk_c", [P, N])
        ring = sb("ring", [P, TILES, N])
        score = ring
        expo = sb("expo", [P, 2, N])
        work = sb("work", [P, 2, N])
        prob_t = sb("prob_t", [P, 2, TILES, P])
        dbu = [sb("dbu0", [P, N]), sb("dbu1", [P, N])]
        unused_a, unused_v = (tile[:, :].bitcast(BF16).rearrange("p (a n) -> p a n", a=2) for tile in dbu)
        top8 = sb("top8", [P, 8])
        row_max = sb("row_max", [P, TILES])
        neg_max = sb("neg_max", [P, TILES])
        sum_sq = sb("sum_sq", [P, TILES])
        score_var = sb("score_var", [P, TILES])
        score_std = sb("score_std", [P, TILES])
        correction = sb("correction", [P, TILES])
        thresh = sb("thresh", [P, TILES])
        neg_thresh = sb("neg_thresh", [P, TILES])
        count = sb("count", [P, TILES])
        delta = sb("delta", [P, TILES])
        rank = sb("rank", [P, TILES])
        ladder = sb("ladder", [P, TILES, WINDOW + 1])
        rungs = sb("rungs", [P, TILES, WINDOW])
        hit = sb("hit", [P, TILES, WINDOW])
        at_rank = sb("at_rank", [P, TILES, WINDOW])
        after_rank = sb("after_rank", [P, TILES, WINDOW])
        kept_from = sb("kept_from", [P, TILES])
        next_below = sb("next_below", [P, TILES])
        found = sb("found", [P, TILES])
        missed = sb("missed", [P, TILES])
        ones = sb("ones", [P, 1])
        half_pow = sb("half_pow", [P, TILES])
        gn_kbias = sb("gn_kbias", [P, 1])
        missed_tiles = sb("missed_tiles", [1, TILES + 1])
        missed_bits = missed_tiles[:, :].bitcast(mybir.dt.int32)
        row_sum = sb("row_sum", [P, TILES])
        row_inv = sb("row_inv", [P, TILES])
        gn_stats = sb("gn_stats", [P, 2, 6])
        gn_mv = sb("gn_mv", [P, 2])
        gn_dev = sb("gn_dev", [P, 1])
        gn_sq = sb("gn_sq", [P, 1])
        gn_mean = sb("gn_mean", [P, 1])
        gn_var = sb("gn_var", [P, 1])
        gn_scale = sb("gn_scale", [P, 1])
        gn_bias = sb("gn_bias", [P, 1])
        t1 = sb("t1", [P, TILES, P])
        ln_stats = sb("ln_stats", [P, 6])
        ln_mv = sb("ln_mv", [P, TILES, 2])
        ln_var = sb("ln_var", [P, TILES])
        ln_rstd = sb("ln_rstd", [P, TILES])
        ln_var2 = sb("ln_var2", [P, TILES])
        ln_rstd2 = sb("ln_rstd2", [P, TILES])
        xh_scale = sb("xh_scale", [P, TILES])
        xh_bias = sb("xh_bias", [P, TILES])
        tu_scale = sb("tu_scale", [P, TILES])
        tu_bias = sb("tu_bias", [P, TILES])
        xh = sb("xh", [P, TILES, P])
        tu = sb("tu", [P, TILES, P])

        mx = sb("mx", [P, N])
        conv_half = work
        xs = sb("xs", [P, BLOCKS, N])
        z_tmp = [expo, prob_t[:, :, :, :].rearrange("p r a c -> p r (a c)")]
        gate = sb("gate", [P, DIRS, BLOCKS, N])
        dbc = sb("dbc", [P, N])
        bc_parts = sb("bc_parts", [PARTS * BC, N], BF16)
        bc_rest = sb("bc_rest", [PARTS * BC, N])
        bc_mid = sb("bc_mid", [PARTS * BC, N], BF16)
        dt = sb("dt", [P, BLOCKS, N])
        dtx = sb("dtx", [P, BLOCKS, N])
        dA, c_all, hs_odd, hc_odd = (ring[:, 2 * i:2 * i + 2, :] for i in range(4))
        hs, hc = [expo, hs_odd], [work, hc_odd]
        soft_log = work
        raw_in = hs_odd[:, 0, :].rearrange("p (d k c) -> p d k c", d=DIRS, k=2 * BLOCKS)
        raw_xproj = hs_odd[:, 1, 0:BANK].rearrange("p (d c) -> p d c", d=DIRS)
        raw_out = hs_odd[:, 1, BANK:N].rearrange("p (d c) -> p d c", d=DIRS)
        raw_dtproj = c_all[:, 0, 0:BANK].rearrange("p (d k c) -> p d k c", d=DIRS, k=BLOCKS)

        t2 = dtx[:, 0, :].rearrange("p (a c) -> p a c", c=P)
        en = dtx[:, 1, :].rearrange("p (a c) -> p a c", c=P)
        t2e = t2
        e_c = xs[:, 0, :]
        out_c = xs[:, 1, :]
        logits = sb("logits", [P, TILES, 2 * EXPERTS])
        marked = sb("marked", [P, TILES, 2 * EXPERTS])
        r8 = sb("r8", [P, TILES, 8])
        rexp = sb("rexp", [P, TILES, EXPERTS])
        rsum = sb("rsum", [P, TILES])
        comb = sb("comb", [P, TILES, EXPERTS])
        comb_parts = sb("comb_parts", [P, TILES, PARTS * BC], BF16)
        comb_rest = sb("comb_rest", [P, TILES, EXPERTS])
        comb_t = dbc[0:EXPERTS, :]
        comb_parts_t = bc_parts
        act_e = dt
        sel_e = gate[:, 0, :, :]

        ps = [ctx.enter_context(nc.psum_tensor(f"ps{i}", [P, N], F32)) for i in range(4)]
        ps01, ps23, ps45, ps67 = ps

        w_loaded = sem("w_loaded")
        const_step = sem("const_step")
        waits_passed = sem("waits_passed")
        const_done = sem("const_done")
        setup_cleared = sem("setup_cleared")
        setup_t = sem("setup_t")
        setup_evac = sem("setup_evac")
        setup_scaled = sem("setup_scaled")
        setup_act = sem("setup_act")
        vstep = sem("vstep")
        tstep = sem("tstep")
        astep = sem("astep")
        gate_step = sem("gate_step")
        x_loaded = sem("x_loaded")
        gn_dev_ready = sem("gn_dev_ready")
        gn_mean_ready = sem("gn_mean_ready")
        gn_vec_ready = sem("gn_vec_ready")
        gn_sq_ready = sem("gn_sq_ready")
        gn_pow = sem("gn_pow")
        gn_coef = sem("gn_coef")
        xtok_t = sem("xtok_t")
        xtok_copied = sem("xtok_copied")
        xn_ready = sem("xn_ready")
        qv_ready = sem("qv_ready")
        qv_copied = sem("qv_copied")
        scores_ready = sem("scores_ready")
        scores_copied = sem("scores_copied")
        squares_ready = sem("squares_ready")
        score_var_ready = sem("score_var_ready")
        score_std_ready = sem("score_std_ready")
        thresh_ready = sem("thresh_ready")
        counted = sem("counted")
        missed_ready = sem("missed_ready")
        missed_summed = sem("missed_summed")
        missed_read = sem("missed_read")
        exact_step = sem("exact_step")
        neg_max_ready = sem("neg_max_ready")
        exp_ready = sem("exp_ready")
        prob_ready = sem("prob_ready")
        prob_transposed = sem("prob_transposed")
        probt_copied = sem("probt_copied")
        attn_ready = sem("attn_ready")
        t1_ready = sem("t1_ready")
        var_ready = sem("var_ready")
        rstd_ready = sem("rstd_ready")
        var2_ready = sem("var2_ready")
        rstd2_ready = sem("rstd2_ready")
        ln_coef = sem("ln_coef")
        xh_ready = sem("xh_ready")
        xh_t = sem("xh_t")
        tu_ready = sem("tu_ready")
        mx_ready = sem("mx_ready")
        conv_filled = sem("conv_filled")
        z_filled = sem("z_filled")
        dbc_filled = sem("dbc_filled")
        dt_filled = sem("dt_filled")
        tap_ready = sem("tap_ready")
        conv_step = sem("conv_step")
        conv_summed = sem("conv_summed")
        tanh_ready = sem("tanh_ready")
        xs_ready = sem("xs_ready")
        z_acts = sem("z_acts")
        gate_ready = sem("gate_ready")
        hi_ready = sem("hi_ready")
        rest_ready = sem("rest_ready")
        mid_ready = sem("mid_ready")
        mid_step = sem("mid_step")
        parts_ready = sem("parts_ready")
        abs_ready = sem("abs_ready")
        relu_ready = sem("relu_ready")
        log_ready = sem("log_ready")
        dt_ready = sem("dt_ready")
        dtx_ready = sem("dtx_ready")
        b_ready = sem("b_ready")
        dbu_ready = sem("dbu_ready")
        c_ready = sem("c_ready")
        c_copied = sem("c_copied")
        dA_ready = sem("dA_ready")
        scan_ready = sem("scan_ready")
        hc_ready = sem("hc_ready")
        y_added = sem("y_added")
        y_ready = sem("y_ready")
        gated = sem("gated")
        mamba_out = sem("mamba_out")
        t2_ready = sem("t2_ready")
        var3_ready = sem("var3_ready")
        rstd3_ready = sem("rstd3_ready")
        ln3_coef = sem("ln3_coef")
        en_ready = sem("en_ready")
        en_t = sem("en_t")
        ec_ready = sem("ec_ready")
        t2e_ready = sem("t2e_ready")
        logits_ready = sem("logits_ready")
        rdiff_ready = sem("rdiff_ready")
        rexp_ready = sem("rexp_ready")
        comb_ready = sem("comb_ready")
        comb_transposed = sem("comb_transposed")
        comb_copied = sem("comb_copied")
        hidden_ready = sem("hidden_ready")
        gelu_ready = sem("gelu_ready")
        weight_ready = sem("weight_ready")
        sel_ready = sem("sel_ready")
        expert_added = sem("expert_added")
        out_copied = sem("out_copied")
        out_stored = sem("out_stored")

        block = ctx.enter_context(nc.Block())

        dt_ps = (ps67, ps01)

        def halves(tile):
            return [tile[:, h * BANK:(h + 1) * BANK] for h in range(HALVES)]

        WAYS = ["f", "b"]
        jobs = [(raw_qkv[:, 2, :], wv_t[:, :], 1.0)]
        for d in range(DIRS):
            for k in range(BLOCKS):
                jobs.append((raw_in[:, d, k, :], x_in_t[:, d, k, :], 1.0))
                jobs.append((raw_in[:, d, BLOCKS + k, :], z_in_t[:, d, k, :], 1.0))
                jobs.append((raw_xproj[:, d, k * P:(k + 1) * P], xproj_t[:, d, k, :], 1.0))
                jobs.append((raw_dtproj[:, d, k, :], dtproj_t[:, d, k, :], 1.0))
                jobs.append((raw_out[:, d, k * P:(k + 1) * P], outproj_t[:, d, k, :], 0.5))
        jobs.append((raw_vec[:, :], vec[:, :], 1.0))
        jobs.append((raw_small[:, 0, :], router_t[:, :], 1.0))
        jobs.append((raw_small[:, 1, :], b1_t[:, :], 1.0))
        QK_JOB = len(jobs)
        N_LOADS = 32

        CONSTS = 9 + WINDOW

        def passed(eng):
            eng.sem_inc(waits_passed, 1)

        def step_counter(eng, signal, per_round):
            rnd, steps = [0], [0]

            def begin(r):
                rnd[0], steps[0] = r, 0

            def end():
                assert steps[0] == per_round, steps[0] - per_round

            def step(ins):
                steps[0] += 1
                ins.then_inc(signal, 1)

            def after(back=1):
                eng.wait_ge(signal, rnd[0] * per_round + steps[0] - back)
                passed(eng)

            def link(ins):
                step(ins)
                after(0)

            return begin, end, step, after, link

        @block.sync
        def _(sp):
            loads = 0

            def load(dst, src):
                sp.dma_start(dst, src).then_inc(w_loaded, 16)

            for i, name in enumerate(("Wq", "Wk", "Wv")):
                load(raw_qkv[:, i, :], t_in["L0_conv_" + name][:, :])
            sp.wait_ge(setup_cleared, 2)
            loads = 3
            for d, way in enumerate(WAYS):
                g = lambda s: t_in[f"L1_attn_{way}_{s}"]
                xp = g("x_proj_w")
                for part in range(PARTS):
                    load(raw_xproj[part * BC:(part + 1) * BC, d, :], xp[DT_RANK:DT_RANK + BC, :])
                load(raw_xproj[PARTS * BC:PARTS * BC + DT_RANK, d, :], xp[0:DT_RANK, :])
                load(raw_dtproj[:, d, :, PARTS * BC:PARTS * BC + DT_RANK],
                     g("dt_proj_w").rearrange("(k p) r -> p k r", p=P))
                load(raw_in[:, d, :, :], g("in_proj_w").rearrange("(k p) c -> p k c", p=P))
                load(raw_out[:, d, :], g("out_proj_w")[:, :])
                load(conv_w[:, d, :, :], g("conv_w").rearrange("(k p) o j -> p k (o j)", p=P))
                for i, name in enumerate(("conv_b", "dt_proj_b", "D")):
                    row = (i * DIRS + d) * BLOCKS
                    load(raw_vec[row:row + BLOCKS, :], g(name).rearrange("(k p) -> k p", p=P))
                load(decay[:, d, :, :], g("A_log").rearrange("(k p) s -> p k s", p=P))
                loads += 12
            load(w1[:, :, :], t_in["L1_ffn_w1"].rearrange("e d f -> d e f"))
            load(w2[:, :, :], t_in["L1_ffn_w2"].rearrange("e f d -> f e d"))
            load(raw_small[:, 0, :], t_in["L1_ffn_router_w"][:, :])
            load(raw_small[:, 1, :], t_in["L1_ffn_b1"][:, :])
            load(b2[:, :], t_in["L1_ffn_b2"][:, :])
            load(raw_vec[VECS - 2:VECS - 1, :], t_in["L1_attn_ln_gamma"].rearrange("(o p) -> o p", o=1))
            load(raw_vec[VECS - 1:VECS, :], t_in["L1_attn_ln_beta"].rearrange("(o p) -> o p", o=1))
            loads += 7
            assert loads == N_LOADS + 2, loads
            def load_image(b):
                sp.wait_ge(xn_ready, 2 * b)
                sp.dma_start(x_c[:, :], x_v[ds(b, 1), :, :].rearrange("o c n -> (o c) n")).then_inc(x_loaded, 16)

            def store_image(b):
                sp.wait_ge(out_copied, b + 1)
                passed(sp)
                sp.dma_start(out_v[ds(b, 1), :, :].rearrange("o c n -> (o c) n"), out_c).then_inc(out_stored, 16)
                sp.wait_ge(out_stored, 16 * (b + 1))
                passed(sp)

            load_image(0)
            with sp.Fori(1, BATCH) as b:
                load_image(b)
                store_image(b - 1)
            store_image(BATCH - 1)

        @block.gpsimd
        def _(pool):
            pool.memset(raw_xproj[:, :, :], 0.0).then_inc(setup_cleared, 1)
            pool.memset(raw_dtproj[:, :, :, :], 0.0).then_inc(setup_cleared, 1)
            pool.memset(neg_half[:, :], -0.5).then_inc(const_done, 1)
            pool.memset(half_pow[:, :], 0.5).then_inc(const_done, 1)
            pool.memset(ones[:, :], 1.0).then_inc(const_done, 1)
            for j in range(WINDOW):
                pool.memset(rungs[:, :, j], float(j)).then_inc(const_done, 1)
            pool.memset(logits[:, :, :], REPLACED).then_inc(const_done, 1)
            pool.memset(comb_parts[:, :, :], 0.0).then_inc(const_done, 1)
            pool.memset(ident[:, :], 0.0).then_inc(const_step, 1)
            pool.memset(ident_bf[:, :], 0.0).then_inc(const_step, 1)
            pool.memset(group_avg[:, :], 1.0 / GROUP).then_inc(const_step, 1)
            pool.memset(pick[:, :, :], 0.0).then_inc(const_step, 1)
            pool.wait_ge(const_step, 4)
            for m in (ident, ident_bf):
                pool.affine_select(out=m[:, :], in_=m[:, :], compare_op=ALU.not_equal, fill=1.0, base=0,
                                   pattern=[[-1, P]], channel_multiplier=1).then_inc(const_done, 1)
            gv = group_avg[:, :].rearrange("p (g c) -> p g c", c=GROUP)
            pool.affine_select(out=gv, in_=gv, compare_op=ALU.is_ge, fill=0.0, base=0,
                               pattern=[[-GROUP, P // GROUP], [0, GROUP]], channel_multiplier=1).then_inc(const_step, 1)
            pool.wait_ge(const_step, 5)
            pool.affine_select(out=gv, in_=gv, compare_op=ALU.is_ge, fill=0.0, base=GROUP - 1,
                               pattern=[[GROUP, P // GROUP], [0, GROUP]], channel_multiplier=-1).then_inc(const_done, 1)
            for part in range(PARTS):
                pool.wait_ge(const_step, 5 + part)
                pool.affine_select(out=pick[:, :, :], in_=pick[:, :, :], compare_op=ALU.not_equal, fill=1.0,
                                   base=-part * BC, pattern=[[-1, BC], [0, P]],
                                   channel_multiplier=1).then_inc(const_step, 1)
            pool.wait_ge(const_step, 5 + PARTS)
            pool.sem_inc(const_done, 1)

            def expert_norm(m):
                pool.wait_ge(var3_ready, m + 1)
                pool.tensor_tensor(ln_rstd[:, :], ln_var[:, :], neg_half[:, :], ALU.pow).then_inc(rstd3_ready, 1)
                for i in range(TILES):
                    pool.wait_ge(en_ready, TILES * m + i + 1)
                    pool.tensor_tensor(t2e[:, i, :], t2[:, i, :], en[:, i, :], ALU.add).then_inc(t2e_ready, 1)

            def group_norm(b):
                pool.wait_ge(gn_sq_ready, 2 * b + 2)
                pool.tensor_tensor(gn_scale[:, :], gn_var[:, :], neg_half[:, 0:1], ALU.pow).then_inc(gn_pow, 1)

            def layer_norm(b):
                pool.wait_ge(score_var_ready, b + 1)
                pool.tensor_tensor(score_std[:, :], score_var[:, :], half_pow[:, :], ALU.pow).then_inc(score_std_ready, 1)
                pool.wait_ge(var_ready, b + 1)
                pool.tensor_tensor(ln_rstd[:, :], ln_var[:, :], neg_half[:, :], ALU.pow).then_inc(rstd_ready, 1)
                pool.wait_ge(var2_ready, b + 1)
                pool.tensor_tensor(ln_rstd2[:, :], ln_var2[:, :], neg_half[:, :], ALU.pow).then_inc(rstd2_ready, 1)
                pool.wait_ge(ln_coef, b + 1)
                passed(pool)
                for i in range(TILES):
                    pool.tensor_scalar(tu[:, i, :], t1[:, i, :], tu_scale[:, i:i + 1], tu_bias[:, i:i + 1],
                                       ALU.mult, ALU.add).then_inc(tu_ready, 1)

            def direction(b, d):
                for k in range(BLOCKS):
                    g = (b * DIRS + d) * BLOCKS + k
                    pool.wait_ge(z_acts, 2 * g + 2)
                    pool.wait_ge(expert_added, b * EXPERTS)
                    passed(pool)
                    pool.tensor_scalar(z_tmp[k][:, 0, :], z_tmp[k][:, 0, :], 1.0, None, ALU.add).then_inc(gate_step, 1)
                    pool.wait_ge(gate_step, g + 1)
                    pool.tensor_tensor(gate[:, d, k, :], z_tmp[k][:, 0, :], z_tmp[k][:, 1, :],
                                       ALU.mult).then_inc(gate_ready, 1)
                base = b * UNITS + d * BLOCKS * D_STATE
                base_s = (b * DIRS + d) * D_STATE

                def weigh(s, odd, first=False):
                    for k in range(BLOCKS):
                        pool.wait_ge(scan_ready, base + 2 * s + k + 1)
                        pool.wait_ge(c_copied, base_s + s + 1)
                        pool.wait_ge(y_added, base if first else base + 2 * s + k - 3)
                        pool.tensor_tensor(hc[odd][:, k, :], hs[odd][:, k, :], c_all[:, odd, :],
                                           ALU.mult).then_inc(hc_ready, 1)

                weigh(0, 0, first=True)
                weigh(1, 1, first=True)
                with pool.Fori(1, D_STATE // 2) as r:
                    for odd in range(2):
                        weigh(2 * r + odd, odd)

            def pool_image(b, m=None):
                group_norm(b)
                if m is not None:
                    expert_norm(m)
                layer_norm(b)
                for d in range(DIRS):
                    direction(b, d)

            pool_image(0)
            with pool.Fori(1, BATCH) as b:
                pool_image(b, b - 1)
            expert_norm(BATCH - 1)

        @block.scalar
        def _(act):
            def copy(dst, src, **kw):
                return nc.scalar.activation(dst, src, ACT.Copy, **kw)

            act.wait_ge(w_loaded, 16 * (N_LOADS + 2))
            flat = decay[:, :, :, :].rearrange("p d k s -> p (d k s)")
            nc.scalar.activation(flat, flat, ACT.Exp).then_inc(setup_act, 1)
            act.wait_ge(setup_act, 1)
            nc.scalar.mul(flat, flat, -1.0).then_inc(setup_act, 1)
            act.wait_ge(setup_act, 2)
            act.wait_ge(setup_evac, QK_JOB + 1)
            act.wait_ge(setup_scaled, DIRS * BLOCKS + 2)
            act.wait_ge(const_done, CONSTS)

            def inputs(b):
                act.wait_ge(xtok_t, b + 1)
                copy(x_tok[:, :, :].rearrange("p a c -> p (a c)"), ps45[:, :]).then_inc(xtok_copied, 1)
                act.wait_ge(gn_coef, b + 1)
                nc.scalar.activation(xn_c[:, :], x_c[:, :], ACT.Identity, bias=gn_bias[:, 0:1],
                                     scale=gn_scale[:, 0:1]).then_inc(xn_ready, 1)
                nc.scalar.activation(xk_c[:, :], x_c[:, :], ACT.Identity, bias=gn_kbias[:, 0:1],
                                     scale=gn_scale[:, 0:1]).then_inc(xn_ready, 1)
                act.wait_ge(qv_ready, 2 * b + 1)
                copy(q_c[:, :], ps01[:, :]).then_inc(qv_copied, 1)
                act.wait_ge(qv_ready, 2 * b + 2)
                copy(v_tok[:, :, :].rearrange("p a c -> p (a c)"), ps45[:, :]).then_inc(qv_copied, 1)

            def squares(b, tiles):
                for i in tiles:
                    act.wait_ge(scores_copied, b * TILES + i + 1)
                    act.wait_ge(squares_ready, b * TILES + max(i - 1, 0))
                    nc.scalar.activation(unused_a[:, i % 2, :], score[:, i, :], ACT.Square,
                                         accum_out=sum_sq[:, i:i + 1]).then_inc(squares_ready, 1)

            def expert_norm(m):
                act.wait_ge(ln3_coef, m + 1)
                for i in range(TILES):
                    nc.scalar.activation(en[:, i, :], t2[:, i, :], ACT.Identity, bias=xh_bias[:, i:i + 1],
                                         scale=xh_scale[:, i:i + 1]).then_inc(en_ready, 1)

            def expert_input(m):
                act.wait_ge(en_t, m + 1)
                copy(e_c, ps67[:, :]).then_inc(ec_ready, 1)

            def router_exp(m):
                act.wait_ge(rdiff_ready, m + 1)
                nc.scalar.activation(rexp[:, :, :], rexp[:, :, :], ACT.Exp).then_inc(rexp_ready, 1)

            def router_copies(m):
                act.wait_ge(comb_transposed, 2 * m + 1)
                copy(comb_t, ps45[0:EXPERTS, :]).then_inc(comb_copied, 1)
                act.wait_ge(comb_transposed, 2 * m + 2)
                copy(comb_parts_t[:, :], ps67[0:PARTS * BC, :].bitcast(BF16)[:, 0:N]).then_inc(comb_copied, 1)

            def gelu(m, x):
                n = m * EXPERTS + x
                act.wait_ge(hidden_ready, n + 1)
                act.wait_ge(sel_ready, m * EXPERTS + max(x - 1, 0))
                nc.scalar.activation(act_e[:, x % 2, :], ps[1 + 2 * (x % 2)][:, :], ACT.Gelu,
                                     bias=b1_t[:, x:x + 1]).then_inc(gelu_ready, 1)

            def result(m):
                act.wait_ge(expert_added, (m + 1) * EXPERTS)
                act.wait_ge(out_stored, 16 * m)
                copy(out_c, ps01[:, :]).then_inc(out_copied, 1)

            def count_signs(b, c, half):
                if half == 0:
                    act.wait_ge(thresh_ready, b * COUNTS + c + 1)
                    if c == 0:
                        act.wait_ge(squares_ready, TILES * (b + 1))
                for i in range(half * ACT_TILES // 2, (half + 1) * ACT_TILES // 2):
                    act.wait_ge(counted, (b * COUNTS + c) * ACT_TILES + max(i - 1, 0))
                    nc.scalar.activation(unused_a[:, i % 2, :], score[:, i, :], ACT.Sign, bias=neg_thresh[:, i:i + 1],
                                         accum_out=count[:, i:i + 1]).then_inc(counted, 1)

            def exponent(b, i):
                act.wait_ge(prob_transposed, b * TILES + max(i - 1, 0))
                nc.scalar.activation(expo[:, i % 2, :], score[:, i, :], ACT.Exp,
                                     bias=neg_max[:, i:i + 1]).then_inc(exp_ready, 1)

            def attend(b):
                act.wait_ge(neg_max_ready, b + 1)
                exponent(b, 0)
                exponent(b, 1)
                for i in range(TILES):
                    act.wait_ge(prob_transposed, b * TILES + i + 1)
                    act.wait_ge(attn_ready, b * TILES + max(i - 1, 0))
                    copy(prob_t[:, i % 2, :, :].rearrange("p a c -> p (a c)"), ps[1 + i % 2][:, :]).then_inc(probt_copied, 1)
                    if i + 2 < TILES:
                        exponent(b, i + 2)
                act.wait_ge(ln_coef, b + 1)
                for i in range(TILES):
                    nc.scalar.activation(xh[:, i, :], t1[:, i, :], ACT.Identity, bias=xh_bias[:, i:i + 1],
                                         scale=xh_scale[:, i:i + 1]).then_inc(xh_ready, 1)
                act.wait_ge(xh_t, b + 1)
                nc.scalar.activation(mx[:, :], ps01[:, :], ACT.Identity, bias=beta[:, 0:1],
                                     scale=gamma[:, 0:1]).then_inc(mx_ready, 1)

            def conv_tap(b, d, k):
                act.wait_ge(conv_filled, (b * DIRS + d) * BLOCKS + k + 1)
                act.wait_ge(y_added, b * UNITS + (BLOCKS * D_STATE - 2 if d else 0))
                nc.scalar.activation(conv_half[:, k, :], ps[1 + 2 * k][:, :], ACT.Identity, bias=conv_b[:, d, k:k + 1],
                                     scale=conv_w[:, d, k, TAPS - 1:TAPS]).then_inc(tap_ready, 1)

            def conv_tanh(b, d, k):
                act.wait_ge(conv_summed, (b * DIRS + d) * BLOCKS + k + 1)
                act.wait_ge(out_stored, 16 * b)
                nc.scalar.activation(xs[:, k, :], conv_half[:, k, :], ACT.Tanh).then_inc(tanh_ready, 1)

            def z_parts(b, d, k):
                act.wait_ge(z_filled, (b * DIRS + d) * BLOCKS + k + 1)
                act.wait_ge(attn_ready, TILES * (b + 1))
                act.wait_ge(gate_ready, (b * DIRS + d) * BLOCKS)
                act.wait_ge(hc_ready, b * UNITS + d * BLOCKS * D_STATE)
                src = ps[2 * k]
                nc.scalar.activation(z_tmp[k][:, 0, :], src[:, :], ACT.Tanh, scale=0.5).then_inc(z_acts, 1)
                copy(z_tmp[k][:, 1, :], src[:, :]).then_inc(z_acts, 1)

            def direction(b, d):
                e = b * DIRS + d
                conv_tap(b, d, 0)
                conv_tap(b, d, 1)
                if d == 0:
                    z_parts(b, d, 0)
                    conv_tanh(b, d, 0)
                    z_parts(b, d, 1)
                    conv_tanh(b, d, 1)
                else:
                    conv_tanh(b, d, 0)
                    z_parts(b, d, 0)
                    conv_tanh(b, d, 1)
                    z_parts(b, d, 1)
                act.wait_ge(dbc_filled, e + 1)
                act.wait_ge(dt_filled, e * BLOCKS)
                copy(dbc[:, :], ps23[:, :]).then_inc(hi_ready, 1)
                copy(bc_parts[:, :], ps23[0:PARTS * BC, :]).then_inc(hi_ready, 1)
                for k in range(BLOCKS):
                    g = e * BLOCKS + k
                    act.wait_ge(dt_filled, g + 1)
                    act.wait_ge(xs_ready, (e + 1) * BLOCKS)
                    log = soft_log[:, k, :]
                    nc.scalar.activation(log, dt_ps[k][:, :], ACT.Abs, bias=dt_b[:, d, k:k + 1]).then_inc(abs_ready, 1)
                    if k == 0:
                        act.wait_ge(rest_ready, e + 1)
                        copy(bc_parts[BC:2 * BC, :], bc_rest[BC:2 * BC, :]).then_inc(mid_ready, 1)
                    act.wait_ge(abs_ready, g + 1)
                    nc.scalar.activation(log, log, ACT.Exp, scale=-1.0).then_inc(astep, 1)
                    act.wait_ge(astep, g + 1)
                    nc.scalar.activation(log, log, ACT.Ln, bias=1.0).then_inc(log_ready, 1)
                base = b * UNITS + d * BLOCKS * D_STATE
                base_s = e * D_STATE

                def decay_and_c(s, odd, first=False):
                    for k in range(BLOCKS):
                        if first:
                            act.wait_ge(dt_ready, e * BLOCKS + k + 1)
                        act.wait_ge(scan_ready, base if first else base + 2 * s + k - 1)
                        nc.scalar.activation(dA[:, k, :], dt[:, k, :], ACT.Exp,
                                             scale=decay[:, d, k, ds(s, 1)]).then_inc(dA_ready, 1)
                        if k == 0:
                            act.wait_ge(c_ready, base_s + s + 1)
                            act.wait_ge(hc_ready, base + 2 * s - (0 if first else 2))
                            copy(c_all[:, odd, :], ps67[:, :]).then_inc(c_copied, 1)

                decay_and_c(0, 0, first=True)
                decay_and_c(1, 1)
                with act.Fori(1, D_STATE // 2) as r:
                    for odd in range(2):
                        decay_and_c(2 * r + odd, odd)

            def act_image(b, m=None):
                inputs(b)
                if m is not None:
                    expert_norm(m)
                squares(b, range(0, 2))
                if m is not None:
                    expert_input(m)
                squares(b, range(2, TILES))
                if m is not None:
                    router_exp(m)
                for c in range(COUNTS):
                    count_signs(b, c, 0)
                    if m is not None:
                        if c == 0:
                            router_copies(m)
                            gelu(m, 0)
                        gelu(m, 2 * c + 1)
                    count_signs(b, c, 1)
                    if m is not None and c < COUNTS - 1:
                        gelu(m, 2 * c + 2)
                if m is not None:
                    result(m)
                attend(b)
                for d in range(DIRS):
                    direction(b, d)

            act_image(0)
            with act.Fori(1, BATCH) as b:
                act_image(b, b - 1)
            expert_norm(BATCH - 1)
            expert_input(BATCH - 1)
            router_exp(BATCH - 1)
            router_copies(BATCH - 1)
            for x in range(EXPERTS):
                gelu(BATCH - 1, x)
            result(BATCH - 1)

        @block.vector
        def _(dve):
            v = nc.vector
            dve.wait_ge(w_loaded, 16 * (N_LOADS + 2))
            dve.wait_ge(const_done, CONSTS)
            for n, (src, dst, factor) in enumerate(jobs):
                dve.wait_ge(setup_t, n + 1)
                v.tensor_scalar(dst, ps[n % 4][:, 0:dst.shape[1]], factor, None, ALU.mult).then_inc(setup_evac, 1)
            dve.wait_ge(setup_t, QK_JOB + 1)
            v.tensor_scalar(qk_w[:, :], ps[QK_JOB % 4][:, 0:P], float(C) ** -0.5, None, ALU.mult).then_inc(setup_evac, 1)
            dve.wait_ge(setup_evac, QK_JOB + 1)
            for d in range(DIRS):
                for k in range(BLOCKS):
                    v.tensor_scalar(skip_diag[:, d, k, :], ident[:, :], skip[:, d, k:k + 1], None,
                                    ALU.mult).then_inc(setup_scaled, 1)
            v.tensor_scalar(vec[:, 0:DIRS * BLOCKS], vec[:, 0:DIRS * BLOCKS], 0.5, None,
                            ALU.mult).then_inc(setup_scaled, 1)
            flat_w = conv_w[:, :, :, :].rearrange("p d k j -> p (d k j)")
            v.tensor_scalar(flat_w, flat_w, 0.5, None, ALU.mult).then_inc(setup_scaled, 1)

            begin, end, step, after, link = step_counter(dve, vstep, 12 + 2 * COUNTS + COUNTS * (TILES - ACT_TILES) + 9 * TILES)
            begin_tail, end_tail, _, _, link_tail = step_counter(dve, tstep, 13 + 2 * TILES)
            mean, var = ln_mv[:, :, 0], ln_mv[:, :, 1]

            def group_norm(b):
                dve.wait_ge(x_loaded, 16 * (b + 1))
                for h, part in enumerate(halves(x_c)):
                    step(v.bn_stats(gn_stats[:, h, :], part))
                after(0)
                link(v.bn_aggr(gn_mv[:, :], gn_stats[:, :, :].rearrange("p a s -> p (a s)")))
                dve.sem_inc(gn_dev_ready, 1)
                dve.wait_ge(gn_mean_ready, 2 * b + 1)
                link(v.tensor_copy(gn_mean[:, :], ps23[:, 0:1]))
                link(v.tensor_tensor(gn_dev[:, :], gn_mv[:, 0:1], gn_mean[:, :], ALU.subtract))
                v.scalar_tensor_tensor(gn_sq[:, :], gn_dev[:, :], gn_dev[:, 0:1], gn_mv[:, 1:2], ALU.mult,
                                       ALU.add).then_inc(gn_sq_ready, 1)
                dve.wait_ge(gn_mean_ready, 2 * b + 2)
                v.tensor_scalar(gn_var[:, :], ps23[:, 0:1], 1e-5, None, ALU.add).then_inc(gn_sq_ready, 1)
                dve.wait_ge(gn_pow, b + 1)
                v.scalar_tensor_tensor(gn_kbias[:, :], gn_mv[:, 0:1], -1.0, gn_scale[:, :], ALU.mult, ALU.mult)
                v.scalar_tensor_tensor(gn_bias[:, :], gn_mean[:, :], -1.0, gn_scale[:, :], ALU.mult,
                                       ALU.mult).then_inc(gn_coef, 1)

            def take_scores(b):
                dve.wait_ge(y_added, b * UNITS)
                for i in range(TILES):
                    dve.wait_ge(scores_ready, b * TILES + i + 1)
                    v.tensor_scalar(score[:, i, :], ps[(i + 1) % 2][:, :], 0.0, None, ALU.add, ALU.max,
                                    accum_out=row_max[:, i:i + 1]).then_inc(scores_copied, 1)
                dve.wait_ge(scores_copied, TILES * (b + 1))
                v.tensor_scalar(neg_max[:, :], row_max[:, :], -1.0, None, ALU.mult).then_inc(neg_max_ready, 1)

            by_sign, by_count = slice(0, ACT_TILES), slice(ACT_TILES, TILES)

            def score_variance(b):
                dve.wait_ge(squares_ready, TILES * (b + 1))
                v.tensor_scalar(score_var[:, :], sum_sq[:, :], 1.0 / N, None, ALU.mult).then_inc(score_var_ready, 1)

            def first_thresholds(b):
                dve.wait_ge(score_std_ready, b + 1)
                v.tensor_scalar(correction[:, by_sign], score_std[:, by_sign], STEP / 2, None, ALU.mult)
                v.tensor_scalar(correction[:, by_count], score_std[:, by_count], STEP, None, ALU.mult)
                v.tensor_scalar(neg_thresh[:, :], score_std[:, :], -Z0, None, ALU.mult).then_inc(thresh_ready, 1)
                link(v.tensor_scalar(thresh[:, :], score_std[:, :], Z0, None, ALU.mult))

            def count_above(half):
                middle = (ACT_TILES + TILES) // 2
                for i in range(ACT_TILES, middle) if half == 0 else range(middle, TILES):
                    after()
                    step(v.tensor_scalar(unused_v[:, i % 2, :], score[:, i, :], thresh[:, i:i + 1], None,
                                           ALU.is_ge, ALU.add, accum_out=count[:, i:i + 1]))

            def correct(b, c):
                after(0)
                dve.wait_ge(counted, (b * COUNTS + c + 1) * ACT_TILES)
                v.scalar_tensor_tensor(delta[:, by_sign], count[:, by_sign], N - 2 * TARGET,
                                       correction[:, by_sign], ALU.add, ALU.mult)
                link(v.scalar_tensor_tensor(delta[:, by_count], count[:, by_count], -TARGET,
                                              correction[:, by_count], ALU.add, ALU.mult))
                v.scalar_tensor_tensor(neg_thresh[:, :], delta[:, :], -DAMPING[c], neg_thresh[:, :],
                                       ALU.mult, ALU.add).then_inc(thresh_ready, 1)
                link(v.scalar_tensor_tensor(thresh[:, :], delta[:, :], DAMPING[c], thresh[:, :],
                                              ALU.mult, ALU.add))

            def ranks(b):
                after(0)
                dve.wait_ge(counted, (b + 1) * COUNTS * ACT_TILES)
                v.tensor_scalar(rank[:, by_sign], count[:, by_sign], -0.5, KEEP - N / 2, ALU.mult, ALU.add)
                v.tensor_scalar(rank[:, by_count], count[:, by_count], -1.0, float(KEEP), ALU.mult, ALU.add)
                link(v.tensor_copy(ladder[:, :, 0], thresh[:, :]))

            def below(pair):
                for j in pair:
                    after()
                    step(v.scalar_tensor_tensor(work[:, j % 2, :], score[:, j, :], thresh[:, j:j + 1],
                                                  score[:, j, :], ALU.is_lt, ALU.mult))
                for j in pair:
                    after()
                    step(v.max(ladder[:, j, 1:9], work[:, j % 2, :]))
                for j in pair:
                    after()
                    step(v.match_replace(work[:, j % 2, :], ladder[:, j, 1:9], work[:, j % 2, :], REPLACED))
                for j in pair:
                    after()
                    step(v.max(ladder[:, j, 9:17], work[:, j % 2, :]))

            def resolve(b, half):
                t = slice(half * TILES // 2, (half + 1) * TILES // 2)
                after(0)
                rank_b = rank[:, t].unsqueeze(2).to_broadcast([P, TILES // 2, WINDOW])
                link(v.tensor_tensor(hit[:, t, :], rungs[:, t, :], rank_b, ALU.is_equal))
                v.tensor_tensor(at_rank[:, t, :], hit[:, t, :], ladder[:, t, 0:WINDOW], ALU.mult)
                link(v.tensor_tensor(after_rank[:, t, :], hit[:, t, :], ladder[:, t, 1:WINDOW + 1], ALU.mult))
                v.reduce_sum(kept_from[:, t], at_rank[:, t, :], axis=mybir.AxisListType.X)
                link(v.reduce_sum(next_below[:, t], after_rank[:, t, :], axis=mybir.AxisListType.X))
                link(v.tensor_tensor(found[:, t], kept_from[:, t], next_below[:, t], ALU.is_gt))
                link(v.scalar_tensor_tensor(found[:, t], kept_from[:, t], 0.0, found[:, t], ALU.is_gt, ALU.mult))
                v.tensor_scalar(missed[:, t], found[:, t], -1.0, 1.0, ALU.mult, ALU.add).then_inc(missed_ready, 1)

            def read_missed(b, half):
                lo, hi = half * TILES // 2, (half + 1) * TILES // 2
                dve.wait_ge(missed_summed, 2 * b + half + 1)
                sums = (ps45, ps01)[half]
                v.tensor_copy(missed_tiles[:, lo:hi], sums[0:1, lo:hi])
                link(v.reduce_sum(missed_tiles[:, TILES:TILES + 1], sums[0:1, lo:hi], axis=mybir.AxisListType.X))
                dve.sem_inc(missed_read, 1)
                return dve.value_load(missed_bits[0:1, TILES:TILES + 1])

            def exact(i):
                dve.sem_clear(exact_step)
                v.tensor_copy(work[:, 0, :], score[:, i, :]).then_inc(exact_step, 1)
                with dve.Fori(0, FULL_ROUNDS) as r:
                    dve.wait_ge(exact_step, 2 * r + 1)
                    passed(dve)
                    v.max(top8[:, :], work[:, 0, :]).then_inc(exact_step, 1)
                    dve.wait_ge(exact_step, 2 * r + 2)
                    passed(dve)
                    v.match_replace(work[:, 0, :], top8[:, :], work[:, 0, :], REPLACED).then_inc(exact_step, 1)
                done = 2 * FULL_ROUNDS + 1
                dve.wait_ge(exact_step, done)
                v.max(top8[:, :], work[:, 0, :]).then_inc(exact_step, 1)
                dve.wait_ge(exact_step, done + 1)
                v.memset(top8[:, LAST_ROUND:8], REPLACED).then_inc(exact_step, 1)
                dve.wait_ge(exact_step, done + 2)
                v.match_replace(work[:, 0, :], top8[:, :], work[:, 0, :], REPLACED).then_inc(exact_step, 1)
                dve.wait_ge(exact_step, done + 3)
                v.tensor_scalar(score[:, i, :], work[:, 0, :], REPLACED, 0.5, ALU.is_equal,
                                ALU.subtract).then_inc(exact_step, 1)
                v.memset(kept_from[:, i:i + 1], 0.0).then_inc(exact_step, 1)
                dve.wait_ge(exact_step, done + 5)

            def probabilities(b, i, any_missed):
                dve.wait_ge(exp_ready, b * TILES + i + 1)
                passed(dve)
                with dve.If(any_missed != 0):
                    rows_missed = dve.value_load(missed_bits[0:1, i:i + 1])
                    with dve.If(rows_missed != 0):
                        after(0)
                        exact(i)
                link(v.scalar_tensor_tensor(expo[:, i % 2, :], score[:, i, :], kept_from[:, i:i + 1],
                                              expo[:, i % 2, :], ALU.is_ge, ALU.mult,
                                              accum_out=row_sum[:, i:i + 1]))
                dve.sem_inc(prob_ready, 1)

            def attended(b, i):
                link(v.reciprocal(row_inv[:, i:i + 1], row_sum[:, i:i + 1]))
                dve.wait_ge(attn_ready, b * TILES + i + 1)
                at = i % 2 * BANK
                v.scalar_tensor_tensor(t1[:, i, :], ps67[:, at:at + P], row_inv[:, i:i + 1],
                                       x_tok[:, i, :], ALU.mult, ALU.add).then_inc(t1_ready, 1)
                dve.wait_ge(t1_ready, b * TILES + i + 1)
                link(v.bn_stats(ln_stats[:, :], t1[:, i, :]))
                link(v.bn_aggr(ln_mv[:, i, :], ln_stats[:, :]))

            def layer_norm(b):
                v.tensor_scalar(ln_var[:, :], var, LN_EPS, None, ALU.add).then_inc(var_ready, 1)
                dve.wait_ge(rstd_ready, b + 1)
                link(v.tensor_tensor(ln_var2[:, :], var, ln_rstd[:, :], ALU.mult))
                link(v.tensor_tensor(ln_var2[:, :], ln_var2[:, :], ln_rstd[:, :], ALU.mult))
                v.tensor_scalar(ln_var2[:, :], ln_var2[:, :], LN_EPS, None, ALU.add).then_inc(var2_ready, 1)
                v.tensor_scalar(tu_scale[:, :], ln_rstd[:, :], 1.0, None, ALU.add)
                v.scalar_tensor_tensor(tu_bias[:, :], mean, -1.0, ln_rstd[:, :], ALU.mult, ALU.mult)
                dve.wait_ge(rstd2_ready, b + 1)
                link(v.tensor_tensor(xh_scale[:, :], ln_rstd[:, :], ln_rstd2[:, :], ALU.mult))
                v.scalar_tensor_tensor(xh_bias[:, :], mean, -1.0, xh_scale[:, :], ALU.mult,
                                       ALU.mult).then_inc(ln_coef, 1)

            def convolve(b, d, k, taps=range(1, TAPS)):
                g = (b * DIRS + d) * BLOCKS + k
                dve.wait_ge(tap_ready, g + 1)
                for n in taps:
                    if n > 1:
                        dve.wait_ge(conv_step, (TAPS - 2) * g + n - 1)
                    near, far = slice(n, N), slice(0, N - n)
                    to, src = (near, far) if d == 0 else (far, near)
                    v.scalar_tensor_tensor(conv_half[:, k, to], ps[1 + 2 * k][:, src],
                                           conv_w[:, d, k, TAPS - 1 - n:TAPS - n], conv_half[:, k, to], ALU.mult,
                                           ALU.add).then_inc(conv_step if n < TAPS - 1 else conv_summed, 1)

            def silu(b, d, k):
                dve.wait_ge(tanh_ready, (b * DIRS + d) * BLOCKS + k + 1)
                v.scalar_tensor_tensor(xs[:, k, :], xs[:, k, :], 1.0, conv_half[:, k, :], ALU.add,
                                       ALU.mult).then_inc(xs_ready, 1)

            def apply_gate(b, d, k):
                g = (b * DIRS + d) * BLOCKS + k
                dve.wait_ge(y_ready, g + 1)
                dve.wait_ge(gate_ready, g + 1)
                v.tensor_tensor(gate[:, d, k, :], gate[:, d, k, :], ps[2 * k][:, :], ALU.mult).then_inc(gated, 1)

            def dt_of(b, d, k):
                g = (b * DIRS + d) * BLOCKS + k
                dve.wait_ge(abs_ready, g + 1)
                dve.wait_ge(dA_ready, b * UNITS + d * BLOCKS * D_STATE)
                v.tensor_scalar(dt[:, k, :], dt_ps[k][:, :], dt_b[:, d, k:k + 1], 0.0, ALU.add,
                                ALU.max).then_inc(relu_ready, 1)
                dve.wait_ge(relu_ready, g + 1)
                dve.wait_ge(log_ready, g + 1)
                v.tensor_tensor(dt[:, k, :], dt[:, k, :], soft_log[:, k, :], ALU.add).then_inc(dt_ready, 1)
                dve.wait_ge(dt_ready, g + 1)
                v.tensor_tensor(dtx[:, k, :], dt[:, k, :], xs[:, k, :], ALU.mult).then_inc(dtx_ready, 1)

            def direction(b, d):
                e = b * DIRS + d
                dve.wait_ge(hi_ready, 2 * e + 2)
                v.tensor_tensor(bc_rest[:, :], dbc[0:PARTS * BC, :], bc_parts[:, :],
                                ALU.subtract).then_inc(rest_ready, 1)
                dve.wait_ge(rest_ready, e + 1)
                v.tensor_copy(bc_mid[2 * BC:3 * BC, :], bc_rest[2 * BC:3 * BC, :]).then_inc(mid_step, 1)
                dve.wait_ge(mid_step, e + 1)
                v.tensor_tensor(bc_parts[2 * BC:3 * BC, :], bc_rest[2 * BC:3 * BC, :],
                                bc_mid[2 * BC:3 * BC, :], ALU.subtract).then_inc(parts_ready, 1)
                base = b * UNITS + d * BLOCKS * D_STATE
                base_s = e * D_STATE
                dve.wait_ge(gate_ready, e * BLOCKS + 1)
                order = slice(None) if d == 0 else slice(None, None, -1)

                def scan(s, odd, first=False):
                    for k in range(BLOCKS):
                        if first and odd == 0:
                            dt_of(b, d, k)
                            dve.wait_ge(dtx_ready, e * BLOCKS + k + 1)
                        dve.wait_ge(b_ready, base_s + s + 1)
                        dve.wait_ge(scan_ready, base if first and odd == 0 else base + 2 * s + k - 1)
                        v.tensor_tensor(dbu[k][:, :], dtx[:, k, :], ps23[:, :], ALU.mult).then_inc(dbu_ready, 1)
                    for k in range(BLOCKS):
                        dve.wait_ge(dA_ready, base + 2 * s + k + 1)
                        dve.wait_ge(dbu_ready, base + 2 * s + k + 1)
                        dve.wait_ge(hc_ready, base if first else base + 2 * s + k - 3)
                        v.tensor_tensor_scan(hs[odd][:, k, order], dA[:, k, order], dbu[k][:, order], 0.0,
                                             ALU.mult, ALU.add).then_inc(scan_ready, 1)

                scan(0, 0, first=True)
                scan(1, 1, first=True)
                with dve.Fori(1, D_STATE // 2) as r:
                    for odd in range(2):
                        scan(2 * r + odd, odd)

            def mamba(b):
                convolve(b, 0, 0)
                convolve(b, 0, 1, range(1, 2))
                silu(b, 0, 0)
                convolve(b, 0, 1, range(2, TAPS))
                silu(b, 0, 1)
                direction(b, 0)
                convolve(b, 1, 0)
                apply_gate(b, 0, 0)
                convolve(b, 1, 1, range(1, 2))
                silu(b, 1, 0)
                convolve(b, 1, 1, range(2, TAPS))
                apply_gate(b, 0, 1)
                silu(b, 1, 1)
                direction(b, 1)
                apply_gate(b, 1, 0)
                apply_gate(b, 1, 1)

            def tokens_out(m):
                dve.wait_ge(mamba_out, m + 1)
                dve.wait_ge(tu_ready, TILES * (m + 1))
                link_tail(v.tensor_tensor(t2[:, :, :].rearrange("p a c -> p (a c)"),
                                       tu[:, :, :].rearrange("p a c -> p (a c)"), ps67[:, :], ALU.add))
                dve.sem_inc(t2_ready, 1)
                for i in range(TILES):
                    link_tail(v.bn_stats(ln_stats[:, :], t2[:, i, :]))
                    link_tail(v.bn_aggr(ln_mv[:, i, :], ln_stats[:, :]))
                v.tensor_scalar(ln_var[:, :], var, LN_EPS, None, ALU.add).then_inc(var3_ready, 1)
                dve.wait_ge(rstd3_ready, m + 1)
                dve.wait_ge(xh_ready, TILES * (m + 1))
                link_tail(v.tensor_copy(xh_scale[:, :], ln_rstd[:, :]))
                v.scalar_tensor_tensor(xh_bias[:, :], mean, -1.0, ln_rstd[:, :], ALU.mult,
                                       ALU.mult).then_inc(ln3_coef, 1)

            def router_logits(m):
                dve.wait_ge(logits_ready, m + 1)
                link_tail(v.tensor_copy(logits[:, :, 0:EXPERTS],
                                     ps45[:, 0:TILES * EXPERTS].rearrange("p (a e) -> p a e", e=EXPERTS)))
                for i in range(TILES):
                    last = v.max(r8[:, i, :], logits[:, i, :])
                link_tail(last)
                v.tensor_tensor(rexp[:, :, :], logits[:, :, 0:EXPERTS],
                                r8[:, :, 0:1].to_broadcast([P, TILES, EXPERTS]), ALU.subtract).then_inc(rdiff_ready, 1)

            def router_weights(m):
                dve.wait_ge(rdiff_ready, m + 1)
                link_tail(v.memset(r8[:, :, 2:8], REPLACED))
                for i in range(TILES):
                    last = v.match_replace(marked[:, i, :], r8[:, i, :], logits[:, i, :], CHOSEN)
                link_tail(last)
                dve.wait_ge(rexp_ready, m + 1)
                link_tail(v.scalar_tensor_tensor(comb[:, :, :], marked[:, :, 0:EXPERTS], CHOSEN, rexp[:, :, :],
                                              ALU.is_equal, ALU.mult))
                link_tail(v.reduce_sum(rsum[:, :], comb[:, :, :], axis=mybir.AxisListType.X))
                link_tail(v.reciprocal(rsum[:, :], rsum[:, :]))
                link_tail(v.tensor_tensor(comb[:, :, :], comb[:, :, :],
                                       rsum[:, :].unsqueeze(2).to_broadcast([P, TILES, EXPERTS]), ALU.mult))
                part = [comb_parts[:, :, i * BC:i * BC + EXPERTS] for i in range(PARTS)]
                link_tail(v.tensor_copy(part[0], comb[:, :, :]))
                link_tail(v.tensor_tensor(comb_rest[:, :, :], comb[:, :, :], part[0], ALU.subtract))
                link_tail(v.tensor_copy(part[1], comb_rest[:, :, :]))
                v.tensor_tensor(part[2], comb_rest[:, :, :], part[1], ALU.subtract).then_inc(comb_ready, 1)

            def select(m, x):
                n = m * EXPERTS + x
                dve.wait_ge(weight_ready, n + 1)
                dve.wait_ge(gelu_ready, n + 1)
                dve.wait_ge(expert_added, m * EXPERTS + max(x - 1, 0))
                v.tensor_tensor(sel_e[:, x % 2, :], act_e[:, x % 2, :], ps45[:, :], ALU.mult).then_inc(sel_ready, 1)

            def dve_image(b, m=None):
                begin(b)
                group_norm(b)
                if m is not None:
                    begin_tail(m)
                    tokens_out(m)
                take_scores(b)
                score_variance(b)
                if m is not None:
                    router_logits(m)
                first_thresholds(b)
                if m is not None:
                    router_weights(m)
                    end_tail()
                for c in range(COUNTS):
                    count_above(0)
                    if m is not None:
                        select(m, 2 * c)
                    count_above(1)
                    if c < COUNTS - 1:
                        correct(b, c)
                    if m is not None:
                        select(m, 2 * c + 1)
                ranks(b)
                below((0, 1))
                below((2, 3))
                resolve(b, 0)
                below((4, 5))
                any_missed = read_missed(b, 0)
                probabilities(b, 0, any_missed)
                probabilities(b, 1, any_missed)
                below((6, 7))
                probabilities(b, 2, any_missed)
                resolve(b, 1)
                attended(b, 0)
                probabilities(b, 3, any_missed)
                attended(b, 1)
                any_missed = read_missed(b, 1)
                for i in range(4, TILES):
                    probabilities(b, i, any_missed)
                    attended(b, i - 2)
                attended(b, TILES - 2)
                attended(b, TILES - 1)
                layer_norm(b)
                end()
                mamba(b)

            dve_image(0)
            with dve.Fori(1, BATCH) as b:
                dve_image(b, b - 1)
            begin_tail(BATCH - 1)
            tokens_out(BATCH - 1)
            router_logits(BATCH - 1)
            router_weights(BATCH - 1)
            for x in range(EXPERTS):
                select(BATCH - 1, x)
            end_tail()

        @block.tensor
        def _(pe):
            mm, tr = nc.tensor.matmul, nc.tensor.transpose
            pe.wait_ge(w_loaded, 16 * (N_LOADS + 2))
            pe.wait_ge(const_done, CONSTS)
            for n, (src, dst, _) in enumerate(jobs):
                if n >= 4:
                    pe.wait_ge(setup_evac, n - 3)
                k = src.shape[0]
                tr(ps[n % 4][:, 0:k], src, ident[0:k, 0:k]).then_inc(setup_t, 1)
            pe.wait_ge(setup_evac, QK_JOB - 3)
            mm(ps[QK_JOB % 4][:, 0:P], raw_qkv[:, 0, :], raw_qkv[:, 1, :], start=True, stop=True).then_inc(setup_t, 1)
            pe.wait_ge(setup_evac, QK_JOB + 1)
            pe.wait_ge(setup_scaled, DIRS * BLOCKS + 2)
            pe.wait_ge(setup_act, 2)

            def transpose_input(b):
                pe.wait_ge(x_loaded, 16 * (b + 1))
                pe.wait_ge(gated, DIRS * BLOCKS * b)
                for i in range(TILES):
                    last = tr(ps45[:, i * P:(i + 1) * P], x_c[:, i * P:(i + 1) * P], ident[:, :])
                last.then_inc(xtok_t, 1)
                pe.wait_ge(gn_dev_ready, b + 1)
                mm(ps23[:, 0:1], group_avg[:, :], gn_mv[:, 0:1], start=True, stop=True).then_inc(gn_mean_ready, 1)

                pe.wait_ge(gn_sq_ready, 2 * b + 1)
                mm(ps23[:, 0:1], group_avg[:, :], gn_sq[:, :], start=True, stop=True).then_inc(gn_mean_ready, 1)

            def queries_and_values(b):
                pe.wait_ge(xn_ready, 2 * b + 1)
                pe.wait_ge(gated, DIRS * BLOCKS * b)
                for h in range(HALVES):
                    last = mm(halves(ps01)[h], qk_w[:, :], halves(xn_c)[h], start=True, stop=True)
                last.then_inc(qv_ready, 1)
                pe.wait_ge(xtok_copied, b + 1)
                for i in range(TILES):
                    last = mm(ps45[:, i * P:(i + 1) * P], xn_c[:, i * P:(i + 1) * P], wv_t[:, :],
                              start=True, stop=True)
                last.then_inc(qv_ready, 1)
                pe.wait_ge(qv_copied, 2 * b + 1)
                pe.wait_ge(xn_ready, 2 * b + 2)
                pe.wait_ge(gn_sq_ready, 2 * b + 2)

            def scores(b, i):
                if i >= 2:
                    pe.wait_ge(scores_copied, b * TILES + i - 1)
                for h in range(HALVES):
                    last = mm(halves(ps[(i + 1) % 2])[h], q_c[:, i * P:(i + 1) * P], halves(xk_c)[h],
                              start=True, stop=True)
                last.then_inc(scores_ready, 1)

            def sum_missed(b, half):
                lo, hi = half * TILES // 2, (half + 1) * TILES // 2
                pe.wait_ge(missed_ready, 2 * b + half + 1)
                if half == 1:
                    pe.wait_ge(out_copied, b)
                mm((ps45, ps01)[half][0:1, lo:hi], ones[:, :], missed[:, lo:hi], start=True, stop=True).then_inc(missed_summed, 1)

            def transpose_prob(b, i):
                pe.wait_ge(prob_ready, b * TILES + i + 1)
                pe.wait_ge(probt_copied, b * TILES + max(i - 1, 0))
                pe.wait_ge(missed_read, 2 * b + (1 if i < TILES // 2 else 2))
                for j in range(TILES):
                    last = tr(ps[1 + i % 2][:, j * P:(j + 1) * P], expo[:, i % 2, j * P:(j + 1) * P], ident[:, :])
                last.then_inc(prob_transposed, 1)

            def attend(b, i):
                pe.wait_ge(probt_copied, b * TILES + i + 1)
                pe.wait_ge(t1_ready, b * TILES + max(i - 1, 0))
                at = i % 2 * BANK
                for j in range(TILES):
                    last = mm(ps67[:, at:at + P], prob_t[:, i % 2, j, :], v_tok[:, j, :], start=j == 0,
                              stop=j == TILES - 1)
                last.then_inc(attn_ready, 1)

            def mamba_input(b):
                pe.wait_ge(xh_ready, TILES * (b + 1))
                pe.wait_ge(out_copied, b)
                for i in range(TILES):
                    last = tr(ps01[:, i * P:(i + 1) * P], xh[:, i, :], ident[:, :])
                last.then_inc(xh_t, 1)
                pe.wait_ge(mx_ready, b + 1)

            def project_x(b, d, k):
                dst = ps[1 + 2 * k]
                for h in range(HALVES):
                    last = mm(halves(dst)[h], x_in_t[:, d, k, :], halves(mx)[h], start=True, stop=True)
                last.then_inc(conv_filled, 1)

            def project_z(b, d, k):
                pe.wait_ge(gated, b * DIRS * BLOCKS + (k + 1 if d else 0))
                for h in range(HALVES):
                    last = mm(halves(ps[2 * k])[h], z_in_t[:, d, k, :], halves(mx)[h], start=True, stop=True)
                last.then_inc(z_filled, 1)

            def project_dbc(b, d, k):
                pe.wait_ge(conv_summed, (b * DIRS + d) * BLOCKS + 1)
                pe.wait_ge(xs_ready, (b * DIRS + d) * BLOCKS + k + 1)
                for h in range(HALVES):
                    last = mm(halves(ps23)[h], xproj_t[:, d, k, :], xs[:, k, h * BANK:(h + 1) * BANK],
                              start=k == 0, stop=k == BLOCKS - 1)
                if k == BLOCKS - 1:
                    last.then_inc(dbc_filled, 1)

            def direction(b, d):
                e = b * DIRS + d
                if d == 0:
                    pe.wait_ge(t1_ready, TILES * (b + 1))
                    pe.wait_ge(probt_copied, TILES * (b + 1))
                    project_x(b, d, 0)
                    project_x(b, d, 1)
                    project_z(b, d, 0)
                    project_z(b, d, 1)
                    project_dbc(b, d, 0)
                    project_dbc(b, d, 1)
                else:
                    project_z(b, d, 0)
                    project_dbc(b, d, 0)
                    project_z(b, d, 1)
                    project_dbc(b, d, 1)
                pe.wait_ge(hi_ready, 2 * e + 1)
                rows = slice(PARTS * BC, PARTS * BC + DT_RANK)
                for k in range(BLOCKS):
                    if k == 0:
                        pe.wait_ge(conv_summed, (e + 1) * BLOCKS)
                    else:
                        pe.wait_ge(z_acts, 2 * e * BLOCKS + 2)
                    for h in range(HALVES):
                        last = mm(halves(dt_ps[k])[h], dtproj_t[rows, d, k, :], dbc[rows, h * BANK:(h + 1) * BANK],
                                  start=True, stop=True)
                    last.then_inc(dt_filled, 1)
                base = b * UNITS + d * BLOCKS * D_STATE
                base_s = e * D_STATE

                def spread(s):
                    pe.wait_ge(dbu_ready, base + 2 * s)
                    for h in range(HALVES):
                        last = mm(halves(ps23)[h], pick[:, ds(s, 1), :].rearrange("p o m -> p (o m)"),
                                  bc_parts[:, h * BANK:(h + 1) * BANK], start=True, stop=True)
                    last.then_inc(b_ready, 1)
                    pe.wait_ge(c_copied, base_s + s)
                    for h in range(HALVES):
                        last = mm(halves(ps67)[h], pick[:, ds(s + D_STATE, 1), :].rearrange("p o m -> p (o m)"),
                                  bc_parts[:, h * BANK:(h + 1) * BANK], start=True, stop=True)
                    last.then_inc(c_ready, 1)

                def add(s, odd, stop=False):
                    for k in range(BLOCKS):
                        pe.wait_ge(hc_ready, base + 2 * s + k + 1)
                        for h in range(HALVES):
                            last = mm(halves(ps[2 * k])[h], ident[:, :], hc[odd][:, k, h * BANK:(h + 1) * BANK],
                                      start=False, stop=stop)
                        last.then_inc(y_added, 1)
                        if stop:
                            pe.wait_ge(y_added, base + 2 * s + k + 1)
                            pe.sem_inc(y_ready, 1)

                pe.wait_ge(hi_ready, 2 * e + 2)
                pe.wait_ge(parts_ready, e + 1)
                pe.wait_ge(mid_ready, e + 1)
                pe.wait_ge(relu_ready, e * BLOCKS + 1)
                spread(0)
                for k in range(BLOCKS):
                    pe.wait_ge((relu_ready, z_acts)[k], (1 + k) * (e + 1) * BLOCKS)
                    for h in range(HALVES):
                        mm(halves(ps[2 * k])[h], skip_diag[:, d, k, :], xs[:, k, h * BANK:(h + 1) * BANK],
                           start=True, stop=False)
                spread(1)
                with pe.Fori(1, D_STATE // 2) as r:
                    for odd in range(2):
                        spread(2 * r + odd)
                        add(2 * r + odd - 2, odd)
                if d == 0:
                    pe.wait_ge(dbu_ready, base + BLOCKS * D_STATE)
                    pe.wait_ge(c_copied, base_s + D_STATE)
                add(D_STATE - 2, 0)
                if d == 0:
                    project_x(b, 1, 0)
                    project_x(b, 1, 1)
                add(D_STATE - 1, 1, stop=True)

            def project_out(m):
                pe.wait_ge(gated, DIRS * BLOCKS * (m + 1))
                pe.wait_ge(c_copied, DIRS * D_STATE * (m + 1))
                for i in range(TILES):
                    for d in range(DIRS):
                        for k in range(BLOCKS):
                            last = mm(ps67[:, i * P:(i + 1) * P], gate[:, d, k, i * P:(i + 1) * P],
                                      outproj_t[:, d, k, :], start=d + k == 0, stop=d + k == DIRS + BLOCKS - 2)
                last.then_inc(mamba_out, 1)

            def expert_input(m):
                pe.wait_ge(en_ready, TILES * (m + 1))
                pe.wait_ge(t2_ready, m + 1)
                for i in range(TILES):
                    last = tr(ps67[:, i * P:(i + 1) * P], en[:, i, :], ident[:, :])
                last.then_inc(en_t, 1)

            def route(m, b=None):
                pe.wait_ge(ec_ready, m + 1)
                if b is not None:
                    pe.wait_ge(qv_copied, 2 * b + 2)
                for i in range(TILES):
                    last = mm(ps45[:, i * EXPERTS:(i + 1) * EXPERTS], e_c[:, i * P:(i + 1) * P], router_t[:, :],
                              start=True, stop=True)
                last.then_inc(logits_ready, 1)

            def hidden(m, x):
                pe.wait_ge(gelu_ready, m * EXPERTS + max(x - 1, 0))
                for h in range(HALVES):
                    last = mm(halves(ps[1 + 2 * (x % 2)])[h], w1[:, x, :], halves(e_c)[h], start=True, stop=True)
                last.then_inc(hidden_ready, 1)

            def weights(m, x):
                pe.wait_ge(sel_ready, m * EXPERTS + x)
                for h in range(HALVES):
                    last = mm(halves(ps45)[h], pick[:, x, :], comb_parts_t[:, h * BANK:(h + 1) * BANK],
                              start=True, stop=True)
                last.then_inc(weight_ready, 1)

            def add_expert(m, x):
                pe.wait_ge(sel_ready, m * EXPERTS + x + 1)
                for h in range(HALVES):
                    last = mm(halves(ps01)[h], w2[:, x, :], sel_e[:, x % 2, h * BANK:(h + 1) * BANK],
                              start=False, stop=x == EXPERTS - 1)
                last.then_inc(expert_added, 1)

            def experts(m, b=None):
                if b is not None:
                    pe.wait_ge(scores_copied, TILES * (b + 1))
                hidden(m, 0)
                pe.wait_ge(comb_ready, m + 1)
                for i in range(TILES):
                    last = tr(ps45[0:EXPERTS, i * P:(i + 1) * P], comb[:, i, :], ident[:, :])
                last.then_inc(comb_transposed, 1)
                parts_ps = ps67[0:PARTS * BC, :].bitcast(BF16)
                for i in range(TILES):
                    last = tr(parts_ps[:, i * P:(i + 1) * P], comb_parts[:, i, :], ident_bf[:, :])
                last.then_inc(comb_transposed, 1)
                pe.wait_ge(comb_copied, 2 * m + 2)
                weights(m, 0)
                hidden(m, 1)
                pe.wait_ge(t2e_ready, TILES * (m + 1))
                for h in range(HALVES):
                    mm(halves(ps01)[h], b2[:, :], comb_t[:, h * BANK:(h + 1) * BANK], start=True, stop=False)
                for i in range(TILES):
                    mm(ps01[:, i * P:(i + 1) * P], t2e[:, i, :], ident[:, :], start=False, stop=False)
                for x in range(1, EXPERTS):
                    weights(m, x)
                    if x + 1 < EXPERTS:
                        hidden(m, x + 1)
                    add_expert(m, x - 1)
                add_expert(m, EXPERTS - 1)

            def pe_image(b, m=None):
                transpose_input(b)
                if m is not None:
                    project_out(m)
                queries_and_values(b)
                for i in range(TILES):
                    scores(b, i)
                    if m is not None and i == 3:
                        expert_input(m)
                if m is not None:
                    route(m, b)
                    experts(m, b)
                pe.wait_ge(qv_copied, 2 * b + 2)
                sum_missed(b, 0)
                transpose_prob(b, 0)
                for i in range(TILES):
                    if i + 1 < TILES:
                        transpose_prob(b, i + 1)
                    if i == 1:
                        sum_missed(b, 1)
                    attend(b, i)
                mamba_input(b)
                for d in range(DIRS):
                    direction(b, d)

            pe_image(0)
            with pe.Fori(1, BATCH) as b:
                pe_image(b, b - 1)
            m = BATCH - 1
            project_out(m)
            expert_input(m)
            route(m)
            experts(m)


_WAY = ["in_proj_w", "conv_w", "conv_b", "x_proj_w", "dt_proj_w", "dt_proj_b", "A_log", "D", "out_proj_w"]
_INS = (["x", "L0_conv_Wq", "L0_conv_Wk", "L0_conv_Wv", "L1_attn_ln_gamma", "L1_attn_ln_beta"]
        + [f"L1_attn_{way}_{name}" for way in "fb" for name in _WAY]
        + ["L1_ffn_" + name for name in ("router_w", "w1", "b1", "w2", "b2")])


def kernel(**inputs):
    import numpy as _np
    import concourse.bacc as _bacc
    from concourse import mybir as _mybir
    from concourse.bass_utils import run_bass_kernel_spmd as _run

    nc = _bacc.Bacc("TRN2", target_bir_lowering=False, num_devices=1)
    arrays, args = {}, {}
    for name in _INS:
        a = _np.ascontiguousarray(inputs[name])
        arrays[f"in_{name}"] = a
        args[name] = nc.dram_tensor(f"in_{name}", a.shape, _mybir.dt.from_np(a.dtype), kind="ExternalInput").ap()
    out = nc.dram_tensor("out_0", inputs["x"].shape, _mybir.dt.from_np(_np.dtype("float32")),
                         kind="ExternalOutput").ap()
    hybrid_block(nc, args, out)
    r = _run(nc, [arrays], core_ids=[0])
    return r.results[0]["out_0"]
```

```python
import concourse.bass as bass
from concourse import mybir
from contextlib import ExitStack
import math


def normal_tail(share):
    low, high = -9.0, 9.0
    for _ in range(60):
        mid = (low + high) / 2
        low, high = (mid, high) if 0.5 * math.erfc(mid / math.sqrt(2.0)) > share else (low, mid)
    return low


def hybrid_block(nc, t_in, out):
    F32, BF16 = mybir.dt.float32, mybir.dt.bfloat16
    ALU, ACT = mybir.AluOpType, mybir.ActivationFunctionType
    ds = bass.ds

    BATCH, C, H, W = t_in["x"].shape
    N = H * W
    P = 128
    TILES = N // P
    BANK = 512
    HALVES = N // BANK
    KEEP = max(1, int(0.1 * N))
    FULL_ROUNDS, LAST_ROUND = divmod(KEEP, 8)
    GROUP = C // 32
    D_INNER, D_STATE, DT_RANK, TAPS = 256, 16, 16, 4
    BLOCKS = D_INNER // P
    DIRS = 2
    EXPERTS = t_in["L1_ffn_router_w"].shape[0]
    UNITS = DIRS * BLOCKS * D_STATE
    BC = 2 * D_STATE
    PARTS = 3
    WINDOW = 16
    TARGET = KEEP - (WINDOW - 1) / 2
    Z0 = normal_tail(TARGET / N)
    DENSITY = math.exp(-Z0 * Z0 / 2) / math.sqrt(2 * math.pi)
    STEP = 1 / (N * DENSITY)
    DAMPING = (1.0, 0.6, 0.5)
    COUNTS = len(DAMPING) + 1
    ACT_TILES = 4
    REPLACED = -3.0e38
    CHOSEN = 3.0e38
    LN_EPS = 1e-5

    x_v = t_in["x"].rearrange("b c h w -> b c (h w)")
    out_v = out.rearrange("b c h w -> b c (h w)")

    ctx = ExitStack()
    with ctx:
        def sb(name, shape, dt=F32):
            return ctx.enter_context(nc.sbuf_tensor(name, shape, dt))

        def sem(name):
            return ctx.enter_context(nc.semaphore(name))

        ident = sb("ident", [P, P])
        ident_bf = sb("ident_bf", [P, P], BF16)
        group_avg = sb("group_avg", [P, P])
        pick = sb("pick", [PARTS * BC, BC, P], BF16)
        neg_half = sb("neg_half", [P, TILES])
        qk_w = sb("qk_w", [P, P])
        wv_t = sb("wv_t", [P, P])
        x_in_t = sb("x_in_t", [P, DIRS, BLOCKS, P])
        z_in_t = sb("z_in_t", [P, DIRS, BLOCKS, P])
        xproj_t = sb("xproj_t", [P, DIRS, BLOCKS, P])
        dtproj_t = sb("dtproj_t", [P, DIRS, BLOCKS, P])
        outproj_t = sb("outproj_t", [P, DIRS, BLOCKS, P])
        skip_diag = sb("skip_diag", [P, DIRS, BLOCKS, P])
        w1 = sb("w1", [P, EXPERTS, P])
        w2 = sb("w2", [P, EXPERTS, P])
        router_t = sb("router_t", [P, EXPERTS])
        b1_t = sb("b1_t", [P, EXPERTS])
        b2 = sb("b2", [EXPERTS, P])
        conv_w = sb("conv_w", [P, DIRS, BLOCKS, TAPS])
        VECS = 3 * DIRS * BLOCKS + 2
        vec = sb("vec", [P, VECS])
        conv_b, dt_b, skip = (vec[:, i * DIRS * BLOCKS:(i + 1) * DIRS * BLOCKS].rearrange("p (d k) -> p d k", d=DIRS)
                              for i in range(3))
        gamma, beta = vec[:, VECS - 2:VECS - 1], vec[:, VECS - 1:VECS]
        decay = sb("decay", [P, DIRS, BLOCKS, D_STATE])
        raw_qkv = sb("raw_qkv", [P, 3, P])
        raw_vec = sb("raw_vec", [VECS, P])
        raw_small = sb("raw_small", [EXPERTS, 2, P])

        x_c = sb("x_c", [P, N])
        xn_c = sb("xn_c", [P, N])
        q_c = sb("q_c", [P, N])
        v_tok = sb("v_tok", [P, TILES, P])
        x_tok = sb("x_tok", [P, TILES, P])
        xk_c = sb("xk_c", [P, N])
        ring = sb("ring", [P, TILES, N])
        score = ring
        expo = sb("expo", [P, 2, N])
        work = sb("work", [P, 2, N])
        prob_t = sb("prob_t", [P, 2, TILES, P])
        dbu = [sb("dbu0", [P, N]), sb("dbu1", [P, N])]
        unused_a, unused_v = (tile[:, :].bitcast(BF16).rearrange("p (a n) -> p a n", a=2) for tile in dbu)
        top8 = sb("top8", [P, 8])
        row_max = sb("row_max", [P, TILES])
        neg_max = sb("neg_max", [P, TILES])
        sum_sq = sb("sum_sq", [P, TILES])
        score_var = sb("score_var", [P, TILES])
        score_std = sb("score_std", [P, TILES])
        correction = sb("correction", [P, TILES])
        thresh = sb("thresh", [P, TILES])
        neg_thresh = sb("neg_thresh", [P, TILES])
        count = sb("count", [P, TILES])
        delta = sb("delta", [P, TILES])
        rank = sb("rank", [P, TILES])
        ladder = sb("ladder", [P, TILES, WINDOW + 1])
        rungs = sb("rungs", [P, TILES, WINDOW])
        hit = sb("hit", [P, TILES, WINDOW])
        at_rank = sb("at_rank", [P, TILES, WINDOW])
        after_rank = sb("after_rank", [P, TILES, WINDOW])
        kept_from = sb("kept_from", [P, TILES])
        one_less = sb("one_less", [P, TILES])
        found = sb("found", [P, TILES])
        missed = sb("missed", [P, TILES])
        ones = sb("ones", [P, 1])
        half_pow = sb("half_pow", [P, TILES])
        gn_kbias = sb("gn_kbias", [P, 1])
        missed_tiles = sb("missed_tiles", [1, TILES + 1])
        missed_bits = missed_tiles[:, :].bitcast(mybir.dt.int32)
        row_sum = sb("row_sum", [P, TILES])
        row_inv = sb("row_inv", [P, TILES])
        gn_stats = sb("gn_stats", [P, 2, 6])
        gn_mv = sb("gn_mv", [P, 2])
        gn_dev = sb("gn_dev", [P, 1])
        gn_sq = sb("gn_sq", [P, 1])
        gn_mean = sb("gn_mean", [P, 1])
        gn_var = sb("gn_var", [P, 1])
        gn_scale = sb("gn_scale", [P, 1])
        gn_bias = sb("gn_bias", [P, 1])
        t1 = sb("t1", [P, TILES, P])
        ln_stats = sb("ln_stats", [P, TILES, 6])
        ln_mv = sb("ln_mv", [P, TILES, 2])
        ln_var = sb("ln_var", [P, TILES])
        ln_rstd = sb("ln_rstd", [P, TILES])
        ln_var2 = sb("ln_var2", [P, TILES])
        ln_rstd2 = sb("ln_rstd2", [P, TILES])
        xh_scale = sb("xh_scale", [P, TILES])
        xh_bias = sb("xh_bias", [P, TILES])
        tu_scale = sb("tu_scale", [P, TILES])
        tu_bias = sb("tu_bias", [P, TILES])
        xh = sb("xh", [P, TILES, P])
        tu = sb("tu", [P, TILES, P])

        mx = sb("mx", [P, N])
        xs_f = sb("xs_f", [P, BLOCKS, N])
        dt_f = sb("dt_f", [P, BLOCKS, N])
        dtx_f = sb("dtx_f", [P, BLOCKS, N])
        dbc_f = sb("dbc_f", [P, N])
        flat_tile = lambda tile: tile[:, :, :].rearrange("p a c -> p (a c)")
        xs = [[xs_f[:, 0, :], xs_f[:, 1, :]], [xn_c[:, :], q_c[:, :]]]
        dt = [[dt_f[:, 0, :], dt_f[:, 1, :]], [xk_c[:, :], flat_tile(v_tok)]]
        dtx = [[dtx_f[:, 0, :], dtx_f[:, 1, :]], [flat_tile(x_tok), flat_tile(t1)]]
        dbc = [dbc_f[:, :], flat_tile(xh)]
        bc_parts = [sb("bc_parts_f", [PARTS * BC, N], BF16), sb("bc_parts_b", [PARTS * BC, N], BF16)]
        bc_rest = sb("bc_rest", [PARTS * BC, N])
        bc_mid = sb("bc_mid", [PARTS * BC, N], BF16)
        gate = sb("gate", [P, DIRS, BLOCKS, N])
        dA, c_all, hs_odd, hc_odd = (ring[:, 2 * i:2 * i + 2, :] for i in range(4))
        hs, hc = [expo, hs_odd], [work, hc_odd]
        conv_half = soft_log = [work, hc_odd]
        z_tmp = [[expo, prob_t[:, :, :, :].rearrange("p r a c -> p r (a c)")], [c_all, hs_odd]]
        raw_in = hs_odd[:, 0, :].rearrange("p (d k c) -> p d k c", d=DIRS, k=2 * BLOCKS)
        raw_xproj = hs_odd[:, 1, 0:BANK].rearrange("p (d c) -> p d c", d=DIRS)
        raw_out = hs_odd[:, 1, BANK:N].rearrange("p (d c) -> p d c", d=DIRS)
        raw_dtproj = c_all[:, 0, 0:BANK].rearrange("p (d k c) -> p d k c", d=DIRS, k=BLOCKS)

        t2 = dtx_f[:, 0, :].rearrange("p (a c) -> p a c", c=P)
        en = dtx_f[:, 1, :].rearrange("p (a c) -> p a c", c=P)
        t2e = t2
        e_c = xs_f[:, 0, :]
        out_c = xs_f[:, 1, :]
        logits = sb("logits", [P, TILES, 2 * EXPERTS])
        marked = sb("marked", [P, TILES, 2 * EXPERTS])
        r8 = sb("r8", [P, TILES, 8])
        rexp = sb("rexp", [P, TILES, EXPERTS])
        rsum = sb("rsum", [P, TILES])
        comb = sb("comb", [P, TILES, EXPERTS])
        comb_parts = sb("comb_parts", [P, TILES, PARTS * BC], BF16)
        comb_rest = sb("comb_rest", [P, TILES, EXPERTS])
        comb_t = dbc_f[0:EXPERTS, :]
        comb_parts_t = bc_parts[0]
        act_e = dt_f
        sel_e = gate[:, 0, :, :]

        ps = [ctx.enter_context(nc.psum_tensor(f"ps{i}", [P, N], F32)) for i in range(4)]
        ps01, ps23, ps45, ps67 = ps

        w_loaded = sem("w_loaded")
        const_step = sem("const_step")
        waits_passed = sem("waits_passed")
        const_done = sem("const_done")
        setup_cleared = sem("setup_cleared")
        setup_t = sem("setup_t")
        setup_evac = sem("setup_evac")
        setup_scaled = sem("setup_scaled")
        setup_act = sem("setup_act")
        vstep = sem("vstep")
        tstep = sem("tstep")
        astep = sem("astep")
        gate_step = sem("gate_step")
        x_loaded = sem("x_loaded")
        gn_dev_ready = sem("gn_dev_ready")
        gn_mean_ready = sem("gn_mean_ready")
        gn_sq_ready = sem("gn_sq_ready")
        gn_pow = sem("gn_pow")
        gn_coef = sem("gn_coef")
        xtok_t = sem("xtok_t")
        xtok_copied = sem("xtok_copied")
        xn_ready = sem("xn_ready")
        qv_ready = sem("qv_ready")
        qv_copied = sem("qv_copied")
        scores_ready = sem("scores_ready")
        scores_copied = sem("scores_copied")
        squares_ready = sem("squares_ready")
        score_var_ready = sem("score_var_ready")
        score_std_ready = sem("score_std_ready")
        thresh_ready = sem("thresh_ready")
        counted = sem("counted")
        missed_ready = sem("missed_ready")
        missed_summed = sem("missed_summed")
        missed_read = sem("missed_read")
        exact_step = sem("exact_step")
        neg_max_ready = sem("neg_max_ready")
        exp_ready = sem("exp_ready")
        prob_ready = sem("prob_ready")
        prob_transposed = sem("prob_transposed")
        probt_copied = sem("probt_copied")
        attn_ready = sem("attn_ready")
        t1_ready = sem("t1_ready")
        var_ready = sem("var_ready")
        rstd_ready = sem("rstd_ready")
        var2_ready = sem("var2_ready")
        rstd2_ready = sem("rstd2_ready")
        ln_coef = sem("ln_coef")
        xh_ready = sem("xh_ready")
        xh_t = sem("xh_t")
        tu_ready = sem("tu_ready")
        mx_ready = sem("mx_ready")
        conv_filled = sem("conv_filled")
        z_filled = sem("z_filled")
        dbc_filled = sem("dbc_filled")
        dt_filled = sem("dt_filled")
        tap_ready = sem("tap_ready")
        conv_step = sem("conv_step")
        conv_summed = sem("conv_summed")
        tanh_ready = sem("tanh_ready")
        xs_ready = sem("xs_ready")
        z_acts = sem("z_acts")
        gate_ready = sem("gate_ready")
        hi_ready = sem("hi_ready")
        rest_ready = sem("rest_ready")
        mid_ready = sem("mid_ready")
        mid_step = sem("mid_step")
        parts_ready = sem("parts_ready")
        abs_ready = sem("abs_ready")
        relu_ready = sem("relu_ready")
        log_ready = sem("log_ready")
        dt_ready = sem("dt_ready")
        dtx_ready = sem("dtx_ready")
        dtx_b_ready = sem("dtx_b_ready")
        b_ready = sem("b_ready")
        dbu_ready = sem("dbu_ready")
        c_ready = sem("c_ready")
        c_copied = sem("c_copied")
        dA_ready = sem("dA_ready")
        scan_ready = sem("scan_ready")
        hc_ready = sem("hc_ready")
        y_added = sem("y_added")
        y_ready = sem("y_ready")
        gated = sem("gated")
        mamba_out = sem("mamba_out")
        t2_ready = sem("t2_ready")
        var3_ready = sem("var3_ready")
        rstd3_ready = sem("rstd3_ready")
        ln3_coef = sem("ln3_coef")
        en_ready = sem("en_ready")
        en_t = sem("en_t")
        ec_ready = sem("ec_ready")
        t2e_ready = sem("t2e_ready")
        logits_ready = sem("logits_ready")
        rdiff_ready = sem("rdiff_ready")
        rexp_ready = sem("rexp_ready")
        comb_ready = sem("comb_ready")
        comb_transposed = sem("comb_transposed")
        comb_copied = sem("comb_copied")
        hidden_ready = sem("hidden_ready")
        gelu_ready = sem("gelu_ready")
        weight_ready = sem("weight_ready")
        sel_ready = sem("sel_ready")
        expert_added = sem("expert_added")
        out_copied = sem("out_copied")
        out_stored = sem("out_stored")

        block = ctx.enter_context(nc.Block())

        conv_ps = ((ps23, ps67), (ps01, ps45))
        z_ps = ((ps01, ps45), (ps67, ps01))
        dbc_ps = (ps23, ps45)
        dt_ps = ((ps67, ps23), (ps01, ps45))

        def token_half(half):
            return slice(half * TILES // 2, (half + 1) * TILES // 2)

        def halves(tile):
            return [tile[:, h * BANK:(h + 1) * BANK] for h in range(HALVES)]

        WAYS = ["f", "b"]
        jobs = [(raw_qkv[:, 2, :], wv_t[:, :], 1.0)]
        for d in range(DIRS):
            for k in range(BLOCKS):
                jobs.append((raw_in[:, d, k, :], x_in_t[:, d, k, :], 1.0))
                jobs.append((raw_in[:, d, BLOCKS + k, :], z_in_t[:, d, k, :], 1.0))
                jobs.append((raw_xproj[:, d, k * P:(k + 1) * P], xproj_t[:, d, k, :], 1.0))
                jobs.append((raw_dtproj[:, d, k, :], dtproj_t[:, d, k, :], 1.0))
                jobs.append((raw_out[:, d, k * P:(k + 1) * P], outproj_t[:, d, k, :], 0.5))
        jobs.append((raw_vec[:, :], vec[:, :], 1.0))
        jobs.append((raw_small[:, 0, :], router_t[:, :], 1.0))
        jobs.append((raw_small[:, 1, :], b1_t[:, :], 1.0))
        QK_JOB = len(jobs)
        N_LOADS = 32

        CONSTS = 9 + WINDOW

        def passed(eng):
            eng.sem_inc(waits_passed, 1)

        def step_counter(eng, signal, per_round):
            rnd, steps = [0], [0]

            def begin(r):
                rnd[0], steps[0] = r, 0

            def end():
                assert steps[0] == per_round, steps[0] - per_round

            def step(ins):
                steps[0] += 1
                ins.then_inc(signal, 1)

            def after(back=1):
                eng.wait_ge(signal, rnd[0] * per_round + steps[0] - back)
                passed(eng)

            def link(ins):
                step(ins)
                after(0)

            def steps_now(back_to=None):
                if back_to is not None:
                    steps[0] = back_to
                return steps[0]

            return begin, end, step, after, link, steps_now

        @block.sync
        def _(sp):
            loads = 0

            def load(dst, src):
                sp.dma_start(dst, src).then_inc(w_loaded, 16)

            for i, name in enumerate(("Wq", "Wk", "Wv")):
                load(raw_qkv[:, i, :], t_in["L0_conv_" + name][:, :])
            sp.wait_ge(setup_cleared, 2)
            loads = 3
            for d, way in enumerate(WAYS):
                g = lambda s: t_in[f"L1_attn_{way}_{s}"]
                xp = g("x_proj_w")
                for part in range(PARTS):
                    load(raw_xproj[part * BC:(part + 1) * BC, d, :], xp[DT_RANK:DT_RANK + BC, :])
                load(raw_xproj[PARTS * BC:PARTS * BC + DT_RANK, d, :], xp[0:DT_RANK, :])
                load(raw_dtproj[:, d, :, PARTS * BC:PARTS * BC + DT_RANK],
                     g("dt_proj_w").rearrange("(k p) r -> p k r", p=P))
                load(raw_in[:, d, :, :], g("in_proj_w").rearrange("(k p) c -> p k c", p=P))
                load(raw_out[:, d, :], g("out_proj_w")[:, :])
                load(conv_w[:, d, :, :], g("conv_w").rearrange("(k p) o j -> p k (o j)", p=P))
                for i, name in enumerate(("conv_b", "dt_proj_b", "D")):
                    row = (i * DIRS + d) * BLOCKS
                    load(raw_vec[row:row + BLOCKS, :], g(name).rearrange("(k p) -> k p", p=P))
                load(decay[:, d, :, :], g("A_log").rearrange("(k p) s -> p k s", p=P))
                loads += 12
            load(w1[:, :, :], t_in["L1_ffn_w1"].rearrange("e d f -> d e f"))
            load(w2[:, :, :], t_in["L1_ffn_w2"].rearrange("e f d -> f e d"))
            load(raw_small[:, 0, :], t_in["L1_ffn_router_w"][:, :])
            load(raw_small[:, 1, :], t_in["L1_ffn_b1"][:, :])
            load(b2[:, :], t_in["L1_ffn_b2"][:, :])
            load(raw_vec[VECS - 2:VECS - 1, :], t_in["L1_attn_ln_gamma"].rearrange("(o p) -> o p", o=1))
            load(raw_vec[VECS - 1:VECS, :], t_in["L1_attn_ln_beta"].rearrange("(o p) -> o p", o=1))
            loads += 7
            assert loads == N_LOADS + 2, loads

            def load_image(b):
                sp.wait_ge(xn_ready, 2 * b)
                sp.wait_ge(xtok_copied, b)
                sp.dma_start(x_c[:, :], x_v[ds(b, 1), :, :].rearrange("o c n -> (o c) n")).then_inc(x_loaded, 16)

            def store_image(b):
                sp.wait_ge(out_copied, b + 1)
                passed(sp)
                sp.dma_start(out_v[ds(b, 1), :, :].rearrange("o c n -> (o c) n"), out_c).then_inc(out_stored, 16)
                sp.wait_ge(out_stored, 16 * (b + 1))
                passed(sp)

            load_image(0)
            with sp.Fori(1, BATCH) as b:
                load_image(b)
                store_image(b - 1)
            store_image(BATCH - 1)

        @block.gpsimd
        def _(pool):
            pool.memset(raw_xproj[:, :, :], 0.0).then_inc(setup_cleared, 1)
            pool.memset(raw_dtproj[:, :, :, :], 0.0).then_inc(setup_cleared, 1)
            pool.memset(neg_half[:, :], -0.5).then_inc(const_done, 1)
            pool.memset(half_pow[:, :], 0.5).then_inc(const_done, 1)
            pool.memset(ones[:, :], 1.0).then_inc(const_done, 1)
            for j in range(WINDOW):
                pool.memset(rungs[:, :, j], float(j)).then_inc(const_done, 1)
            pool.memset(logits[:, :, :], REPLACED).then_inc(const_done, 1)
            pool.memset(comb_parts[:, :, :], 0.0).then_inc(const_done, 1)
            pool.memset(ident[:, :], 0.0).then_inc(const_step, 1)
            pool.memset(ident_bf[:, :], 0.0).then_inc(const_step, 1)
            pool.memset(group_avg[:, :], 1.0 / GROUP).then_inc(const_step, 1)
            pool.memset(pick[:, :, :], 0.0).then_inc(const_step, 1)
            pool.wait_ge(const_step, 4)
            for m in (ident, ident_bf):
                pool.affine_select(out=m[:, :], in_=m[:, :], compare_op=ALU.not_equal, fill=1.0, base=0,
                                   pattern=[[-1, P]], channel_multiplier=1).then_inc(const_done, 1)
            gv = group_avg[:, :].rearrange("p (g c) -> p g c", c=GROUP)
            pool.affine_select(out=gv, in_=gv, compare_op=ALU.is_ge, fill=0.0, base=0,
                               pattern=[[-GROUP, P // GROUP], [0, GROUP]], channel_multiplier=1).then_inc(const_step, 1)
            pool.wait_ge(const_step, 5)
            pool.affine_select(out=gv, in_=gv, compare_op=ALU.is_ge, fill=0.0, base=GROUP - 1,
                               pattern=[[GROUP, P // GROUP], [0, GROUP]], channel_multiplier=-1).then_inc(const_done, 1)
            for part in range(PARTS):
                pool.wait_ge(const_step, 5 + part)
                pool.affine_select(out=pick[:, :, :], in_=pick[:, :, :], compare_op=ALU.not_equal, fill=1.0,
                                   base=-part * BC, pattern=[[-1, BC], [0, P]],
                                   channel_multiplier=1).then_inc(const_step, 1)
            pool.wait_ge(const_step, 5 + PARTS)
            pool.sem_inc(const_done, 1)

            def expert_norm(m):
                pool.wait_ge(var3_ready, m + 1)
                pool.tensor_tensor(ln_rstd[:, :], ln_var[:, :], neg_half[:, :], ALU.pow).then_inc(rstd3_ready, 1)
                for i in range(TILES):
                    pool.wait_ge(en_ready, TILES * m + i + 1)
                    pool.tensor_tensor(t2e[:, i, :], t2[:, i, :], en[:, i, :], ALU.add).then_inc(t2e_ready, 1)

            def group_norm(b):
                pool.wait_ge(gn_sq_ready, 2 * b + 2)
                pool.tensor_tensor(gn_scale[:, :], gn_var[:, :], neg_half[:, 0:1], ALU.pow).then_inc(gn_pow, 1)

            def score_deviation(b):
                pool.wait_ge(score_var_ready, b + 1)
                pool.tensor_tensor(score_std[:, :], score_var[:, :], half_pow[:, :], ALU.pow).then_inc(score_std_ready, 1)

            def layer_norm(b):
                for half in range(2):
                    t = token_half(half)
                    pool.wait_ge(var_ready, 2 * b + half + 1)
                    pool.tensor_tensor(ln_rstd[:, t], ln_var[:, t], neg_half[:, t], ALU.pow).then_inc(rstd_ready, 1)
                    pool.wait_ge(var2_ready, 2 * b + half + 1)
                    pool.tensor_tensor(ln_rstd2[:, t], ln_var2[:, t], neg_half[:, t], ALU.pow).then_inc(rstd2_ready, 1)
                pool.wait_ge(ln_coef, 2 * b + 2)
                passed(pool)
                for i in range(TILES):
                    pool.tensor_scalar(tu[:, i, :], t1[:, i, :], tu_scale[:, i:i + 1], tu_bias[:, i:i + 1],
                                       ALU.mult, ALU.add).then_inc(tu_ready, 1)

            def gates(b, d):
                for k in range(BLOCKS):
                    g = (b * DIRS + d) * BLOCKS + k
                    tanh_z, z = z_tmp[d][k][:, 0, :], z_tmp[d][k][:, 1, :]
                    out = gate[:, d, k, :]
                    pool.wait_ge(z_acts, 2 * g + 2)
                    pool.wait_ge(expert_added, b * EXPERTS)
                    pool.tensor_tensor(out, tanh_z, z, ALU.mult).then_inc(gate_step, 1)
                    pool.wait_ge(gate_step, g + 1)
                    pool.tensor_tensor(out, out, z, ALU.add).then_inc(gate_ready, 1)

            def dtx_backward(b):
                pool.wait_ge(tu_ready, TILES * (b + 1))
                for k in range(BLOCKS):
                    pool.wait_ge(dt_ready, (b * DIRS + 1) * BLOCKS + k + 1)
                    pool.tensor_tensor(dtx[1][k], dt[1][k], xs[1][k], ALU.mult).then_inc(dtx_b_ready, 1)

            def direction(b, d):
                base = b * UNITS + d * BLOCKS * D_STATE
                base_s = (b * DIRS + d) * D_STATE

                def weigh(s, odd, first=False):
                    for k in range(BLOCKS):
                        pool.wait_ge(scan_ready, base + 2 * s + k + 1)
                        pool.wait_ge(c_copied, base_s + s + 1)
                        pool.wait_ge(y_added, base if first else base + 2 * s + k - 3)
                        pool.tensor_tensor(hc[odd][:, k, :], hs[odd][:, k, :], c_all[:, odd, :],
                                           ALU.mult).then_inc(hc_ready, 1)

                weigh(0, 0, first=d == 0)
                weigh(1, 1, first=d == 0)
                with pool.Fori(1, D_STATE // 2) as r:
                    for odd in range(2):
                        weigh(2 * r + odd, odd)

            def pool_image(b, m=None):
                group_norm(b)
                score_deviation(b)
                if m is not None:
                    expert_norm(m)
                layer_norm(b)
                gates(b, 0)
                gates(b, 1)
                dtx_backward(b)
                for d in range(DIRS):
                    direction(b, d)

            pool_image(0)
            with pool.Fori(1, BATCH) as b:
                pool_image(b, b - 1)
            expert_norm(BATCH - 1)

        @block.scalar
        def _(act):
            def copy(dst, src, **kw):
                return nc.scalar.activation(dst, src, ACT.Copy, **kw)

            act.wait_ge(w_loaded, 16 * (N_LOADS + 2))
            flat = decay[:, :, :, :].rearrange("p d k s -> p (d k s)")
            nc.scalar.activation(flat, flat, ACT.Exp).then_inc(setup_act, 1)
            act.wait_ge(setup_act, 1)
            nc.scalar.mul(flat, flat, -1.0).then_inc(setup_act, 1)
            act.wait_ge(setup_act, 2)
            act.wait_ge(setup_evac, QK_JOB + 1)
            act.wait_ge(setup_scaled, DIRS * BLOCKS + 2)
            act.wait_ge(const_done, CONSTS)

            def inputs(b):
                act.wait_ge(gn_coef, b + 1)
                act.wait_ge(dA_ready, b * UNITS)
                nc.scalar.activation(xn_c[:, :], x_c[:, :], ACT.Identity, bias=gn_bias[:, 0:1],
                                     scale=gn_scale[:, 0:1]).then_inc(xn_ready, 1)
                nc.scalar.activation(xk_c[:, :], x_c[:, :], ACT.Identity, bias=gn_kbias[:, 0:1],
                                     scale=gn_scale[:, 0:1]).then_inc(xn_ready, 1)
                act.wait_ge(qv_ready, 2 * b + 1)
                copy(q_c[:, :], ps67[:, :]).then_inc(qv_copied, 1)

            def values(b):
                act.wait_ge(qv_ready, 2 * b + 2)
                copy(v_tok[:, :, :].rearrange("p a c -> p (a c)"), ps67[:, :]).then_inc(qv_copied, 1)
                act.wait_ge(xtok_t, b + 1)
                copy(x_tok[:, :, :].rearrange("p a c -> p (a c)"), ps45[:, :]).then_inc(xtok_copied, 1)

            def squares(b):
                for i in range(TILES):
                    act.wait_ge(scores_copied, b * TILES + i + 1)
                    act.wait_ge(squares_ready, b * TILES + max(i - 1, 0))
                    nc.scalar.activation(unused_a[:, i % 2, :], score[:, i, :], ACT.Square,
                                         accum_out=sum_sq[:, i:i + 1]).then_inc(squares_ready, 1)

            def expert_norm(m):
                act.wait_ge(ln3_coef, m + 1)
                for i in range(TILES):
                    nc.scalar.activation(en[:, i, :], t2[:, i, :], ACT.Identity, bias=xh_bias[:, i:i + 1],
                                         scale=xh_scale[:, i:i + 1]).then_inc(en_ready, 1)

            def expert_input(m):
                act.wait_ge(en_t, m + 1)
                copy(e_c, ps67[:, :]).then_inc(ec_ready, 1)

            def router_exp(m):
                act.wait_ge(rdiff_ready, m + 1)
                nc.scalar.activation(rexp[:, :, :], rexp[:, :, :], ACT.Exp).then_inc(rexp_ready, 1)

            def router_copies(m):
                act.wait_ge(comb_transposed, 2 * m + 1)
                copy(comb_t, ps45[0:EXPERTS, :]).then_inc(comb_copied, 1)
                act.wait_ge(comb_transposed, 2 * m + 2)
                copy(comb_parts_t[:, :], ps67[0:PARTS * BC, :].bitcast(BF16)[:, 0:N]).then_inc(comb_copied, 1)

            def gelu(m, x):
                n = m * EXPERTS + x
                act.wait_ge(hidden_ready, n + 1)
                act.wait_ge(sel_ready, m * EXPERTS + max(x - 1, 0))
                nc.scalar.activation(act_e[:, x % 2, :], ps[1 + 2 * (x % 2)][:, :], ACT.Gelu,
                                     bias=b1_t[:, x:x + 1]).then_inc(gelu_ready, 1)

            def result(m):
                act.wait_ge(expert_added, (m + 1) * EXPERTS)
                act.wait_ge(out_stored, 16 * m)
                copy(out_c, ps01[:, :]).then_inc(out_copied, 1)

            def count_signs(b, c):
                act.wait_ge(thresh_ready, b * COUNTS + c + 1)
                if c == 0:
                    act.wait_ge(squares_ready, TILES * (b + 1))
                for i in range(ACT_TILES):
                    act.wait_ge(counted, (b * COUNTS + c) * ACT_TILES + max(i - 1, 0))
                    nc.scalar.activation(unused_a[:, i % 2, :], score[:, i, :], ACT.Sign, bias=neg_thresh[:, i:i + 1],
                                         accum_out=count[:, i:i + 1]).then_inc(counted, 1)

            def exponent(b, i):
                act.wait_ge(neg_max_ready, b + 1)
                act.wait_ge(prob_transposed, b * TILES + max(i - 1, 0))
                nc.scalar.activation(expo[:, i % 2, :], score[:, i, :], ACT.Exp,
                                     bias=neg_max[:, i:i + 1]).then_inc(exp_ready, 1)

            def attend(b):
                for i in range(TILES):
                    act.wait_ge(prob_transposed, b * TILES + i + 1)
                    act.wait_ge(attn_ready, b * TILES + max(i - 1, 0))
                    copy(prob_t[:, i % 2, :, :].rearrange("p a c -> p (a c)"), ps[1 + i % 2][:, :]).then_inc(probt_copied, 1)
                    if i + 2 < TILES:
                        exponent(b, i + 2)
                for half in range(2):
                    act.wait_ge(ln_coef, 2 * b + half + 1)
                    for i in range(half * TILES // 2, (half + 1) * TILES // 2):
                        nc.scalar.activation(xh[:, i, :], t1[:, i, :], ACT.Identity, bias=xh_bias[:, i:i + 1],
                                             scale=xh_scale[:, i:i + 1]).then_inc(xh_ready, 1)
                    act.wait_ge(xh_t, 2 * b + half + 1)
                    nc.scalar.activation(halves(mx)[half], halves(ps01)[half], ACT.Identity, bias=beta[:, 0:1],
                                         scale=gamma[:, 0:1]).then_inc(mx_ready, 1)

            def conv_tap(b, d, k):
                act.wait_ge(conv_filled, (b * DIRS + d) * BLOCKS + k + 1)
                act.wait_ge(y_added, b * UNITS)
                nc.scalar.activation(conv_half[d][:, k, :], conv_ps[d][k][:, :], ACT.Identity,
                                     bias=conv_b[:, d, k:k + 1],
                                     scale=conv_w[:, d, k, TAPS - 1:TAPS]).then_inc(tap_ready, 1)

            def conv_tanh(b, d, k):
                act.wait_ge(conv_summed, (b * DIRS + d) * BLOCKS + k + 1)
                act.wait_ge(out_stored, 16 * b)
                nc.scalar.activation(xs[d][k], conv_half[d][:, k, :], ACT.Tanh).then_inc(tanh_ready, 1)

            def z_parts(b, d, k):
                act.wait_ge(z_filled, (b * DIRS + d) * BLOCKS + k + 1)
                act.wait_ge(attn_ready, TILES * (b + 1))
                act.wait_ge(hc_ready, b * UNITS)
                nc.scalar.activation(z_tmp[d][k][:, 0, :], z_ps[d][k][:, :], ACT.Tanh, scale=0.5).then_inc(z_acts, 1)
                copy(z_tmp[d][k][:, 1, :], z_ps[d][k][:, :]).then_inc(z_acts, 1)

            def b_and_c(b, d):
                act.wait_ge(dbc_filled, b * DIRS + d + 1)
                copy(dbc[d], dbc_ps[d][:, :]).then_inc(hi_ready, 1)
                copy(bc_parts[d][:, :], dbc_ps[d][0:PARTS * BC, :]).then_inc(hi_ready, 1)

            def middle_part(b, d):
                act.wait_ge(rest_ready, b * DIRS + d + 1)
                copy(bc_parts[d][BC:2 * BC, :], bc_rest[BC:2 * BC, :]).then_inc(mid_ready, 1)

            def dt_abs(b, d, k):
                g = (b * DIRS + d) * BLOCKS + k
                act.wait_ge(dt_filled, g + 1)
                act.wait_ge(xs_ready, g + 1)
                nc.scalar.activation(soft_log[d][:, k, :], dt_ps[d][k][:, :], ACT.Abs,
                                     bias=dt_b[:, d, k:k + 1]).then_inc(abs_ready, 1)

            def dt_log(b, d, k):
                g = (b * DIRS + d) * BLOCKS + k
                log = soft_log[d][:, k, :]
                act.wait_ge(abs_ready, g + 1)
                nc.scalar.activation(log, log, ACT.Exp, scale=-1.0).then_inc(astep, 1)
                act.wait_ge(astep, g + 1)
                nc.scalar.activation(log, log, ACT.Ln, bias=1.0).then_inc(log_ready, 1)

            def prepare(b):
                conv_tap(b, 0, 0)
                conv_tap(b, 0, 1)
                z_parts(b, 0, 0)
                conv_tanh(b, 0, 0)
                z_parts(b, 0, 1)
                conv_tap(b, 1, 0)
                conv_tanh(b, 0, 1)
                conv_tap(b, 1, 1)
                z_parts(b, 1, 0)
                b_and_c(b, 0)
                dt_abs(b, 0, 0)
                conv_tanh(b, 1, 0)
                middle_part(b, 0)
                dt_abs(b, 0, 1)
                z_parts(b, 1, 1)
                conv_tanh(b, 1, 1)
                dt_log(b, 0, 0)
                b_and_c(b, 1)
                dt_log(b, 0, 1)
                dt_abs(b, 1, 0)
                middle_part(b, 1)
                dt_abs(b, 1, 1)
                dt_log(b, 1, 0)
                dt_log(b, 1, 1)

            def direction(b, d):
                e = b * DIRS + d
                base = b * UNITS + d * BLOCKS * D_STATE
                base_s = e * D_STATE

                def decay_and_c(s, odd, first=False):
                    for k in range(BLOCKS):
                        if first:
                            act.wait_ge(dt_ready, e * BLOCKS + k + 1)
                        act.wait_ge(scan_ready, base if first and d == 0 else base + 2 * s + k - 1)
                        nc.scalar.activation(dA[:, k, :], dt[d][k], ACT.Exp,
                                             scale=decay[:, d, k, ds(s, 1)]).then_inc(dA_ready, 1)
                        if k == 0:
                            act.wait_ge(c_ready, base_s + s + 1)
                            act.wait_ge(hc_ready, base if first and d == 0 else base + 2 * s - 2)
                            copy(c_all[:, odd, :], ps67[:, :]).then_inc(c_copied, 1)

                if d == 0:
                    act.wait_ge(gate_ready, (b * DIRS + 1) * BLOCKS + 1)
                decay_and_c(0, 0, first=True)
                decay_and_c(1, 1)
                with act.Fori(1, D_STATE // 2) as r:
                    for odd in range(2):
                        decay_and_c(2 * r + odd, odd)

            def act_image(b, m=None):
                inputs(b)
                squares(b)
                values(b)
                for c in range(COUNTS):
                    if m is not None and c == COUNTS - 2:
                        expert_norm(m)
                    count_signs(b, c)
                    if m is not None and c == COUNTS - 2:
                        expert_input(m)
                if m is not None:
                    router_exp(m)
                    router_copies(m)
                    for x in range(EXPERTS):
                        gelu(m, x)
                exponent(b, 0)
                exponent(b, 1)
                if m is not None:
                    result(m)
                attend(b)
                prepare(b)
                for d in range(DIRS):
                    direction(b, d)

            act_image(0)
            with act.Fori(1, BATCH) as b:
                act_image(b, b - 1)
            expert_norm(BATCH - 1)
            expert_input(BATCH - 1)
            router_exp(BATCH - 1)
            router_copies(BATCH - 1)
            for x in range(EXPERTS):
                gelu(BATCH - 1, x)
            result(BATCH - 1)

        @block.vector
        def _(dve):
            v = nc.vector
            dve.wait_ge(w_loaded, 16 * (N_LOADS + 2))
            dve.wait_ge(const_done, CONSTS)
            for n, (src, dst, factor) in enumerate(jobs):
                dve.wait_ge(setup_t, n + 1)
                v.tensor_scalar(dst, ps[n % 4][:, 0:dst.shape[1]], factor, None, ALU.mult).then_inc(setup_evac, 1)
            dve.wait_ge(setup_t, QK_JOB + 1)
            v.tensor_scalar(qk_w[:, :], ps[QK_JOB % 4][:, 0:P], float(C) ** -0.5, None, ALU.mult).then_inc(setup_evac, 1)
            dve.wait_ge(setup_evac, QK_JOB + 1)
            for d in range(DIRS):
                for k in range(BLOCKS):
                    v.tensor_scalar(skip_diag[:, d, k, :], ident[:, :], skip[:, d, k:k + 1], None,
                                    ALU.mult).then_inc(setup_scaled, 1)
            v.tensor_scalar(vec[:, 0:DIRS * BLOCKS], vec[:, 0:DIRS * BLOCKS], 0.5, None,
                            ALU.mult).then_inc(setup_scaled, 1)
            flat_w = conv_w[:, :, :, :].rearrange("p d k j -> p (d k j)")
            v.tensor_scalar(flat_w, flat_w, 0.5, None, ALU.mult).then_inc(setup_scaled, 1)

            begin, end, step, after, link, steps_now = step_counter(
                dve, vstep, 9 + 2 * COUNTS + COUNTS * (TILES - ACT_TILES) + 8 * TILES)
            begin_tail, end_tail, step_tail, after_tail, link_tail, _ = step_counter(dve, tstep, 13 + 2 * TILES)
            mean, var = ln_mv[:, :, 0], ln_mv[:, :, 1]

            def group_norm(b):
                dve.wait_ge(x_loaded, 16 * (b + 1))
                for h, part in enumerate(halves(x_c)):
                    step(v.bn_stats(gn_stats[:, h, :], part))
                after(0)
                link(v.bn_aggr(gn_mv[:, :], gn_stats[:, :, :].rearrange("p a s -> p (a s)")))
                dve.sem_inc(gn_dev_ready, 1)
                dve.wait_ge(gn_mean_ready, 2 * b + 1)
                link(v.tensor_copy(gn_mean[:, :], ps23[:, 0:1]))
                link(v.tensor_tensor(gn_dev[:, :], gn_mv[:, 0:1], gn_mean[:, :], ALU.subtract))
                v.scalar_tensor_tensor(gn_sq[:, :], gn_dev[:, :], gn_dev[:, 0:1], gn_mv[:, 1:2], ALU.mult,
                                       ALU.add).then_inc(gn_sq_ready, 1)
                dve.wait_ge(gn_mean_ready, 2 * b + 2)
                v.tensor_scalar(gn_var[:, :], ps23[:, 0:1], 1e-5, None, ALU.add).then_inc(gn_sq_ready, 1)
                dve.wait_ge(gn_pow, b + 1)
                v.scalar_tensor_tensor(gn_kbias[:, :], gn_mv[:, 0:1], -1.0, gn_scale[:, :], ALU.mult, ALU.mult)
                v.scalar_tensor_tensor(gn_bias[:, :], gn_mean[:, :], -1.0, gn_scale[:, :], ALU.mult,
                                       ALU.mult).then_inc(gn_coef, 1)

            def take_scores(b):
                dve.wait_ge(y_added, b * UNITS)
                for i in range(TILES):
                    dve.wait_ge(scores_ready, b * TILES + i + 1)
                    v.tensor_scalar(score[:, i, :], ps[(i + 1) % 2][:, :], 0.0, None, ALU.add, ALU.max,
                                    accum_out=row_max[:, i:i + 1]).then_inc(scores_copied, 1)
                dve.wait_ge(scores_copied, TILES * (b + 1))
                v.tensor_scalar(neg_max[:, :], row_max[:, :], -1.0, None, ALU.mult).then_inc(neg_max_ready, 1)

            by_sign, by_count = slice(0, ACT_TILES), slice(ACT_TILES, TILES)

            def score_variance(b):
                dve.wait_ge(squares_ready, TILES * (b + 1))
                v.tensor_scalar(score_var[:, :], sum_sq[:, :], 1.0 / N, None, ALU.mult).then_inc(score_var_ready, 1)

            def first_thresholds(b):
                dve.wait_ge(score_std_ready, b + 1)
                v.tensor_scalar(correction[:, by_sign], score_std[:, by_sign], STEP / 2, None, ALU.mult)
                v.tensor_scalar(correction[:, by_count], score_std[:, by_count], STEP, None, ALU.mult)
                v.tensor_scalar(neg_thresh[:, :], score_std[:, :], -Z0, None, ALU.mult).then_inc(thresh_ready, 1)
                link(v.tensor_scalar(thresh[:, :], score_std[:, :], Z0, None, ALU.mult))

            def count_above():
                for i in range(ACT_TILES, TILES):
                    after()
                    step(v.tensor_scalar(unused_v[:, i % 2, :], score[:, i, :], thresh[:, i:i + 1], None,
                                         ALU.is_ge, ALU.add, accum_out=count[:, i:i + 1]))

            def correct(b, c):
                after(0)
                dve.wait_ge(counted, (b * COUNTS + c + 1) * ACT_TILES)
                v.scalar_tensor_tensor(delta[:, by_sign], count[:, by_sign], N - 2 * TARGET,
                                       correction[:, by_sign], ALU.add, ALU.mult)
                link(v.scalar_tensor_tensor(delta[:, by_count], count[:, by_count], -TARGET,
                                              correction[:, by_count], ALU.add, ALU.mult))
                v.scalar_tensor_tensor(neg_thresh[:, :], delta[:, :], -DAMPING[c], neg_thresh[:, :],
                                       ALU.mult, ALU.add).then_inc(thresh_ready, 1)
                link(v.scalar_tensor_tensor(thresh[:, :], delta[:, :], DAMPING[c], thresh[:, :],
                                              ALU.mult, ALU.add))

            def ranks(b):
                after(0)
                dve.wait_ge(counted, (b + 1) * COUNTS * ACT_TILES)
                v.tensor_scalar(rank[:, by_sign], count[:, by_sign], -0.5, KEEP - N / 2, ALU.mult, ALU.add)
                v.tensor_scalar(rank[:, by_count], count[:, by_count], -1.0, float(KEEP), ALU.mult, ALU.add)
                link(v.tensor_copy(ladder[:, :, 0], thresh[:, :]))

            def first_below(pair):
                for j in pair:
                    after()
                    step(v.scalar_tensor_tensor(work[:, j % 2, :], score[:, j, :], thresh[:, j:j + 1],
                                                score[:, j, :], ALU.is_lt, ALU.mult))
                for j in pair:
                    after()
                    step(v.max(ladder[:, j, 1:9], work[:, j % 2, :]))

            def next_below(pair):
                for j in pair:
                    after()
                    step(v.match_replace(work[:, j % 2, :], ladder[:, j, 1:9], work[:, j % 2, :], REPLACED))
                for j in pair:
                    after()
                    step(v.max(ladder[:, j, 9:17], work[:, j % 2, :]))

            def resolve(b):
                after(0)
                rank_b = rank[:, :].unsqueeze(2).to_broadcast([P, TILES, WINDOW])
                link(v.tensor_tensor(hit[:, :, :], rungs[:, :, :], rank_b, ALU.is_equal))
                v.tensor_tensor(at_rank[:, :, :], hit[:, :, :], ladder[:, :, 0:WINDOW], ALU.mult)
                link(v.tensor_tensor(after_rank[:, :, :], hit[:, :, :], ladder[:, :, 1:WINDOW + 1], ALU.mult))
                v.reduce_sum(kept_from[:, :], at_rank[:, :, :], axis=mybir.AxisListType.X)
                link(v.reduce_sum(one_less[:, :], after_rank[:, :, :], axis=mybir.AxisListType.X))
                link(v.tensor_tensor(found[:, :], kept_from[:, :], one_less[:, :], ALU.is_gt))
                link(v.scalar_tensor_tensor(found[:, :], kept_from[:, :], 0.0, found[:, :], ALU.is_gt, ALU.mult))
                v.tensor_scalar(missed[:, :], found[:, :], -1.0, 1.0, ALU.mult, ALU.add).then_inc(missed_ready, 1)

            def read_missed(b):
                dve.wait_ge(missed_summed, b + 1)
                v.tensor_copy(missed_tiles[:, 0:TILES], ps45[0:1, 0:TILES])
                link(v.reduce_sum(missed_tiles[:, TILES:TILES + 1], ps45[0:1, 0:TILES], axis=mybir.AxisListType.X))
                dve.sem_inc(missed_read, 1)
                return dve.value_load(missed_bits[0:1, TILES:TILES + 1])

            def exact(i):
                dve.sem_clear(exact_step)
                v.tensor_copy(work[:, 0, :], score[:, i, :]).then_inc(exact_step, 1)
                with dve.Fori(0, FULL_ROUNDS) as r:
                    dve.wait_ge(exact_step, 2 * r + 1)
                    passed(dve)
                    v.max(top8[:, :], work[:, 0, :]).then_inc(exact_step, 1)
                    dve.wait_ge(exact_step, 2 * r + 2)
                    passed(dve)
                    v.match_replace(work[:, 0, :], top8[:, :], work[:, 0, :], REPLACED).then_inc(exact_step, 1)
                done = 2 * FULL_ROUNDS + 1
                dve.wait_ge(exact_step, done)
                v.max(top8[:, :], work[:, 0, :]).then_inc(exact_step, 1)
                dve.wait_ge(exact_step, done + 1)
                v.memset(top8[:, LAST_ROUND:8], REPLACED).then_inc(exact_step, 1)
                dve.wait_ge(exact_step, done + 2)
                v.match_replace(work[:, 0, :], top8[:, :], work[:, 0, :], REPLACED).then_inc(exact_step, 1)
                dve.wait_ge(exact_step, done + 3)
                v.tensor_scalar(score[:, i, :], work[:, 0, :], REPLACED, 0.5, ALU.is_equal,
                                ALU.subtract).then_inc(exact_step, 1)
                v.memset(kept_from[:, i:i + 1], 0.0).then_inc(exact_step, 1)
                dve.wait_ge(exact_step, done + 5)

            def probabilities(b, i, some_missed):
                dve.wait_ge(exp_ready, b * TILES + i + 1)
                if some_missed:
                    passed(dve)
                    rows_missed = dve.value_load(missed_bits[0:1, i:i + 1])
                    with dve.If(rows_missed != 0):
                        after(0)
                        exact(i)
                v.scalar_tensor_tensor(expo[:, i % 2, :], score[:, i, :], kept_from[:, i:i + 1],
                                       expo[:, i % 2, :], ALU.is_ge, ALU.mult,
                                       accum_out=row_sum[:, i:i + 1]).then_inc(prob_ready, 1)

            def invert_sum(b, i):
                dve.wait_ge(prob_ready, b * TILES + i + 1)
                step(v.reciprocal(row_inv[:, i:i + 1], row_sum[:, i:i + 1]))

            def attended(b, i):
                after()
                dve.wait_ge(attn_ready, b * TILES + i + 1)
                at = i % 2 * BANK
                v.scalar_tensor_tensor(t1[:, i, :], ps67[:, at:at + P], row_inv[:, i:i + 1],
                                       x_tok[:, i, :], ALU.mult, ALU.add).then_inc(t1_ready, 1)
                dve.wait_ge(t1_ready, b * TILES + i + 1)
                step(v.bn_stats(ln_stats[:, i, :], t1[:, i, :]))

            def aggregate(half):
                after(0)
                for i in range(half * TILES // 2, (half + 1) * TILES // 2):
                    step(v.bn_aggr(ln_mv[:, i, :], ln_stats[:, i, :]))
                after(0)

            def norm_variance(b, half):
                t = token_half(half)
                v.tensor_scalar(ln_var[:, t], ln_mv[:, t, 1], LN_EPS, None, ALU.add).then_inc(var_ready, 1)

            def norm_variance_again(b, half):
                t = token_half(half)
                dve.wait_ge(rstd_ready, 2 * b + half + 1)
                link(v.tensor_tensor(ln_var2[:, t], ln_mv[:, t, 1], ln_rstd[:, t], ALU.mult))
                link(v.tensor_tensor(ln_var2[:, t], ln_var2[:, t], ln_rstd[:, t], ALU.mult))
                v.tensor_scalar(ln_var2[:, t], ln_var2[:, t], LN_EPS, None, ALU.add).then_inc(var2_ready, 1)
                v.tensor_scalar(tu_scale[:, t], ln_rstd[:, t], 1.0, None, ALU.add)
                v.scalar_tensor_tensor(tu_bias[:, t], ln_mv[:, t, 0], -1.0, ln_rstd[:, t], ALU.mult, ALU.mult)

            def norm_coefficients(b, half):
                t = token_half(half)
                dve.wait_ge(rstd2_ready, 2 * b + half + 1)
                link(v.tensor_tensor(xh_scale[:, t], ln_rstd[:, t], ln_rstd2[:, t], ALU.mult))
                v.scalar_tensor_tensor(xh_bias[:, t], ln_mv[:, t, 0], -1.0, xh_scale[:, t], ALU.mult,
                                       ALU.mult).then_inc(ln_coef, 1)

            def convolve(b, d, k, taps=range(1, TAPS)):
                g = (b * DIRS + d) * BLOCKS + k
                dve.wait_ge(tap_ready, g + 1)
                half = conv_half[d]
                for n in taps:
                    if n > 1:
                        dve.wait_ge(conv_step, (TAPS - 2) * g + n - 1)
                    near, far = slice(n, N), slice(0, N - n)
                    to, src = (near, far) if d == 0 else (far, near)
                    v.scalar_tensor_tensor(half[:, k, to], conv_ps[d][k][:, src],
                                           conv_w[:, d, k, TAPS - 1 - n:TAPS - n], half[:, k, to], ALU.mult,
                                           ALU.add).then_inc(conv_step if n < TAPS - 1 else conv_summed, 1)

            def silu(b, d, k):
                dve.wait_ge(tanh_ready, (b * DIRS + d) * BLOCKS + k + 1)
                v.scalar_tensor_tensor(xs[d][k], xs[d][k], 1.0, conv_half[d][:, k, :], ALU.add,
                                       ALU.mult).then_inc(xs_ready, 1)

            def rest(b, d):
                e = b * DIRS + d
                dve.wait_ge(hi_ready, 2 * e + 2)
                dve.wait_ge(mid_ready, e)
                dve.wait_ge(parts_ready, e)
                v.tensor_tensor(bc_rest[:, :], dbc[d][0:PARTS * BC, :], bc_parts[d][:, :],
                                ALU.subtract).then_inc(rest_ready, 1)

            def last_part(b, d):
                e = b * DIRS + d
                rows = slice(2 * BC, 3 * BC)
                dve.wait_ge(rest_ready, e + 1)
                v.tensor_copy(bc_mid[rows, :], bc_rest[rows, :]).then_inc(mid_step, 1)
                dve.wait_ge(mid_step, e + 1)
                v.tensor_tensor(bc_parts[d][rows, :], bc_rest[rows, :], bc_mid[rows, :],
                                ALU.subtract).then_inc(parts_ready, 1)

            def dt_positive(b, d, k):
                dve.wait_ge(abs_ready, (b * DIRS + d) * BLOCKS + k + 1)
                dve.wait_ge(dA_ready, b * UNITS)
                v.tensor_scalar(dt[d][k], dt_ps[d][k][:, :], dt_b[:, d, k:k + 1], 0.0, ALU.add,
                                ALU.max).then_inc(relu_ready, 1)

            def dt_sum(b, d, k):
                g = (b * DIRS + d) * BLOCKS + k
                dve.wait_ge(relu_ready, g + 1)
                dve.wait_ge(log_ready, g + 1)
                v.tensor_tensor(dt[d][k], dt[d][k], soft_log[d][:, k, :], ALU.add).then_inc(dt_ready, 1)

            def dtx_forward(b, k):
                dve.wait_ge(dt_ready, b * DIRS * BLOCKS + k + 1)
                v.tensor_tensor(dtx[0][k], dt[0][k], xs[0][k], ALU.mult).then_inc(dtx_ready, 1)

            def products(b, d, s, first=False):
                base = b * UNITS + d * BLOCKS * D_STATE
                for k in range(BLOCKS):
                    dve.wait_ge(b_ready, (b * DIRS + d) * D_STATE + s + 1)
                    dve.wait_ge(scan_ready, base if first and d == 0 else base + 2 * s + k - 1)
                    if first:
                        dve.wait_ge((dtx_ready, dtx_b_ready)[d], b * BLOCKS + k + 1)
                    v.tensor_tensor(dbu[k][:, :], dtx[d][k], ps23[:, :], ALU.mult).then_inc(dbu_ready, 1)

            def scans(b, d, s, odd, first=False):
                base = b * UNITS + d * BLOCKS * D_STATE
                order = slice(None) if d == 0 else slice(None, None, -1)
                for k in range(BLOCKS):
                    dve.wait_ge(dA_ready, base + 2 * s + k + 1)
                    dve.wait_ge(dbu_ready, base + 2 * s + k + 1)
                    dve.wait_ge(hc_ready, base if first else base + 2 * s + k - 3)
                    v.tensor_tensor_scan(hs[odd][:, k, order], dA[:, k, order], dbu[k][:, order], 0.0,
                                         ALU.mult, ALU.add).then_inc(scan_ready, 1)

            def apply_gate(b, d, k):
                g = (b * DIRS + d) * BLOCKS + k
                dve.wait_ge(y_ready, g + 1)
                dve.wait_ge(gate_ready, g + 1)
                v.tensor_tensor(gate[:, d, k, :], gate[:, d, k, :], ps[2 * k][:, :], ALU.mult).then_inc(gated, 1)

            def later_states(b, d):
                with dve.Fori(1, D_STATE // 2) as r:
                    for odd in range(2):
                        products(b, d, 2 * r + odd)
                        scans(b, d, 2 * r + odd, odd)

            def mamba(b):
                convolve(b, 0, 0)
                convolve(b, 0, 1, range(1, 2))
                silu(b, 0, 0)
                convolve(b, 0, 1, range(2, TAPS))
                silu(b, 0, 1)
                convolve(b, 1, 0)
                rest(b, 0)
                convolve(b, 1, 1)
                last_part(b, 0)
                dt_positive(b, 0, 0)
                silu(b, 1, 0)
                dt_positive(b, 0, 1)
                silu(b, 1, 1)
                dt_sum(b, 0, 0)
                dtx_forward(b, 0)
                rest(b, 1)
                dt_sum(b, 0, 1)
                dtx_forward(b, 1)
                last_part(b, 1)
                dt_positive(b, 1, 0)
                dt_positive(b, 1, 1)
                products(b, 0, 0, first=True)
                dt_sum(b, 1, 0)
                dt_sum(b, 1, 1)
                dve.wait_ge(gate_ready, DIRS * BLOCKS * (b + 1))
                scans(b, 0, 0, 0, first=True)
                products(b, 0, 1)
                scans(b, 0, 1, 1, first=True)
                later_states(b, 0)
                products(b, 1, 0, first=True)
                scans(b, 1, 0, 0)
                products(b, 1, 1)
                apply_gate(b, 0, 0)
                apply_gate(b, 0, 1)
                scans(b, 1, 1, 1)
                later_states(b, 1)

            def tokens_out(m):
                dve.wait_ge(mamba_out, m + 1)
                dve.wait_ge(tu_ready, TILES * (m + 1))
                link_tail(v.tensor_tensor(t2[:, :, :].rearrange("p a c -> p (a c)"),
                                          tu[:, :, :].rearrange("p a c -> p (a c)"), ps67[:, :], ALU.add))
                dve.sem_inc(t2_ready, 1)
                for i in range(TILES):
                    step_tail(v.bn_stats(ln_stats[:, i, :], t2[:, i, :]))
                after_tail(0)
                for i in range(TILES):
                    step_tail(v.bn_aggr(ln_mv[:, i, :], ln_stats[:, i, :]))
                after_tail(0)
                v.tensor_scalar(ln_var[:, :], var, LN_EPS, None, ALU.add).then_inc(var3_ready, 1)

            def expert_norm(m):
                dve.wait_ge(rstd3_ready, m + 1)
                dve.wait_ge(xh_ready, TILES * (m + 1))
                link_tail(v.tensor_copy(xh_scale[:, :], ln_rstd[:, :]))
                v.scalar_tensor_tensor(xh_bias[:, :], mean, -1.0, ln_rstd[:, :], ALU.mult,
                                       ALU.mult).then_inc(ln3_coef, 1)

            def router_logits(m):
                dve.wait_ge(logits_ready, m + 1)
                link_tail(v.tensor_copy(logits[:, :, 0:EXPERTS],
                                     ps45[:, 0:TILES * EXPERTS].rearrange("p (a e) -> p a e", e=EXPERTS)))
                for i in range(TILES):
                    last = v.max(r8[:, i, :], logits[:, i, :])
                link_tail(last)
                v.tensor_tensor(rexp[:, :, :], logits[:, :, 0:EXPERTS],
                                r8[:, :, 0:1].to_broadcast([P, TILES, EXPERTS]), ALU.subtract).then_inc(rdiff_ready, 1)

            def router_weights(m):
                dve.wait_ge(rdiff_ready, m + 1)
                link_tail(v.memset(r8[:, :, 2:8], REPLACED))
                for i in range(TILES):
                    last = v.match_replace(marked[:, i, :], r8[:, i, :], logits[:, i, :], CHOSEN)
                link_tail(last)
                dve.wait_ge(rexp_ready, m + 1)
                link_tail(v.scalar_tensor_tensor(comb[:, :, :], marked[:, :, 0:EXPERTS], CHOSEN, rexp[:, :, :],
                                              ALU.is_equal, ALU.mult))
                link_tail(v.reduce_sum(rsum[:, :], comb[:, :, :], axis=mybir.AxisListType.X))
                link_tail(v.reciprocal(rsum[:, :], rsum[:, :]))
                link_tail(v.tensor_tensor(comb[:, :, :], comb[:, :, :],
                                       rsum[:, :].unsqueeze(2).to_broadcast([P, TILES, EXPERTS]), ALU.mult))
                part = [comb_parts[:, :, i * BC:i * BC + EXPERTS] for i in range(PARTS)]
                link_tail(v.tensor_copy(part[0], comb[:, :, :]))
                link_tail(v.tensor_tensor(comb_rest[:, :, :], comb[:, :, :], part[0], ALU.subtract))
                link_tail(v.tensor_copy(part[1], comb_rest[:, :, :]))
                v.tensor_tensor(part[2], comb_rest[:, :, :], part[1], ALU.subtract).then_inc(comb_ready, 1)

            def select(m, x):
                n = m * EXPERTS + x
                dve.wait_ge(weight_ready, n + 1)
                dve.wait_ge(gelu_ready, n + 1)
                dve.wait_ge(expert_added, m * EXPERTS + max(x - 1, 0))
                v.tensor_tensor(sel_e[:, x % 2, :], act_e[:, x % 2, :], ps45[:, :], ALU.mult).then_inc(sel_ready, 1)

            def attention_out(b, some_missed):
                probabilities(b, 0, some_missed)
                probabilities(b, 1, some_missed)
                invert_sum(b, 0)
                for i in range(2, TILES):
                    probabilities(b, i, some_missed)
                    invert_sum(b, i - 1)
                    attended(b, i - 2)
                    if i == 5:
                        aggregate(0)
                        norm_variance(b, 0)
                    elif i == 6:
                        norm_variance_again(b, 0)
                invert_sum(b, TILES - 1)
                norm_coefficients(b, 0)
                attended(b, TILES - 2)
                attended(b, TILES - 1)
                aggregate(1)
                norm_variance(b, 1)
                norm_variance_again(b, 1)
                norm_coefficients(b, 1)

            def mamba_end(m):
                apply_gate(m, 1, 0)
                apply_gate(m, 1, 1)

            def dve_image(b, m=None):
                begin(b)
                group_norm(b)
                if m is not None:
                    mamba_end(m)
                    begin_tail(m)
                take_scores(b)
                score_variance(b)
                first_thresholds(b)
                count_above()
                correct(b, 0)
                if m is not None:
                    tokens_out(m)
                count_above()
                if m is not None:
                    expert_norm(m)
                correct(b, 1)
                count_above()
                correct(b, 2)
                count_above()
                ranks(b)
                if m is not None:
                    router_logits(m)
                    router_weights(m)
                    end_tail()
                for j in range(0, TILES, 2):
                    first_below((j, j + 1))
                    if m is not None:
                        select(m, j)
                    next_below((j, j + 1))
                    if m is not None:
                        select(m, j + 1)
                resolve(b)
                any_missed = read_missed(b)
                counted_steps = steps_now()
                with dve.If(any_missed != 0):
                    attention_out(b, some_missed=True)
                steps_now(counted_steps)
                with dve.If(any_missed == 0):
                    attention_out(b, some_missed=False)
                end()
                mamba(b)

            dve_image(0)
            with dve.Fori(1, BATCH) as b:
                dve_image(b, b - 1)
            mamba_end(BATCH - 1)
            begin_tail(BATCH - 1)
            tokens_out(BATCH - 1)
            expert_norm(BATCH - 1)
            router_logits(BATCH - 1)
            router_weights(BATCH - 1)
            for x in range(EXPERTS):
                select(BATCH - 1, x)
            end_tail()

        @block.tensor
        def _(pe):
            mm, tr = nc.tensor.matmul, nc.tensor.transpose
            pe.wait_ge(w_loaded, 16 * (N_LOADS + 2))
            pe.wait_ge(const_done, CONSTS)
            for n, (src, dst, _) in enumerate(jobs):
                if n >= 4:
                    pe.wait_ge(setup_evac, n - 3)
                k = src.shape[0]
                tr(ps[n % 4][:, 0:k], src, ident[0:k, 0:k]).then_inc(setup_t, 1)
            pe.wait_ge(setup_evac, QK_JOB - 3)
            mm(ps[QK_JOB % 4][:, 0:P], raw_qkv[:, 0, :], raw_qkv[:, 1, :], start=True, stop=True).then_inc(setup_t, 1)
            pe.wait_ge(setup_evac, QK_JOB + 1)
            pe.wait_ge(setup_scaled, DIRS * BLOCKS + 2)
            pe.wait_ge(setup_act, 2)

            def group_norm(b):
                pe.wait_ge(dbu_ready, b * UNITS)
                pe.wait_ge(gn_dev_ready, b + 1)
                mm(ps23[:, 0:1], group_avg[:, :], gn_mv[:, 0:1], start=True, stop=True).then_inc(gn_mean_ready, 1)
                pe.wait_ge(gn_sq_ready, 2 * b + 1)
                mm(ps23[:, 0:1], group_avg[:, :], gn_sq[:, :], start=True, stop=True).then_inc(gn_mean_ready, 1)

            def queries(b):
                pe.wait_ge(xn_ready, 2 * b + 1)
                pe.wait_ge(c_copied, DIRS * D_STATE * b)
                for h in range(HALVES):
                    last = mm(halves(ps67)[h], qk_w[:, :], halves(xn_c)[h], start=True, stop=True)
                last.then_inc(qv_ready, 1)

            def transpose_input(b):
                pe.wait_ge(x_loaded, 16 * (b + 1))
                pe.wait_ge(gated, DIRS * BLOCKS * b)
                for i in range(TILES):
                    last = tr(ps45[:, i * P:(i + 1) * P], x_c[:, i * P:(i + 1) * P], ident[:, :])
                last.then_inc(xtok_t, 1)

            def values(b):
                pe.wait_ge(qv_copied, 2 * b + 1)
                for i in range(TILES):
                    last = mm(ps67[:, i * P:(i + 1) * P], xn_c[:, i * P:(i + 1) * P], wv_t[:, :],
                              start=True, stop=True)
                last.then_inc(qv_ready, 1)

            def scores(b, i):
                if i == 0:
                    pe.wait_ge(qv_copied, 2 * b + 1)
                    pe.wait_ge(xn_ready, 2 * b + 2)
                    pe.wait_ge(gn_sq_ready, 2 * b + 2)
                if i == 1:
                    pe.wait_ge(gated, DIRS * BLOCKS * b)
                if i >= 2:
                    pe.wait_ge(scores_copied, b * TILES + i - 1)
                for h in range(HALVES):
                    last = mm(halves(ps[(i + 1) % 2])[h], q_c[:, i * P:(i + 1) * P], halves(xk_c)[h],
                              start=True, stop=True)
                last.then_inc(scores_ready, 1)

            def sum_missed(b):
                pe.wait_ge(xtok_copied, b + 1)
                pe.wait_ge(missed_ready, b + 1)
                mm(ps45[0:1, 0:TILES], ones[:, :], missed[:, :], start=True, stop=True).then_inc(missed_summed, 1)

            def transpose_prob(b, i):
                pe.wait_ge(prob_ready, b * TILES + i + 1)
                pe.wait_ge(probt_copied, b * TILES + max(i - 1, 0))
                pe.wait_ge(missed_read, b + 1)
                for j in range(TILES):
                    last = tr(ps[1 + i % 2][:, j * P:(j + 1) * P], expo[:, i % 2, j * P:(j + 1) * P], ident[:, :])
                last.then_inc(prob_transposed, 1)

            def attend(b, i):
                pe.wait_ge(probt_copied, b * TILES + i + 1)
                pe.wait_ge(t1_ready, b * TILES + max(i - 1, 0))
                at = i % 2 * BANK
                for j in range(TILES):
                    last = mm(ps67[:, at:at + P], prob_t[:, i % 2, j, :], v_tok[:, j, :], start=j == 0,
                              stop=j == TILES - 1)
                last.then_inc(attn_ready, 1)

            def mamba_input(b):
                pe.wait_ge(out_copied, b)
                pe.wait_ge(probt_copied, TILES * (b + 1))
                for half in range(2):
                    pe.wait_ge(xh_ready, TILES * b + (half + 1) * TILES // 2)
                    for i in range(half * TILES // 2, (half + 1) * TILES // 2):
                        last = tr(ps01[:, i * P:(i + 1) * P], xh[:, i, :], ident[:, :])
                    last.then_inc(xh_t, 1)
                    pe.wait_ge(mx_ready, 2 * b + half + 1)
                    for k in range(BLOCKS):
                        if half == 0 and k == 1:
                            pe.wait_ge(t1_ready, TILES * (b + 1))
                        last = mm(halves(conv_ps[0][k])[half], x_in_t[:, 0, k, :], halves(mx)[half],
                                  start=True, stop=True)
                        if half == 1:
                            last.then_inc(conv_filled, 1)

            def project_x_backward(b, k):
                pe.wait_ge(z_acts, 2 * (b * DIRS * BLOCKS + k) + 2)
                for h in range(HALVES):
                    last = mm(halves(conv_ps[1][k])[h], x_in_t[:, 1, k, :], halves(mx)[h], start=True, stop=True)
                last.then_inc(conv_filled, 1)

            def project_z(b, d, k):
                if d:
                    pe.wait_ge(conv_summed, b * DIRS * BLOCKS + 2 + k)
                for h in range(HALVES):
                    last = mm(halves(z_ps[d][k])[h], z_in_t[:, d, k, :], halves(mx)[h], start=True, stop=True)
                last.then_inc(z_filled, 1)

            def project_dbc(b, d, k):
                e = b * DIRS + d
                if k == 0:
                    pe.wait_ge(conv_summed, e * BLOCKS + 1 + d)
                pe.wait_ge(xs_ready, e * BLOCKS + k + 1)
                for h in range(HALVES):
                    last = mm(halves(dbc_ps[d])[h], xproj_t[:, d, k, :], xs[d][k][:, h * BANK:(h + 1) * BANK],
                              start=k == 0, stop=k == BLOCKS - 1)
                if k == BLOCKS - 1:
                    last.then_inc(dbc_filled, 1)

            def project_dt(b, d, k):
                e = b * DIRS + d
                if k == 0:
                    pe.wait_ge(hi_ready, 2 * e + 1)
                    pe.wait_ge(z_acts, 2 * (b * DIRS * BLOCKS + 3 + d))
                else:
                    pe.wait_ge(hi_ready, 2 * e + 2)
                rows = slice(PARTS * BC, PARTS * BC + DT_RANK)
                for h in range(HALVES):
                    last = mm(halves(dt_ps[d][k])[h], dtproj_t[rows, d, k, :], dbc[d][rows, h * BANK:(h + 1) * BANK],
                              start=True, stop=True)
                last.then_inc(dt_filled, 1)

            def skip_term(d, k):
                for h in range(HALVES):
                    mm(halves(ps[2 * k])[h], skip_diag[:, d, k, :], xs[d][k][:, h * BANK:(h + 1) * BANK],
                       start=True, stop=False)

            def spread(b, d, s):
                pe.wait_ge(dbu_ready, b * UNITS + d * BLOCKS * D_STATE + 2 * s)
                for h in range(HALVES):
                    last = mm(halves(ps23)[h], pick[:, ds(s, 1), :].rearrange("p o m -> p (o m)"),
                              bc_parts[d][:, h * BANK:(h + 1) * BANK], start=True, stop=True)
                last.then_inc(b_ready, 1)
                pe.wait_ge(c_copied, (b * DIRS + d) * D_STATE + s)
                for h in range(HALVES):
                    last = mm(halves(ps67)[h], pick[:, ds(s + D_STATE, 1), :].rearrange("p o m -> p (o m)"),
                              bc_parts[d][:, h * BANK:(h + 1) * BANK], start=True, stop=True)
                last.then_inc(c_ready, 1)

            def add(b, d, s, odd, stop=False):
                for k in range(BLOCKS):
                    unit = b * UNITS + d * BLOCKS * D_STATE + 2 * s + k
                    pe.wait_ge(hc_ready, unit + 1)
                    for h in range(HALVES):
                        last = mm(halves(ps[2 * k])[h], ident[:, :], hc[odd][:, k, h * BANK:(h + 1) * BANK],
                                  start=False, stop=stop)
                    last.then_inc(y_added, 1)
                    if stop:
                        pe.wait_ge(y_added, unit + 1)
                        pe.sem_inc(y_ready, 1)

            def later_states(b, d):
                with pe.Fori(1, D_STATE // 2) as r:
                    for odd in range(2):
                        spread(b, d, 2 * r + odd)
                        add(b, d, 2 * r + odd - 2, odd)

            def mamba(b):
                project_z(b, 0, 0)
                project_z(b, 0, 1)
                project_x_backward(b, 0)
                project_x_backward(b, 1)
                project_dbc(b, 0, 0)
                project_z(b, 1, 0)
                project_dbc(b, 0, 1)
                project_dt(b, 0, 0)
                project_dt(b, 0, 1)
                project_z(b, 1, 1)
                project_dbc(b, 1, 0)
                project_dbc(b, 1, 1)
                project_dt(b, 1, 0)
                project_dt(b, 1, 1)
                pe.wait_ge(parts_ready, b * DIRS + 1)
                pe.wait_ge(mid_ready, b * DIRS + 1)
                pe.wait_ge(relu_ready, b * DIRS * BLOCKS + 2)
                spread(b, 0, 0)
                pe.wait_ge(relu_ready, b * DIRS * BLOCKS + 3)
                skip_term(0, 0)
                pe.wait_ge(relu_ready, b * DIRS * BLOCKS + 4)
                skip_term(0, 1)
                spread(b, 0, 1)
                later_states(b, 0)
                pe.wait_ge(parts_ready, b * DIRS + 2)
                pe.wait_ge(mid_ready, b * DIRS + 2)
                spread(b, 1, 0)
                add(b, 0, D_STATE - 2, 0)
                spread(b, 1, 1)
                add(b, 0, D_STATE - 1, 1, stop=True)
                pe.wait_ge(gated, b * DIRS * BLOCKS + 1)
                skip_term(1, 0)
                pe.wait_ge(gated, b * DIRS * BLOCKS + 2)
                skip_term(1, 1)
                later_states(b, 1)

            def project_out(m):
                pe.wait_ge(gated, DIRS * BLOCKS * (m + 1))
                pe.wait_ge(c_copied, DIRS * D_STATE * (m + 1))
                for i in range(TILES):
                    for d in range(DIRS):
                        for k in range(BLOCKS):
                            last = mm(ps67[:, i * P:(i + 1) * P], gate[:, d, k, i * P:(i + 1) * P],
                                      outproj_t[:, d, k, :], start=d + k == 0, stop=d + k == DIRS + BLOCKS - 2)
                last.then_inc(mamba_out, 1)

            def expert_input(m):
                pe.wait_ge(en_ready, TILES * (m + 1))
                pe.wait_ge(t2_ready, m + 1)
                for i in range(TILES):
                    last = tr(ps67[:, i * P:(i + 1) * P], en[:, i, :], ident[:, :])
                last.then_inc(en_t, 1)

            def route(m, b=None):
                pe.wait_ge(ec_ready, m + 1)
                if b is not None:
                    pe.wait_ge(xtok_copied, b + 1)
                for i in range(TILES):
                    last = mm(ps45[:, i * EXPERTS:(i + 1) * EXPERTS], e_c[:, i * P:(i + 1) * P], router_t[:, :],
                              start=True, stop=True)
                last.then_inc(logits_ready, 1)

            def hidden(m, x):
                pe.wait_ge(gelu_ready, m * EXPERTS + max(x - 1, 0))
                for h in range(HALVES):
                    last = mm(halves(ps[1 + 2 * (x % 2)])[h], w1[:, x, :], halves(e_c)[h], start=True, stop=True)
                last.then_inc(hidden_ready, 1)

            def weights(m, x):
                pe.wait_ge(sel_ready, m * EXPERTS + x)
                for h in range(HALVES):
                    last = mm(halves(ps45)[h], pick[:, x, :], comb_parts_t[:, h * BANK:(h + 1) * BANK],
                              start=True, stop=True)
                last.then_inc(weight_ready, 1)

            def add_expert(m, x):
                pe.wait_ge(sel_ready, m * EXPERTS + x + 1)
                for h in range(HALVES):
                    last = mm(halves(ps01)[h], w2[:, x, :], sel_e[:, x % 2, h * BANK:(h + 1) * BANK],
                              start=False, stop=x == EXPERTS - 1)
                last.then_inc(expert_added, 1)

            def experts(m, b=None):
                if b is not None:
                    pe.wait_ge(scores_copied, TILES * (b + 1))
                hidden(m, 0)
                pe.wait_ge(comb_ready, m + 1)
                for i in range(TILES):
                    last = tr(ps45[0:EXPERTS, i * P:(i + 1) * P], comb[:, i, :], ident[:, :])
                last.then_inc(comb_transposed, 1)
                parts_ps = ps67[0:PARTS * BC, :].bitcast(BF16)
                for i in range(TILES):
                    last = tr(parts_ps[:, i * P:(i + 1) * P], comb_parts[:, i, :], ident_bf[:, :])
                last.then_inc(comb_transposed, 1)
                pe.wait_ge(comb_copied, 2 * m + 2)
                weights(m, 0)
                hidden(m, 1)
                pe.wait_ge(t2e_ready, TILES * (m + 1))
                for h in range(HALVES):
                    mm(halves(ps01)[h], b2[:, :], comb_t[:, h * BANK:(h + 1) * BANK], start=True, stop=False)
                for i in range(TILES):
                    mm(ps01[:, i * P:(i + 1) * P], t2e[:, i, :], ident[:, :], start=False, stop=False)
                for x in range(1, EXPERTS):
                    weights(m, x)
                    if x + 1 < EXPERTS:
                        hidden(m, x + 1)
                    add_expert(m, x - 1)
                add_expert(m, EXPERTS - 1)

            def pe_image(b, m=None):
                if m is not None:
                    add(m, 1, D_STATE - 2, 0)
                group_norm(b)
                if m is not None:
                    add(m, 1, D_STATE - 1, 1, stop=True)
                queries(b)
                for i in range(TILES):
                    scores(b, i)
                values(b)
                transpose_input(b)
                if m is not None:
                    pe.wait_ge(qv_copied, 2 * b + 2)
                    project_out(m)
                    expert_input(m)
                    route(m, b)
                    experts(m, b)
                sum_missed(b)
                transpose_prob(b, 0)
                for i in range(TILES):
                    if i + 1 < TILES:
                        transpose_prob(b, i + 1)
                    attend(b, i)
                mamba_input(b)
                mamba(b)

            pe_image(0)
            with pe.Fori(1, BATCH) as b:
                pe_image(b, b - 1)
            m = BATCH - 1
            add(m, 1, D_STATE - 2, 0)
            add(m, 1, D_STATE - 1, 1, stop=True)
            project_out(m)
            expert_input(m)
            route(m)
            experts(m)


_WAY = ["in_proj_w", "conv_w", "conv_b", "x_proj_w", "dt_proj_w", "dt_proj_b", "A_log", "D", "out_proj_w"]
_INS = (["x", "L0_conv_Wq", "L0_conv_Wk", "L0_conv_Wv", "L1_attn_ln_gamma", "L1_attn_ln_beta"]
        + [f"L1_attn_{way}_{name}" for way in "fb" for name in _WAY]
        + ["L1_ffn_" + name for name in ("router_w", "w1", "b1", "w2", "b2")])


def kernel(**inputs):
    import numpy as _np
    import concourse.bacc as _bacc
    from concourse import mybir as _mybir
    from concourse.bass_utils import run_bass_kernel_spmd as _run

    nc = _bacc.Bacc("TRN2", target_bir_lowering=False, num_devices=1)
    arrays, args = {}, {}
    for name in _INS:
        a = _np.ascontiguousarray(inputs[name])
        arrays[f"in_{name}"] = a
        args[name] = nc.dram_tensor(f"in_{name}", a.shape, _mybir.dt.from_np(a.dtype), kind="ExternalInput").ap()
    out = nc.dram_tensor("out_0", inputs["x"].shape, _mybir.dt.from_np(_np.dtype("float32")),
                         kind="ExternalOutput").ap()
    hybrid_block(nc, args, out)
    r = _run(nc, [arrays], core_ids=[0])
    return r.results[0]["out_0"]
```
